# Optimizing a Trainium2 kernel written in Bass

```python
import numpy as np
import jax
import jax.numpy as jnp

def _softmax(x, axis=-1):
    return jax.nn.softmax(x, axis=axis)

def _gelu(x):
    return jax.nn.gelu(x, approximate=True)

def _silu(x):
    return jax.nn.silu(x)

def _sigmoid(x):
    return jax.nn.sigmoid(x)

def _layernorm(x, axis=-1, eps=1e-05):
    m = jnp.mean(x, axis=axis, keepdims=True)
    v = jnp.var(x, axis=axis, keepdims=True)
    return (x - m) / jnp.sqrt(v + eps)

def _scatter_add(tgt, idx, src, axis=0):
    return tgt.at[idx].add(src)

def _segment_sum(src, seg, n):
    return jax.ops.segment_sum(src, seg, n)
kernel_name = 'mk_flamingo_gated_d2_seqx_r8_c9e13c'

def setup_inputs(seed: int=0):
    np.random.seed(seed)
    _w = jnp.asarray

    def _rec_inputs():
        import jax
        import jax.numpy as jnp
        _rk = jax.random.key(seed)
        x = -0.0002928 + 1 * jax.random.normal(jax.random.fold_in(_rk, 1), (64, 64, 128), jnp.float32)
        _lenS = 64 - jax.random.randint(jax.random.fold_in(_rk, 7), (64,), 0, max(1, 64 // 4) + 1, jnp.int32)
        _lenS2 = 64 - jax.random.randint(jax.random.fold_in(_rk, 8), (64,), 0, max(1, 64 // 4) + 1, jnp.int32)
        _ctx_1024P = jax.random.normal(jax.random.fold_in(_rk, 11), (64, 16, 128), jnp.float32)
        _ctx_1024c = jax.random.dirichlet(jax.random.fold_in(_rk, 511), 0.3 * jnp.ones((16,), jnp.float32), (64, 64))
        _ctx_1024t = jnp.einsum('bsk,bkd->bsd', _ctx_1024c, _ctx_1024P)
        _ctx_1024t = _ctx_1024t * jax.lax.rsqrt(jnp.mean(jnp.square(_ctx_1024t)) + 1e-12) * 0.953939
        ctx_1024 = -1.39393e-06 + 0.999914 * (_ctx_1024t + 0.3 * jax.random.normal(jax.random.fold_in(_rk, 611), (64, 64, 128), jnp.float32))
        _validS = jnp.arange(64)[None, :] < _lenS[:, None]
        _validS2 = jnp.arange(64)[None, :] < _lenS2[:, None]
        _causal = jnp.tril(jnp.ones((64, 64), dtype=bool))
        mask_BxS2_bk0 = jnp.logical_not(jnp.broadcast_to(_validS2[:, :], (64, 64)))
        _g = jax.random.normal(jax.random.fold_in(_rk, 9001), (2, 2), jnp.float32)
        _g = jnp.sign(_g) * jnp.maximum(jnp.abs(_g), 1.0) + (_g == 0) * 1.0
        g_xattn = _g[0]
        g_ffn = _g[1]
        return (x, ctx_1024, mask_BxS2_bk0, g_xattn, g_ffn)
    x, ctx_1024, mask_BxS2_bk0, g_xattn, g_ffn = _rec_inputs()

    def _L0_xattn_setup():
        import jax, jax.numpy as jnp
        import numpy as np
        B, S, D = (2, 256, 128)
        H = 16
        CHUNK = 32
        NEG_INF = -1000000000.0
        key = jax.random.key(seed)
        ks = jax.random.split(key, 11)
        std = 1.0 / np.sqrt(D)
        return {'query': jax.random.normal(ks[0], (B, S, D), jnp.float32), 'key': jax.random.normal(ks[1], (B, S, D), jnp.float32), 'value': jax.random.normal(ks[2], (B, S, D), jnp.float32), 'Wq': jax.random.normal(ks[3], (D, D), jnp.float32) * std, 'bq': jax.random.normal(ks[4], (D,), jnp.float32) * 0.01, 'Wk': jax.random.normal(ks[5], (D, D), jnp.float32) * std, 'bk': jax.random.normal(ks[6], (D,), jnp.float32) * 0.01, 'Wv': jax.random.normal(ks[7], (D, D), jnp.float32) * std, 'bv': jax.random.normal(ks[8], (D,), jnp.float32) * 0.01, 'Wo': jax.random.normal(ks[9], (D, D), jnp.float32) * std, 'bo': jax.random.normal(ks[10], (D,), jnp.float32) * 0.01}
    _L0_xattn_all = _L0_xattn_setup()
    _L0_xattn_in = {k: v for k, v in _L0_xattn_all.items() if k in ('Wq', 'bq', 'Wk', 'bk', 'Wv', 'bv', 'Wo', 'bo')}
    del _L0_xattn_all

    def _L0_ffn_setup():
        import jax, jax.numpy as jnp
        import numpy as np
        DIM = 128
        HIDDEN = 256
        N_EXPERTS = 8
        TOP_K = 2
        EPS = 1e-06

        def rms_norm(x, scale, eps=EPS):
            ms = jnp.mean(jnp.square(x.astype(jnp.float32)), axis=-1, keepdims=True)
            s = scale.astype(jnp.float32) * jax.lax.rsqrt(ms + eps)
            return x * s.astype(x.dtype)

        def moe_linear(xf, ids, W):
            E = W.shape[0]
            out = jnp.zeros((xf.shape[0], W.shape[1]), dtype=xf.dtype)
            for e in range(E):
                out = out + jnp.where((ids == e)[:, None], xf @ W[e].T, 0.0)
            return out
        key = jax.random.key(seed)
        k1, k2, k3, k4 = jax.random.split(key, 4)
        x = jax.random.normal(k1, (4, 512, DIM), dtype=jnp.float32)
        norm_scale = jnp.ones((DIM,), dtype=jnp.float32)
        w_router = jax.random.normal(k2, (N_EXPERTS, DIM), dtype=jnp.float32) / np.sqrt(DIM)
        lim_up = np.sqrt(6.0 / (DIM + 2 * HIDDEN))
        w_up = jax.random.uniform(k3, (N_EXPERTS, 2 * HIDDEN, DIM), dtype=jnp.float32, minval=-lim_up, maxval=lim_up)
        lim_dn = np.sqrt(6.0 / (HIDDEN + DIM))
        w_down = jax.random.uniform(k4, (N_EXPERTS, DIM, HIDDEN), dtype=jnp.float32, minval=-lim_dn, maxval=lim_dn)
        return {'x': x, 'norm_scale': norm_scale, 'w_router': w_router, 'w_up': w_up, 'w_down': w_down}
    _L0_ffn_all = _L0_ffn_setup()
    _L0_ffn_in = {k: v for k, v in _L0_ffn_all.items() if k in ('norm_scale', 'w_router', 'w_up', 'w_down')}
    del _L0_ffn_all

    def _L1_xattn_setup():
        import jax, jax.numpy as jnp
        import numpy as np
        EPS = 1e-05

        def layer_norm(x, g, b):
            mu = jnp.mean(x, axis=-1, keepdims=True)
            var = jnp.mean((x - mu) ** 2, axis=-1, keepdims=True)
            return (x - mu) * jax.lax.rsqrt(var + EPS) * g + b
        key = jax.random.key(seed)
        ks = jax.random.split(key, 8)
        b, n, l, D = (8, 512, 64, 128)
        heads, dim_head = (16, 64)
        inner = heads * dim_head
        x = jax.random.normal(ks[0], (b, n, D), dtype=jnp.float32)
        latents = jax.random.normal(ks[1], (b, l, D), dtype=jnp.float32)
        mask = jax.random.randint(ks[2], (b, n), 0, 2) > 0
        Wq = jax.random.normal(ks[3], (D, inner), dtype=jnp.float32) * D ** (-0.5)
        Wkv = jax.random.normal(ks[4], (D, 2 * inner), dtype=jnp.float32) * D ** (-0.5)
        Wout = jax.random.normal(ks[5], (inner, D), dtype=jnp.float32) * inner ** (-0.5)
        g1 = jnp.ones((D,), jnp.float32)
        b1 = jnp.zeros((D,), jnp.float32)
        g2 = jnp.ones((D,), jnp.float32)
        b2 = jnp.zeros((D,), jnp.float32)
        return {'x': x, 'latents': latents, 'mask': mask, 'g1': g1, 'b1': b1, 'g2': g2, 'b2': b2, 'Wq': Wq, 'Wkv': Wkv, 'Wout': Wout}
    _L1_xattn_all = _L1_xattn_setup()
    _L1_xattn_in = {k: v for k, v in _L1_xattn_all.items() if k in ('g1', 'b1', 'g2', 'b2', 'Wq', 'Wkv', 'Wout')}
    del _L1_xattn_all

    def _L1_ffn_setup():
        import jax, jax.numpy as jnp
        import numpy as np
        B, S, D, E = (2, 256, 128, 8)
        key = jax.random.key(seed)
        ks = jax.random.split(key, 5)
        x = jax.random.normal(ks[0], (B, S, D), dtype=jnp.float32)
        router_w = jax.random.normal(ks[1], (E, D), dtype=jnp.float32) * 0.02
        router_b = jnp.zeros((E,), dtype=jnp.float32)
        expert_w = jax.random.normal(ks[2], (E, D, D), dtype=jnp.float32) * 0.02
        expert_b = jnp.zeros((E, D), dtype=jnp.float32)
        return {'x': x, 'router_w': router_w, 'router_b': router_b, 'expert_w': expert_w, 'expert_b': expert_b}
    _L1_ffn_all = _L1_ffn_setup()
    _L1_ffn_in = {k: v for k, v in _L1_ffn_all.items() if k in ('router_w', 'router_b', 'expert_w', 'expert_b')}
    del _L1_ffn_all
    return {'x': x, 'ctx_1024': ctx_1024, 'mask_BxS2_bk0': mask_BxS2_bk0, 'g_xattn': g_xattn, 'g_ffn': g_ffn, 'L0_xattn_Wq': _L0_xattn_in['Wq'], 'L0_xattn_bq': _L0_xattn_in['bq'], 'L0_xattn_Wk': _L0_xattn_in['Wk'], 'L0_xattn_bk': _L0_xattn_in['bk'], 'L0_xattn_Wv': _L0_xattn_in['Wv'], 'L0_xattn_bv': _L0_xattn_in['bv'], 'L0_xattn_Wo': _L0_xattn_in['Wo'], 'L0_xattn_bo': _L0_xattn_in['bo'], 'L0_ffn_norm_scale': _L0_ffn_in['norm_scale'], 'L0_ffn_w_router': _L0_ffn_in['w_router'], 'L0_ffn_w_up': _L0_ffn_in['w_up'], 'L0_ffn_w_down': _L0_ffn_in['w_down'], 'L1_xattn_g1': _L1_xattn_in['g1'], 'L1_xattn_b1': _L1_xattn_in['b1'], 'L1_xattn_g2': _L1_xattn_in['g2'], 'L1_xattn_b2': _L1_xattn_in['b2'], 'L1_xattn_Wq': _L1_xattn_in['Wq'], 'L1_xattn_Wkv': _L1_xattn_in['Wkv'], 'L1_xattn_Wout': _L1_xattn_in['Wout'], 'L1_ffn_router_w': _L1_ffn_in['router_w'], 'L1_ffn_router_b': _L1_ffn_in['router_b'], 'L1_ffn_expert_w': _L1_ffn_in['expert_w'], 'L1_ffn_expert_b': _L1_ffn_in['expert_b']}

def reference(x, ctx_1024, mask_BxS2_bk0, g_xattn, g_ffn, L0_xattn_Wq, L0_xattn_bq, L0_xattn_Wk, L0_xattn_bk, L0_xattn_Wv, L0_xattn_bv, L0_xattn_Wo, L0_xattn_bo, L0_ffn_norm_scale, L0_ffn_w_router, L0_ffn_w_up, L0_ffn_w_down, L1_xattn_g1, L1_xattn_b1, L1_xattn_g2, L1_xattn_b2, L1_xattn_Wq, L1_xattn_Wkv, L1_xattn_Wout, L1_ffn_router_w, L1_ffn_router_b, L1_ffn_expert_w, L1_ffn_expert_b):
    import jax
    import jax.numpy as jnp

    def _L0_xattn_ref(query, key, value, Wq, bq, Wk, bk, Wv, bv, Wo, bo):
        import jax, jax.numpy as jnp
        import numpy as np
        B, S, D = (2, 256, 128)
        H = 16
        CHUNK = 32
        NEG_INF = -1000000000.0
        b, s, d = query.shape
        hd = d // H
        scale = 1.0 / jnp.sqrt(jnp.asarray(hd, query.dtype))
        q = (query @ Wq + bq).reshape(b, s, H, hd)
        k = (key @ Wk + bk).reshape(b, s, H, hd)
        v = (value @ Wv + bv).reshape(b, s, H, hd)
        scores = jnp.einsum('bqhd,bkhd->bhqk', q, k) * scale
        pos = jnp.arange(s)
        block_end = (pos // CHUNK + 1) * CHUNK
        mask = pos[None, :] < block_end[:, None]
        scores = jnp.where(mask[None, None], scores, NEG_INF)
        attn = jax.nn.softmax(scores, axis=-1)
        out = jnp.einsum('bhqk,bkhd->bqhd', attn, v).reshape(b, s, d)
        return out @ Wo + bo

    def _L0_ffn_ref(x, norm_scale, w_router, w_up, w_down):
        import jax, jax.numpy as jnp
        import numpy as np
        DIM = 128
        HIDDEN = 256
        N_EXPERTS = 8
        TOP_K = 2
        EPS = 1e-06

        def rms_norm(x, scale, eps=EPS):
            ms = jnp.mean(jnp.square(x.astype(jnp.float32)), axis=-1, keepdims=True)
            s = scale.astype(jnp.float32) * jax.lax.rsqrt(ms + eps)
            return x * s.astype(x.dtype)

        def moe_linear(xf, ids, W):
            E = W.shape[0]
            out = jnp.zeros((xf.shape[0], W.shape[1]), dtype=xf.dtype)
            for e in range(E):
                out = out + jnp.where((ids == e)[:, None], xf @ W[e].T, 0.0)
            return out
        B, S, D = x.shape
        skip = x
        xn = rms_norm(x, norm_scale)
        scores = (xn @ w_router.T).astype(jnp.float32)
        scores_topk, idx = jax.lax.top_k(scores, TOP_K)
        weights = jax.nn.softmax(scores_topk, axis=-1)
        xf = jnp.broadcast_to(xn[..., None, :], (B, S, TOP_K, D)).reshape(-1, D)
        ids = idx.reshape(-1)
        up = moe_linear(xf, ids, w_up)
        u, gate = jnp.split(up, 2, axis=-1)
        h = u * jax.nn.silu(gate)
        down = moe_linear(h, ids, w_down)
        down = down.reshape(B, S, TOP_K, D)
        out = jnp.sum(down * weights[..., None].astype(down.dtype), axis=-2)
        return out + skip

    def _L1_xattn_ref(x, latents, mask, g1, b1, g2, b2, Wq, Wkv, Wout):
        import jax, jax.numpy as jnp
        import numpy as np
        EPS = 1e-05

        def layer_norm(x, g, b):
            mu = jnp.mean(x, axis=-1, keepdims=True)
            var = jnp.mean((x - mu) ** 2, axis=-1, keepdims=True)
            return (x - mu) * jax.lax.rsqrt(var + EPS) * g + b
        heads, dim_head = (16, 64)
        b, n, D = x.shape
        l = latents.shape[1]
        xn = layer_norm(x, g1, b1)
        ln_lat = layer_norm(latents, g2, b2)
        q = ln_lat @ Wq
        kv = jnp.concatenate([xn, ln_lat], axis=1) @ Wkv
        k, v = jnp.split(kv, 2, axis=-1)

        def to_heads(t):
            return t.reshape(t.shape[0], t.shape[1], heads, dim_head).transpose(0, 2, 1, 3)
        q, k, v = (to_heads(q), to_heads(k), to_heads(v))
        scale = 1.0 / np.sqrt(np.sqrt(dim_head)).astype(np.float32)
        weight = jnp.einsum('bhld,bhnd->bhln', q * scale, k * scale)
        full_mask = jnp.concatenate([mask, jnp.ones((b, l), dtype=bool)], axis=1)
        neg = -jnp.finfo(weight.dtype).max
        weight = jnp.where(full_mask[:, None, None, :], weight, neg)
        weight = jax.nn.softmax(weight.astype(jnp.float32), axis=-1).astype(q.dtype)
        out = jnp.einsum('bhln,bhnd->bhld', weight, v)
        out = out.transpose(0, 2, 1, 3).reshape(b, l, heads * dim_head)
        return out @ Wout

    def _L1_ffn_ref(x, router_w, router_b, expert_w, expert_b):
        import jax, jax.numpy as jnp
        import numpy as np
        B, S, D, E = (2, 256, 128, 8)
        logits = jnp.einsum('bsd,ed->bse', x, router_w) + router_b
        probs = jax.nn.softmax(logits, axis=-1)
        weights = jnp.max(probs, axis=-1)
        top1 = jnp.argmax(probs, axis=-1)
        y_all = jnp.einsum('bsd,eod->bseo', x, expert_w) + expert_b
        y = jnp.take_along_axis(y_all, top1[:, :, None, None], axis=2)[:, :, 0, :]
        out = y * weights[:, :, None]
        return out
    x = x + jnp.tanh(g_xattn[0]) * _L0_xattn_ref(_layernorm(x, axis=-1), ctx_1024, ctx_1024, L0_xattn_Wq, L0_xattn_bq, L0_xattn_Wk, L0_xattn_bk, L0_xattn_Wv, L0_xattn_bv, L0_xattn_Wo, L0_xattn_bo)
    x = x + jnp.tanh(g_ffn[0]) * _L0_ffn_ref(_layernorm(x, axis=-1), L0_ffn_norm_scale, L0_ffn_w_router, L0_ffn_w_up, L0_ffn_w_down)
    x = x + jnp.tanh(g_xattn[1]) * _L1_xattn_ref(ctx_1024, _layernorm(x, axis=-1), mask_BxS2_bk0, L1_xattn_g1, L1_xattn_b1, L1_xattn_g2, L1_xattn_b2, L1_xattn_Wq, L1_xattn_Wkv, L1_xattn_Wout)
    x = x + jnp.tanh(g_ffn[1]) * _L1_ffn_ref(_layernorm(x, axis=-1), L1_ffn_router_w, L1_ffn_router_b, L1_ffn_expert_w, L1_ffn_expert_b)
    return x

_drawn_inputs = setup_inputs


def setup_inputs(seed=0):
    import zlib

    import numpy as np

    out = dict(_drawn_inputs(seed))
    spreads = {'g_ffn': (-1.0, 0.6),
     'L0_ffn_norm_scale': (1.0, 0.2),
     'L1_xattn_g1': (1.0, 0.2),
     'L1_xattn_b1': (0.0, 0.1),
     'L1_xattn_g2': (1.0, 0.2),
     'L1_xattn_b2': (0.0, 0.1),
     'L1_ffn_router_b': (0.0, 0.1),
     'L1_ffn_expert_b': (0.0, 0.277)}
    factors = {'L0_xattn_bq': 8.0, 'L0_xattn_bk': 8.0}
    for name, (base, spread) in spreads.items():
        noise = np.random.default_rng([zlib.crc32(name.encode()), seed]).standard_normal(out[name].shape)
        drawn = base * np.exp(spread * noise) if base else spread * noise
        out[name] = jnp.asarray(drawn.astype(out[name].dtype))
    for name, factor in factors.items():
        out[name] = (out[name] * factor).astype(out[name].dtype)
    return out
```

```python
import concourse.bass as bass
from concourse import mybir
from contextlib import ExitStack

F32 = mybir.dt.float32
F32R = mybir.dt.float32r
BF16 = mybir.dt.bfloat16
ALU = mybir.AluOpType
ACT = mybir.ActivationFunctionType
AX = mybir.AxisListType

P = 128
BATCH, SEQ, D = 64, 64, 128
NT = BATCH * SEQ // P
GT = 2
NG = NT // GT
GB = GT * 2
H = 16
HD0 = D // H
CHUNK = 32
HD1 = 64
E = 8
HID = 256
LN_EPS = 1e-5
RMS_EPS = 1e-6
BIG = 1e30


class Env:
    pass


def there(g, n=NG):
    return not isinstance(g, int) or 0 <= g < n


def split_products(nc, out, lhs, rhs, start, stop):
    pairs = ((lhs[0], rhs[0]), (lhs[0], rhs[1]), (lhs[1], rhs[0]))
    for i, (a, b) in enumerate(pairs):
        last = nc.tensor.matmul(out, a, b, start=start and i == 0, stop=stop and i == 2)
    return last


def group_norm(nc, pool, v, stat6, rstd, shift, parts, done):
    w = v.norm_work
    twice_mean, diff, squares, diff2, rest, var4, half_rstd, product = (w[:, i] for i in range(8))
    nc.gpsimd.tensor_tensor(twice_mean, stat6[:, :, 1], stat6[:, :, 4], ALU.add)
    nc.gpsimd.tensor_tensor(diff, stat6[:, :, 1], stat6[:, :, 4], ALU.subtract)
    nc.gpsimd.tensor_tensor(squares, stat6[:, :, 2], stat6[:, :, 5], ALU.add).then_inc(parts, 1)
    pool.wait_ge(parts, done + 1)
    nc.gpsimd.tensor_tensor(diff2, diff, diff, ALU.mult)
    nc.gpsimd.tensor_scalar(rest, squares, 4.0 / D, 4 * LN_EPS, ALU.mult, ALU.add).then_inc(parts, 1)
    pool.wait_ge(parts, done + 2)
    nc.gpsimd.tensor_tensor(var4, diff2, rest, ALU.add).then_inc(parts, 1)
    pool.wait_ge(parts, done + 3)
    nc.gpsimd.tensor_tensor(half_rstd, var4, v.minus_half[:, 0:GT], ALU.pow).then_inc(parts, 1)
    pool.wait_ge(parts, done + 4)
    nc.gpsimd.tensor_tensor(product, twice_mean, half_rstd, ALU.mult)
    nc.gpsimd.tensor_scalar(rstd, half_rstd, 2.0, None, ALU.mult).then_inc(parts, 1)
    pool.wait_ge(parts, done + 5)
    return nc.gpsimd.tensor_tensor(shift, v.zeros[:, 0:GT], product, ALU.subtract)


def setup(nc, v, io):
    with ExitStack() as ctx:
        sem = lambda name: ctx.enter_context(nc.semaphore(name))
        sb = lambda name, shape, dt=F32: ctx.enter_context(nc.sbuf_tensor(name, shape, dt))
        consts_zeroed, consts_built = sem("consts_zeroed"), sem("consts_built")
        head_sums = sem("head_sums")
        head_rows = sb("head_rows", [P, 4, 4])
        with nc.Block() as block:

            @block.sync
            def _(sp):
                for name, tile in (("L0_xattn_Wq", v.wq0), ("L0_xattn_Wk", v.wk0), ("L0_xattn_Wv", v.wv0), ("L0_xattn_Wo", v.wo0)):
                    sp.dma_start(tile[:], io[name]).then_inc(v.weights0_loaded, 16)
                for name, col in (("L0_xattn_bq", 0), ("L0_xattn_bk", 1), ("L0_xattn_bv", 2)):
                    sp.dma_start(v.vec0[:, col:col + 1], io[name].rearrange("(d a) -> d a", a=1)).then_inc(v.weights0_loaded, 16)
                sp.dma_start(v.bo_row[:], io["L0_xattn_bo"].rearrange("(a d) -> a d", a=1).broadcast_to([P, D])).then_inc(v.weights0_loaded, 16)
                for name, col in (("g_xattn", 0), ("g_ffn", 2)):
                    sp.dma_start(v.gate[:, col:col + 2], io[name].rearrange("(a d) -> a d", a=1).broadcast_to([P, 2])).then_inc(v.weights0_loaded, 16)
                sp.dma_start(v.xa[:], io["x"].rearrange("(t c) s d -> (c s) t d", c=2)).then_inc(v.x_loaded, 16)
                sp.dma_start(v.cx[:], io["ctx_1024"].rearrange("(t c) s d -> (c s) t d", c=2)).then_inc(v.x_loaded, 16)

            @block.scalar
            def _(act):
                act.dma_start(v.w_up_raw[:], io["L0_ffn_w_up"].rearrange("e (c p) d -> p (e c) d", p=P)).then_inc(v.weights1_loaded, 16)
                act.dma_start(v.w_down_raw[:], io["L0_ffn_w_down"].rearrange("e o f -> o e f")).then_inc(v.weights1_loaded, 16)
                act.dma_start(v.router0_raw[:], io["L0_ffn_w_router"]).then_inc(v.weights1_loaded, 16)
                act.dma_start(v.vec1[:, 0:1], io["L0_ffn_norm_scale"].rearrange("(d a) -> d a", a=1)).then_inc(v.weights1_loaded, 16)
                act.dma_start(v.wq1_raw[:], io["L1_xattn_Wq"]).then_inc(v.weights2_loaded, 16)
                act.dma_start(v.wkv1_raw[:], io["L1_xattn_Wkv"]).then_inc(v.weights2_loaded, 16)
                act.dma_start(v.wout1_raw[:], io["L1_xattn_Wout"].rearrange("(c p) d -> p c d", p=P)).then_inc(v.weights2_loaded, 16)
                for col, name in enumerate(("L1_xattn_g1", "L1_xattn_b1", "L1_xattn_g2", "L1_xattn_b2")):
                    act.dma_start(v.vec2[:, col:col + 1], io[name].rearrange("(d a) -> d a", a=1)).then_inc(v.weights2_loaded, 16)
                act.dma_start(v.mask_u8[:], io["mask_BxS2_bk0"].rearrange("(a b) s -> a (b s)", a=1)).then_inc(v.weights2_loaded, 16)
                act.dma_start(v.expert_raw[:], io["L1_ffn_expert_w"].rearrange("e o d -> o e d")).then_inc(v.weights3_loaded, 16)
                act.dma_start(v.router1_raw[:], io["L1_ffn_router_w"]).then_inc(v.weights3_loaded, 16)
                act.dma_start(v.router_b_row[:], io["L1_ffn_router_b"].rearrange("(a e) -> a e", a=1).broadcast_to([P, E])).then_inc(v.weights3_loaded, 16)
                act.dma_start(v.expert_b_rows[:], io["L1_ffn_expert_b"].rearrange("(a e) d -> a (e d)", a=1).broadcast_to([2, E * D])).then_inc(v.weights3_loaded, 16)
                act.wait_ge(v.weights0_loaded, 160)
                nc.scalar.activation(v.tgate[:], v.gate[:], ACT.Tanh).then_inc(v.gates_ready, 1)

            @block.gpsimd
            def _(pool):
                nc.gpsimd.memset(v.ident[:], 0.0).then_inc(consts_zeroed, 1)
                nc.gpsimd.memset(head_rows[:], 1.0).then_inc(consts_zeroed, 1)
                nc.gpsimd.memset(v.minus_half[:], -0.5)
                nc.gpsimd.memset(v.zeros[:], 0.0)
                nc.gpsimd.memset(v.ones_row[:], 1.0)
                nc.gpsimd.memset(v.ones_pair_f[:], 1.0).then_inc(consts_zeroed, 1)
                for e in range(E):
                    last = nc.gpsimd.memset(v.first_wins[:, e:e + 1], float(E - e))
                last.then_inc(consts_zeroed, 1)
                pool.wait_ge(consts_zeroed, 4)
                nc.gpsimd.affine_select(out=v.ident[:], in_=v.ident[:], compare_op=ALU.not_equal, fill=1.0, base=0,
                                        pattern=[[-1, P]], channel_multiplier=1).then_inc(consts_built, 1)
                nc.gpsimd.affine_select(out=head_rows[:], in_=head_rows[:], compare_op=ALU.is_ge, fill=0.0, base=0,
                                        pattern=[[-4 * HD0, 4], [-HD0, 4]], channel_multiplier=1).then_inc(consts_built, 1)
                pool.wait_ge(consts_built, 2)
                nc.gpsimd.affine_select(out=head_rows[:], in_=head_rows[:], compare_op=ALU.is_ge, fill=0.0, base=HD0 - 1,
                                        pattern=[[4 * HD0, 4], [HD0, 4]], channel_multiplier=-1).then_inc(consts_built, 1)

            @block.vector
            def _(dve):
                dve.wait_ge(consts_built, 3)
                nc.vector.reduce_sum(v.head_in_four[:], head_rows[:].rearrange("p a j -> p j a"), AX.X).then_inc(head_sums, 1)
                nc.vector.reduce_sum(v.four_rows[:], head_rows[:], AX.X).then_inc(head_sums, 1)
                dve.wait_ge(head_sums, 2)
                nc.vector.tensor_scalar(v.q_mask[:], v.head_in_four[:], float(HD0) ** -0.5, None, ALU.mult).then_inc(head_sums, 1)
                nc.vector.tensor_copy(v.four_cols[:].rearrange("p (a c) -> p a c", a=4),
                                      v.four_rows[:].unsqueeze(2).broadcast_to([P, 4, 32])).then_inc(head_sums, 1)
                dve.wait_ge(v.weights0_loaded, 160)
                dve.wait_ge(v.gates_ready, 1)
                nc.vector.tensor_copy(v.wq0_h[:], v.wq0[:]).then_inc(head_sums, 1)
                nc.vector.tensor_copy(v.wk0_h[:], v.wk0[:]).then_inc(head_sums, 1)
                nc.vector.tensor_scalar(v.gbo[:], v.bo_row[:], v.tgate[:, 0:1], None, ALU.mult)
                for j in range(4):
                    nc.vector.tensor_scalar(v.wo0_j[:, j, :], v.wo0[:], v.head_in_four[:, j:j + 1], None, ALU.mult)
                nc.vector.tensor_scalar(v.bk_four[:], v.four_rows[:], v.vec0[:, 1:2], None, ALU.mult)
                nc.vector.tensor_scalar(v.half_gate[:], v.tgate[:, 2:3], 0.5, None, ALU.mult)
                dve.wait_ge(head_sums, 6)
                nc.vector.tensor_tensor(v.wq0_l[:], v.wq0[:], v.wq0_h[:].bitcast(F32), ALU.subtract)
                nc.vector.tensor_tensor(v.wk0_l[:], v.wk0[:], v.wk0_h[:].bitcast(F32), ALU.subtract)


def attention0(nc, v):
    with ExitStack() as ctx:
        sem = lambda name: ctx.enter_context(nc.semaphore(name))
        sb = lambda name, shape, dt=F32: ctx.enter_context(nc.sbuf_tensor(name, shape, dt))
        pb = lambda name, shape: ctx.enter_context(nc.psum_tensor(name, shape, F32))

        stat6 = sb("a_stat6", [P, GT, 6])
        rstd = sb("a_rstd", [P, GT])
        shift = sb("a_shift", [P, GT])
        x_hat = sb("a_x_hat", [P, GT, D])
        ctx_tile = sb("a_ctx_tile", [P, GT, D])
        xc = sb("a_xc", [P, 2, GT * P])
        xc_h = sb("a_xc_h", [P, 2, GT * P], F32R)
        xc_l = sb("a_xc_l", [P, 2, GT * P], F32R)
        ctx_rep = sb("a_ctx_rep", [P, 2 * GB, 4, CHUNK])
        q_flat = sb("a_q_flat", [P, 2 * GB, CHUNK])
        q_exp = [sb(f"a_q_exp{i}", [P, 2 * GB, 4, CHUNK]) for i in range(2)]
        k_exp = [sb(f"a_k_exp{i}", [P, 2 * GB, 4, CHUNK]) for i in range(2)]
        v_exp = [sb(f"a_v_exp{i}", [P, 2 * GB, D]) for i in range(2)]
        row_max = sb("a_row_max", [P, 2, 3, 4])
        row_max3 = sb("a_row_max3", [P, 2, 3, 4])
        shifted = sb("a_shifted", [P, 2, 384])
        probs = [sb(f"a_probs{i}", [P, 2, 384]) for i in range(2)]
        sums = sb("a_sums", [P, 2, 3, 4])
        sums_high = sb("a_sums_high", [P, 2, 4])
        recip = [sb(f"a_recip{i}", [P, 2, 3, 4]) for i in range(2)]
        normed = sb("a_normed", [P, 2, 384])
        probs_t = sb("a_probs_t", [P, 2, 384])
        heads_t = sb("a_heads_t", [P, 4, 4, CHUNK])

        ps_s = pb("a_ps_s", [P, 2, 512])
        ps_t = pb("a_ps_t", [P, 2, 512])
        ps_aux = pb("a_ps_aux", [P, 512])
        ps_qk = pb("a_ps_qk", [P, 512])
        ps_o = pb("a_ps_o", [P, 512])
        ps_y = pb("a_ps_y", [P, 512])

        stats_ready, rstd_ready, rstd_parts = sem("stats_ready"), sem("rstd_ready"), sem("rstd_parts")
        ctx_repeated = sem("ctx_repeated")
        xhat_ready, ctx_staged = sem("xhat_ready"), sem("ctx_staged")
        inputs_turned, xc_copied, xc_high, xc_low = sem("inputs_turned"), sem("xc_copied"), sem("xc_high"), sem("xc_low")
        qk_done, q_copied, k_ready, q_ready = sem("qk_done"), sem("q_copied"), sem("k_ready"), sem("q_ready")
        v_done, v_ready = sem("v_done"), sem("v_ready")
        scores_done, scores_maxed, max_spread, shifted_ready = sem("scores_done"), sem("scores_maxed"), sem("max_spread"), sem("shifted_ready")
        exp_done, sums_done, sums_added, recip_ready, normed_ready = sem("exp_done"), sem("sums_done"), sem("sums_added"), sem("recip_ready"), sem("normed_ready")
        probs_turned, probs_t_ready = sem("probs_turned"), sem("probs_t_ready")
        heads_done, heads_ready, projected, x1_ready = sem("heads_done"), sem("heads_ready"), sem("projected"), sem("x1_ready")
        base_ready = sem("base_ready")

        with nc.Block() as block:

            def each_group(eng, step):
                for g in range(-3, 1):
                    step(g, g % 2)
                with eng.Fori(0, (NG - 4) // 2) as i:
                    step(2 * i + 1, 1)
                    step(2 * i + 2, 0)
                for g in range(NG - 3, NG + 1):
                    step(g, g % 2)

            @block.tensor
            def _(pe):
                def values(g, par, half, bank):
                    pe.wait_ge(ctx_repeated, g + 1)
                    pe.wait_ge(k_ready, g + 1)
                    for i in range(4):
                        c = 4 * half + i
                        last = nc.tensor.matmul(bank[:, i * P:(i + 1) * P], ctx_rep[:, c], v.wv0[:], start=True, stop=True)
                    last.then_inc(v_done, 1)

                def scores(g, par, k):
                    pe.wait_ge(q_ready, g + 1)
                    pe.wait_ge(k_ready, g + 1)
                    if there(g - 1) or k:
                        pe.wait_ge(shifted_ready, 2 * g + k)
                    for b in range(2):
                        c = 2 * (2 * k + b)
                        nc.tensor.matmul(ps_s[:, b, 0:128], q_exp[par][:, c], k_exp[par][:, c], start=True, stop=True)
                        last = nc.tensor.matmul(ps_s[:, b, 128:384], q_exp[par][:, c + 1], k_exp[par][:, c:c + 2], start=True, stop=True)
                    last.then_inc(scores_done, 1)

                def turn_probs(g, k):
                    pe.wait_ge(normed_ready, 2 * g + k + 1)
                    if there(g - 1) or k:
                        pe.wait_ge(probs_t_ready, 2 * g + k)
                    for b in range(2):
                        for n in range(3):
                            cols = slice(n * 128, (n + 1) * 128)
                            last = nc.tensor.transpose(ps_t[:, b, cols], normed[:, b, cols], v.ident[:])
                    last.then_inc(probs_turned, 1)

                def heads(g, par, k):
                    pe.wait_ge(probs_t_ready, 2 * g + k + 1)
                    pe.wait_ge(v_ready, 2 * g + 2)
                    if there(g - 1) or k:
                        pe.wait_ge(heads_ready, 2 * g + k)
                    for b in range(2):
                        c = 2 * (2 * k + b)
                        nc.tensor.matmul(ps_o[:, b * 256:b * 256 + 256], v_exp[par][:, c], probs_t[:, b, 0:256], start=True, stop=False)
                        last = nc.tensor.matmul(ps_o[:, b * 256 + 128:b * 256 + 256], v_exp[par][:, c + 1], probs_t[:, b, 256:384],
                                                start=False, stop=True)
                    last.then_inc(heads_done, 1)

                def project(g, k):
                    pe.wait_ge(heads_ready, 2 * g + k + 1)
                    if there(g - 1) or k:
                        pe.wait_ge(x1_ready, 2 * g + k)
                    for j in range(4):
                        last = nc.tensor.matmul(ps_y[:, 0:D], heads_t[:, j],
                                                v.wo0_j[:, j], start=j == 0, stop=j == 3)
                    last.then_inc(projected, 1)

                def step(g, par):
                    for k in range(2):
                        if there(g):
                            turn_probs(g, k)
                        if k == 0 and there(g + 1):
                            values(g + 1, 1 - par, 0, ps_qk)
                            values(g + 1, 1 - par, 1, ps_aux)
                        if k == 1 and there(g + 2):
                            pe.wait_ge(xc_low, g + 3)
                            pe.wait_ge(xc_high, g + 3)
                            if there(g + 1):
                                pe.wait_ge(v_ready, 2 * (g + 1) + 1)
                            x_pair, c_pair = ((xc_h[:, n], xc_l[:, n]) for n in range(2))
                            split_products(nc, ps_qk[:, 0:256], (v.wq0_h[:], v.wq0_l[:]), x_pair, True, True)
                            split_products(nc, ps_qk[:, 256:512], (v.wk0_h[:], v.wk0_l[:]), c_pair, True, True).then_inc(qk_done, 1)
                        if there(g + 1):
                            scores(g + 1, 1 - par, k)
                        if k == 0 and there(g + 2):
                            pe.wait_ge(xhat_ready, g + 3)
                            pe.wait_ge(ctx_staged, g + 3)
                            if there(g + 1):
                                pe.wait_ge(v_ready, 2 * (g + 1) + 2)
                            for t in range(GT):
                                nc.tensor.transpose(ps_aux[:, t * P:(t + 1) * P], x_hat[:, t], v.ident[:])
                            for t in range(GT):
                                last = nc.tensor.transpose(ps_aux[:, (GT + t) * P:(GT + t + 1) * P], ctx_tile[:, t], v.ident[:])
                            last.then_inc(inputs_turned, 1)
                        if k == 0 and there(g - 1):
                            project(g - 1, 1)
                        if k == 1 and there(g):
                            project(g, 0)
                        if there(g):
                            heads(g, par, k)

                pe.wait_ge(v.weights0_loaded, 160)
                each_group(pe, step)

            @block.scalar
            def _(act):
                def step(g, par):
                    for k in range(2):
                        if there(g):
                            act.wait_ge(probs_turned, 2 * g + k + 1)
                            if there(g - 1) or k:
                                act.wait_ge(heads_done, 2 * g + k)
                            nc.scalar.activation(probs_t[:], ps_t[:, :, 0:384], ACT.Copy).then_inc(probs_t_ready, 1)
                        if k == 1 and there(g + 2):
                            act.wait_ge(qk_done, g + 3)
                            if there(g + 1):
                                act.wait_ge(q_ready, g + 2)
                            nc.scalar.activation(q_flat[:], ps_qk[:, 0:256].rearrange("p (c q) -> p c q", q=CHUNK), ACT.Identity,
                                                 bias=v.vec0[:, 0:1]).then_inc(q_copied, 1)
                            if there(g):
                                act.wait_ge(scores_done, 2 * g + 2)
                            for a in range(4):
                                last = nc.scalar.activation(k_exp[par][:, :, a], ps_qk[:, 256:512].rearrange("p (c q) -> p c q", q=CHUNK),
                                                            ACT.Identity, bias=v.bk_four[:, a:a + 1], scale=v.four_rows[:, a:a + 1])
                            last.then_inc(k_ready, 1)
                        if k == 0 and there(g + 2):
                            act.wait_ge(inputs_turned, g + 3)
                            if there(g + 1):
                                act.wait_ge(xc_low, g + 2)
                            nc.scalar.activation(xc[:], ps_aux[:].rearrange("p (n t) -> p n t", n=2), ACT.Copy).then_inc(xc_copied, 1)
                            act.wait_ge(xc_copied, g + 3)
                            if there(g + 1):
                                act.wait_ge(qk_done, g + 2)
                            nc.scalar.activation(xc_h[:], xc[:], ACT.Copy).then_inc(xc_high, 1)
                            if there(g + 1):
                                act.wait_ge(v_done, 2 * (g + 1) + 2)
                            nc.scalar.activation(ctx_rep[:], xc[:, 1].rearrange("p (c k) -> p c k", k=CHUNK).unsqueeze(2)
                                                 .broadcast_to([P, 2 * GB, 4, CHUNK]), ACT.Copy).then_inc(ctx_repeated, 1)
                        if there(g + 1):
                            act.wait_ge(shifted_ready, 2 * (g + 1) + k + 1)
                            if there(g):
                                act.wait_ge(normed_ready, 2 * g + k + 1)
                            nc.scalar.activation(probs[k][:], shifted[:], ACT.Exp).then_inc(exp_done, 1)
                        if there(g):
                            act.wait_ge(heads_done, 2 * g + k + 1)
                            if there(g - 1) or k:
                                act.wait_ge(projected, 2 * g + k)
                            nc.scalar.activation(heads_t[:].rearrange("p j c q -> p c j q"), ps_o[:].rearrange("p (c j q) -> p c j q", c=4, j=4), ACT.Identity,
                                                 bias=v.vec0[:, 2:3]).then_inc(heads_ready, 1)
                        if k == 1 and there(g + 3):
                            if there(g + 2):
                                act.wait_ge(inputs_turned, g + 3)
                            nc.scalar.activation(ctx_tile[:], v.cx[:, bass.ds(GT * (g + 3), GT), :], ACT.Copy).then_inc(ctx_staged, 1)

                act.wait_ge(v.x_loaded, 32)
                each_group(act, step)

            @block.vector
            def _(dve):
                def step(g, par):
                    for k in range(2):
                        n = 2 * g + k + 1
                        if there(g) and k == 0 or there(g + 1) and k == 1:
                            kk = (k + 1) % 2
                            dve.wait_ge(exp_done, n + 1)
                            if k == 1 and there(g + 2):
                                dve.wait_ge(rstd_ready, g + 3)
                            nc.vector.reduce_sum(sums[:].rearrange("p b c a -> p b (c a)"),
                                                 probs[kk][:].rearrange("p b (c q) -> p b c q", q=CHUNK), AX.X).then_inc(sums_done, 1)
                            dve.wait_ge(sums_done, n + 1)
                            nc.vector.tensor_tensor(sums_high[:], sums[:, :, 1], sums[:, :, 2], ALU.add).then_inc(sums_added, 1)
                            nc.vector.reciprocal(recip[kk][:, :, 0], sums[:, :, 0])
                            dve.wait_ge(sums_added, n + 1)
                            nc.vector.reciprocal(recip[kk][:, :, 1:3], sums_high[:].unsqueeze(2).broadcast_to([P, 2, 2, 4])).then_inc(recip_ready, 1)
                        if k == 1 and there(g + 3):
                            for t in range(GT):
                                last = nc.vector.bn_stats(stat6[:, t], v.xa[:, GT * (g + 3) + t, :])
                            last.then_inc(stats_ready, 1)
                        if k == 0 and there(g + 1):
                            for half, bank in enumerate((ps_qk, ps_aux)):
                                dve.wait_ge(v_done, 2 * (g + 1) + half + 1)
                                if half == 0 and there(g - 1):
                                    dve.wait_ge(heads_done, 2 * (g - 1) + 2)
                                nc.vector.tensor_tensor(v_exp[1 - par][:, 4 * half:4 * half + 4], bank[:].rearrange("p (c d) -> p c d", c=4),
                                                        v.four_cols[:].unsqueeze(1).broadcast_to([P, 4, D]), ALU.mult).then_inc(v_ready, 1)
                        if k == 0 and there(g + 2):
                            dve.wait_ge(xc_high, g + 3)
                            nc.vector.tensor_tensor(xc_l[:], xc[:], xc_h[:].bitcast(F32), ALU.subtract).then_inc(xc_low, 1)
                        if k == 0 and there(g - 1):
                            residual(g - 1, 1)
                        if there(g + 1):
                            m = 2 * (g + 1) + k
                            dve.wait_ge(scores_done, m + 1)
                            nc.vector.reduce_max(row_max[:].rearrange("p b c a -> p b (c a)"),
                                                 ps_s[:, :, 0:384].rearrange("p b (c q) -> p b c q", q=CHUNK), AX.X).then_inc(scores_maxed, 1)
                            dve.wait_ge(scores_maxed, m + 1)
                            nc.vector.tensor_tensor(row_max3[:, :, 1:3], row_max[:, :, 1].unsqueeze(2).broadcast_to([P, 2, 2, 4]),
                                                    row_max[:, :, 2].unsqueeze(2).broadcast_to([P, 2, 2, 4]), ALU.max)
                            nc.vector.tensor_copy(row_max3[:, :, 0], row_max[:, :, 0]).then_inc(max_spread, 1)
                            dve.wait_ge(max_spread, m + 1)
                            if there(g) or k:
                                dve.wait_ge(exp_done, m)
                            nc.vector.tensor_tensor(shifted[:].rearrange("p b (c q) -> p b c q", q=CHUNK),
                                                    ps_s[:, :, 0:384].rearrange("p b (c q) -> p b c q", q=CHUNK),
                                                    row_max3[:].rearrange("p b c a -> p b (c a)").unsqueeze(3).broadcast_to([P, 2, 12, CHUNK]),
                                                    ALU.subtract).then_inc(shifted_ready, 1)
                        if k == 1 and there(g):
                            residual(g, 0)
                        if k == 1 and there(g + 3):
                            dve.wait_ge(rstd_ready, g + 4)
                            if there(g + 2):
                                dve.wait_ge(inputs_turned, g + 3)
                            for t in range(GT):
                                last = nc.vector.tensor_scalar(x_hat[:, t], v.xa[:, GT * (g + 3) + t, :], rstd[:, t:t + 1], shift[:, t:t + 1],
                                                               ALU.mult, ALU.add)
                            last.then_inc(xhat_ready, 1)

                def residual(g, k):
                    n = 2 * g + k
                    dve.wait_ge(projected, n + 1)
                    dve.wait_ge(base_ready, g + 1)
                    if there(g - 1) or k:
                        dve.wait_ge(x1_ready, n)
                    nc.vector.scalar_tensor_tensor(v.xb[:, n, :], ps_y[:, 0:D], v.tgate[:, 0:1], v.xb[:, n, :], ALU.mult, ALU.add).then_inc(x1_ready, 1)
                    if there(g - 1) or k:
                        nc.vector.bn_stats(v.stat6[:, n - 1, :], v.xb[:, n - 1, :])

                dve.wait_ge(v.x_loaded, 32)
                each_group(dve, step)
                dve.wait_ge(x1_ready, NT)
                nc.vector.bn_stats(v.stat6[:, NT - 1, :], v.xb[:, NT - 1, :])

            @block.gpsimd
            def _(pool):
                def step(g, par):
                    for k in range(2):
                        n = 2 * g + k + 1
                        if there(g) and k == 0 or there(g + 1) and k == 1:
                            kk = (k + 1) % 2
                            pool.wait_ge(recip_ready, n + 1)
                            if there(g):
                                pool.wait_ge(probs_turned, n)
                            nc.gpsimd.tensor_tensor(normed[:].rearrange("p b (c q) -> p (b c) q", q=CHUNK),
                                                    probs[kk][:].rearrange("p b (c q) -> p (b c) q", q=CHUNK),
                                                    recip[kk][:].rearrange("p b c a -> p (b c a)").unsqueeze(2).broadcast_to([P, 24, CHUNK]),
                                                    ALU.mult).then_inc(normed_ready, 1)
                        if k == 1 and there(g + 3):
                            pool.wait_ge(stats_ready, g + 4)
                            if there(g + 2):
                                pool.wait_ge(xhat_ready, g + 3)
                            group_norm(nc, pool, v, stat6, rstd[:], shift[:], rstd_parts, 5 * (g + 3)).then_inc(rstd_ready, 1)
                        if k == 1 and there(g + 2):
                            pool.wait_ge(q_copied, g + 3)
                            if there(g):
                                pool.wait_ge(scores_done, 2 * g + 2)
                            nc.gpsimd.tensor_tensor(q_exp[par][:], q_flat[:].unsqueeze(2).broadcast_to([P, 2 * GB, 4, CHUNK]),
                                                    v.q_mask[:].unsqueeze(1).unsqueeze(3).broadcast_to([P, 2 * GB, 4, CHUNK]), ALU.mult
                                                    ).then_inc(q_ready, 1)
                        if k == 0 and there(g):
                            nc.gpsimd.tensor_tensor(v.xb[:, bass.ds(GT * g, GT), :], v.xa[:, bass.ds(GT * g, GT), :],
                                                    v.gbo[:].unsqueeze(1).broadcast_to([P, GT, D]), ALU.add).then_inc(base_ready, 1)

                pool.wait_ge(v.x_loaded, 32)
                each_group(pool, step)


def mixture0(nc, v):
    with ExitStack() as ctx:
        sb = lambda name, shape, dt=F32: ctx.enter_context(nc.sbuf_tensor(name, shape, dt))
        up_h, up_l = sb("b_up_h", [P, E, 2 * HID], F32R), sb("b_up_l", [P, E, 2 * HID], F32R)
        down_w, router_w = sb("b_down_w", [P, E, 2, D]), sb("b_router_w", [P, E])
        rstd, shift, rms = sb("b_rstd", [P, NT]), sb("b_shift", [P, NT]), sb("b_rms", [P, NT])
        mixture0_weights(nc, v, up_h, up_l, down_w, router_w, rstd, shift, rms)
        mixture0_main(nc, v, up_h, up_l, down_w, router_w, rstd, shift, rms)


def mixture0_weights(nc, v, up_h, up_l, down_w, router_w, rstd, shift, rms):
    with ExitStack() as ctx:
        sem = lambda name: ctx.enter_context(nc.semaphore(name))
        banks = [ctx.enter_context(nc.psum_tensor(f"bw_ps{i}", [P, 512], F32)) for i in range(4)]
        turned, high_done, bank_free = sem("turned"), sem("high_done"), sem("bank_free")
        UP, DOWN = E, E // 2
        work = ctx.enter_context(nc.sbuf_tensor("bw_work", [P, 6, NT], F32))
        steps, powed = sem("norm_steps"), sem("powed")
        with nc.Block() as block:

            @block.tensor
            def _(pe):
                pe.wait_ge(v.weights1_loaded, 64)
                for r in range(UP + DOWN + 1):
                    if r >= 4:
                        pe.wait_ge(bank_free, r - 3)
                    bank = banks[r % 4]
                    if r < UP:
                        parts = [v.w_up_raw[:, 4 * r + i] for i in range(4)]
                    elif r < UP + DOWN:
                        parts = [v.w_down_raw[:, 2 * (r - UP) + i // 2, (i % 2) * P:(i % 2 + 1) * P] for i in range(4)]
                    else:
                        nc.tensor.transpose(bank[:, 0:E], v.router0_raw[:], v.ident[0:E, 0:E]).then_inc(turned, 1)
                        break
                    for i, part in enumerate(parts):
                        last = nc.tensor.transpose(bank[:, i * P:(i + 1) * P], part, v.ident[:])
                    last.then_inc(turned, 1)

            @block.scalar
            def _(act):
                for r in range(UP + DOWN + 1):
                    act.wait_ge(turned, r + 1)
                    bank = banks[r % 4]
                    if r < UP:
                        nc.scalar.activation(up_h[:, r], bank[:], ACT.Copy).then_inc(high_done, 1)
                    elif r < UP + DOWN:
                        e = 2 * (r - UP)
                        nc.scalar.activation(down_w[:, e:e + 2], bank[:].rearrange("p (e c d) -> p e c d", e=2, c=2), ACT.Copy).then_inc(bank_free, 1)
                    else:
                        nc.scalar.activation(router_w[:], bank[:, 0:E], ACT.Copy)
                    if r == UP - 1:
                        act.wait_ge(bank_free, UP)

            @block.vector
            def _(dve):
                for r in range(UP):
                    dve.wait_ge(high_done, r + 1)
                    nc.vector.tensor_tensor(up_l[:, r], banks[r % 4][:], up_h[:, r].bitcast(F32), ALU.subtract).then_inc(bank_free, 1)
                mean, diff, var, rest, tmp, tmp2 = (work[:, i] for i in range(6))
                s = v.stat6
                nc.vector.tensor_tensor(mean, s[:, :, 1], s[:, :, 4], ALU.add)
                nc.vector.tensor_tensor(diff, s[:, :, 1], s[:, :, 4], ALU.subtract)
                nc.vector.tensor_tensor(rest, s[:, :, 2], s[:, :, 5], ALU.add).then_inc(steps, 1)
                dve.wait_ge(steps, 1)
                nc.vector.tensor_scalar(mean, mean, 0.5, None, ALU.mult)
                nc.vector.tensor_tensor(diff, diff, diff, ALU.mult)
                nc.vector.tensor_scalar(rest, rest, 1.0 / D, None, ALU.mult).then_inc(steps, 1)
                dve.wait_ge(steps, 2)
                nc.vector.scalar_tensor_tensor(var, diff, 0.25, rest, ALU.mult, ALU.add).then_inc(steps, 1)
                dve.wait_ge(steps, 3)
                nc.vector.tensor_scalar(tmp, var, LN_EPS, None, ALU.add).then_inc(steps, 1)
                dve.wait_ge(powed, 1)
                nc.vector.tensor_tensor(tmp2, rstd[:], rstd[:], ALU.mult)
                nc.vector.scalar_tensor_tensor(shift[:], mean, -1.0, rstd[:], ALU.mult, ALU.mult).then_inc(steps, 1)
                dve.wait_ge(steps, 5)
                nc.vector.tensor_tensor(tmp2, tmp2, var, ALU.mult).then_inc(steps, 1)
                dve.wait_ge(steps, 6)
                nc.vector.tensor_scalar(tmp2, tmp2, RMS_EPS, None, ALU.add).then_inc(steps, 1)

            @block.gpsimd
            def _(pool):
                tmp, tmp2 = work[:, 4], work[:, 5]
                pool.wait_ge(steps, 4)
                nc.gpsimd.tensor_tensor(rstd[:], tmp, v.minus_half[:], ALU.pow).then_inc(powed, 1)
                pool.wait_ge(steps, 7)
                nc.gpsimd.tensor_tensor(rms[:], tmp2, v.minus_half[:], ALU.pow).then_inc(powed, 1)


def mixture0_main(nc, v, up_h, up_l, down_w, router_w, rstd, shift, rms):
    C = GT * P
    with ExitStack() as ctx:
        sem = lambda name: ctx.enter_context(nc.semaphore(name))
        sb = lambda name, shape, dt=F32: ctx.enter_context(nc.sbuf_tensor(name, shape, dt))
        pb = lambda name, shape: ctx.enter_context(nc.psum_tensor(name, shape, F32))
        lat, normed = sb("b_lat", [P, GT, D]), sb("b_normed", [P, GT, D])
        xn = sb("b_xn", [P, C])
        xn_h, xn_l = sb("b_xn_h", [P, NG, C], F32R), sb("b_xn_l", [P, NG, C], F32R)
        weight = sb("b_weight", [P, NT, E])
        scores = sb("b_scores", [P, GT, E])
        best = [sb(f"b_best{i}", [P, GT, 1]) for i in range(2)]
        equal, ranked, chosen = sb("b_equal", [P, GT, E]), sb("b_ranked", [P, GT, E]), [sb(f"b_chosen{i}", [P, GT, E]) for i in range(2)]
        first = sb("b_first", [P, GT, 1])
        gap, ratio, one_plus = sb("b_gap", [P, GT, 1]), sb("b_ratio", [P, GT, 1]), sb("b_one_plus", [P, GT, 1])
        w_best = [sb(f"b_w_best{i}", [P, GT, 1]) for i in range(2)]
        parts = [sb(f"b_part{i}", [P, GT, E]) for i in range(2)]
        tanh_t = [sb(f"b_tanh{i}", [P, 2, C]) for i in range(2)]
        gated = [sb(f"b_gated{i}", [P, 2, C]) for i in range(2)]
        u_copy = [sb(f"b_u_copy{i}", [P, C]) for i in range(2)]
        hidden = [sb(f"b_hidden{i}", [P, 2, C]) for i in range(2)]
        ps_u = [pb(f"b_ps_u{i}", [P, 2, C]) for i in range(2)]
        ps_g = [pb(f"b_ps_g{i}", [P, 2, C]) for i in range(2)]
        ps_d = [pb(f"b_ps_d{i}", [P, 512]) for i in range(2)]
        ps_x, ps_r = pb("b_ps_x", [P, 512]), pb("b_ps_r", [P, 512])

        lat_ready, normed_ready, base_ready = sem("lat_ready"), sem("normed_ready"), sem("base_ready")
        x_turned, xn_ready, xn_high, xn_low = sem("x_turned"), sem("xn_ready"), sem("xn_high"), sem("xn_low")
        routed, routing, ratio_ready, weight_ready, weight_parts = sem("routed"), sem("routing"), sem("ratio_ready"), sem("weight_ready"), sem("weight_parts")
        gate_done, up_done, tanh_done, u_copied, gated_done = sem("gate_done"), sem("up_done"), sem("tanh_done"), sem("u_copied"), sem("gated_done")
        hidden0_done, hidden1_done, down_done, added = sem("hidden0_done"), sem("hidden1_done"), sem("down_done"), sem("added")
        ROUTE = 16

        with nc.Block() as block:

            def each_chunk(eng, step):
                for c in range(-2, 1):
                    step(c)
                with eng.Fori(1, NG - 2) as c:
                    step(c)
                for c in range(NG - 2, NG):
                    step(c)

            @block.tensor
            def _(pe):
                def up(c, e, bank, at):
                    pair = (xn_h[:, c, :], xn_l[:, c, :])
                    for f in range(2):
                        cols = slice(at + f * P, at + (f + 1) * P)
                        last = split_products(nc, bank[:, f], (up_h[:, e, cols], up_l[:, e, cols]), pair, True, True)
                    return last

                def gates(c, e):
                    n, par = E * c + e, e % 2
                    pe.wait_ge(xn_low, c + 1)
                    pe.wait_ge(xn_high, c + 1)
                    if there(c - 1) or e >= 2:
                        pe.wait_ge(gated_done, n - 1)
                    up(c, e, ps_g[par], HID).then_inc(gate_done, 1)

                def values(c, e):
                    n, par = E * c + e, e % 2
                    if there(c - 1) or e >= 2:
                        pe.wait_ge(hidden0_done, n - 1)
                    up(c, e, ps_u[par], 0).then_inc(up_done, 1)

                def down(c, e):
                    n, par = E * c + e, e % 2
                    pe.wait_ge(hidden0_done, n + 1)
                    pe.wait_ge(hidden1_done, n + 1)
                    if there(c - 1) or e >= 2:
                        pe.wait_ge(added, n - 1)
                    for t in range(GT):
                        for f in range(2):
                            last = nc.tensor.matmul(ps_d[par][:, t * P:(t + 1) * P], hidden[par][:, f, t * P:(t + 1) * P], down_w[:, e, f],
                                                    start=f == 0, stop=f == 1)
                    last.then_inc(down_done, 1)

                def step(c):
                    for e in range(E):
                        ahead = (c, e + 2) if e + 2 < E else (c + 1, e + 2 - E)
                        if there(ahead[0]):
                            gates(*ahead)
                        if there(c):
                            down(c, e)
                        if e == 0 and there(c + 1):
                            pe.wait_ge(normed_ready, c + 2)
                            for t in range(GT):
                                last = nc.tensor.transpose(ps_x[:, t * P:(t + 1) * P], normed[:, t], v.ident[:])
                            last.then_inc(x_turned, 1)
                        if e == 1 and there(c + 1):
                            pe.wait_ge(xn_ready, c + 2)
                            for t in range(GT):
                                last = nc.tensor.matmul(ps_r[:, t * E:(t + 1) * E], xn[:, t * P:(t + 1) * P], router_w[:], start=True, stop=True)
                            last.then_inc(routed, 1)
                        if there(ahead[0]):
                            values(*ahead)

                each_chunk(pe, step)

            @block.scalar
            def _(act):
                def unit(c, e, between):
                    n, par = E * c + e, e % 2
                    if there(c):
                        act.wait_ge(gate_done, n + 1)
                        if there(c - 1) or e >= 2:
                            act.wait_ge(gated_done, n - 1)
                        nc.scalar.activation(tanh_t[par][:], ps_g[par][:], ACT.Tanh, scale=0.5).then_inc(tanh_done, 1)
                    between()
                    if there(c):
                        if there(c - 1) or e >= 2:
                            act.wait_ge(hidden1_done, n - 1)
                        act.wait_ge(up_done, n + 1)
                        nc.scalar.activation(u_copy[par][:], ps_u[par][:, 1], ACT.Copy).then_inc(u_copied, 1)

                def prepare(c, e):
                    if e == 1 and there(c + 1):
                        act.wait_ge(x_turned, c + 2)
                        if there(c):
                            act.wait_ge(routed, c + 1)
                            act.wait_ge(xn_low, c + 1)
                        nc.scalar.activation(xn[:], ps_x[:, 0:C], ACT.Copy, scale=v.vec1[:, 0:1]).then_inc(xn_ready, 1)
                        act.wait_ge(xn_ready, c + 2)
                        nc.scalar.activation(xn_h[:, c + 1, :], xn[:], ACT.Copy).then_inc(xn_high, 1)
                    if e == 3 and there(c + 2):
                        if there(c + 1):
                            act.wait_ge(base_ready, c + 2)
                        for t in range(GT):
                            n = GT * (c + 2) + t
                            last = nc.scalar.activation(lat[:, t], v.xb[:, n, :], ACT.Identity, scale=rstd[:, bass.ds(n, 1)], bias=shift[:, bass.ds(n, 1)])
                        last.then_inc(lat_ready, 1)
                    if e == 4 and there(c + 2):
                        act.wait_ge(lat_ready, c + 3)
                        if there(c + 1):
                            act.wait_ge(x_turned, c + 2)
                        for t in range(GT):
                            last = nc.scalar.activation(normed[:, t], lat[:, t], ACT.Copy, scale=rms[:, bass.ds(GT * (c + 2) + t, 1)])
                        last.then_inc(normed_ready, 1)

                def step(c):
                    for e in range(E):
                        unit(*((c, e + 1) if e + 1 < E else (c + 1, 0)), lambda: prepare(c, e))
                        if e == 5 and there(c + 1):
                            act.wait_ge(routing, ROUTE * (c + 1) + 9)
                            nc.scalar.activation(ratio[:], gap[:], ACT.Exp).then_inc(ratio_ready, 1)

                each_chunk(act, step)

            @block.vector
            def _(dve):
                def unit(c, e, between):
                    n, par = E * c + e, e % 2
                    if there(c):
                        dve.wait_ge(tanh_done, n + 1)
                        if there(c - 1) or e >= 2:
                            dve.wait_ge(hidden1_done, n - 1)
                        nc.vector.scalar_tensor_tensor(gated[par][:], tanh_t[par][:], 1.0, ps_g[par][:], ALU.add, ALU.mult).then_inc(gated_done, 1)
                    between()
                    if there(c):
                        dve.wait_ge(u_copied, n + 1)
                        dve.wait_ge(gated_done, n + 1)
                        if there(c - 1) or e >= 2:
                            dve.wait_ge(down_done, n - 1)
                        nc.vector.tensor_tensor(hidden[par][:, 0], gated[par][:, 0], ps_u[par][:, 0], ALU.mult).then_inc(hidden0_done, 1)

                def add(c, e):
                    n, par = E * c + e, e % 2
                    dve.wait_ge(down_done, n + 1)
                    if e == 0:
                        dve.wait_ge(weight_ready, c + 1)
                        dve.wait_ge(base_ready, c + 1)
                    else:
                        dve.wait_ge(added, n)
                    for t in range(GT):
                        tile = v.xa[:, GT * c + t, :]
                        last = nc.vector.scalar_tensor_tensor(tile, ps_d[par][:, t * P:(t + 1) * P], weight[:, GT * c + t, e:e + 1], tile,
                                                              ALU.mult, ALU.add)
                    last.then_inc(added, 1)

                def pick(k, i):
                    if i == 0:
                        return nc.vector.reduce_max(best[k][:, :, 0], scores[:], AX.X)
                    if i == 1:
                        return nc.vector.tensor_tensor(equal[:], scores[:], best[k][:].broadcast_to([P, GT, E]), ALU.is_equal)
                    if i == 2:
                        return nc.vector.tensor_tensor(ranked[:], equal[:], v.first_wins[:].unsqueeze(1).broadcast_to([P, GT, E]), ALU.mult)
                    if i == 3:
                        return nc.vector.reduce_max(first[:, :, 0], ranked[:], AX.X)
                    return nc.vector.tensor_tensor(chosen[k][:], ranked[:], first[:].broadcast_to([P, GT, E]), ALU.is_equal)

                def route(c, i):
                    if not there(c) or not 0 <= i < ROUTE:
                        return
                    if i == 0:
                        dve.wait_ge(routed, c + 1)
                        if there(c - 1):
                            dve.wait_ge(weight_ready, c)
                        last = nc.vector.tensor_copy(scores[:], ps_r[:, 0:GT * E].rearrange("p (t e) -> p t e", t=GT))
                    else:
                        dve.wait_ge(routing, ROUTE * c + i)
                    if 1 <= i <= 5:
                        last = pick(0, i - 1)
                    if i == 6:
                        last = nc.vector.scalar_tensor_tensor(scores[:], chosen[0][:], -BIG, scores[:], ALU.mult, ALU.add)
                    if i == 7:
                        last = pick(1, 0)
                    if i == 8:
                        last = nc.vector.tensor_tensor(gap[:], best[1][:], best[0][:], ALU.subtract)
                    if 9 <= i <= 12:
                        last = pick(1, i - 8)
                    if i == 13:
                        dve.wait_ge(ratio_ready, c + 1)
                        last = nc.vector.tensor_scalar(one_plus[:], ratio[:], 1.0, None, ALU.add)
                    if i == 14:
                        last = nc.vector.reciprocal(one_plus[:], one_plus[:])
                    if i == 15:
                        last = nc.vector.tensor_scalar(w_best[0][:], one_plus[:], v.half_gate[:, 0:1], None, ALU.mult)
                    last.then_inc(routing, 1)

                def step(c):
                    for e in range(E):
                        at = 3 * (e - 2) + (1 if e > 4 else 0)
                        unit(*((c, e + 1) if e + 1 < E else (c + 1, 0)), lambda: route(c + 1, at))
                        route(c + 1, at + 1)
                        if there(c):
                            add(c, e)
                        route(c + 1, at + 2)
                        if e == 4:
                            route(c + 1, at + 3)
                        if e == 3 and there(c) and there(c - 1):
                            for t in range(GT):
                                nc.vector.bn_stats(v.stat6[:, GT * (c - 1) + t, :], v.xa[:, GT * (c - 1) + t, :])
                        if e == 0 and there(c + 1):
                            dve.wait_ge(lat_ready, c + 2)
                            nc.vector.scalar_tensor_tensor(v.xa[:, bass.ds(GT * (c + 1), GT), :], lat[:], v.tgate[:, 2:3],
                                                           v.xb[:, bass.ds(GT * (c + 1), GT), :], ALU.mult, ALU.add).then_inc(base_ready, 1)
                        if e == 1 and there(c + 1):
                            dve.wait_ge(xn_high, c + 2)
                            nc.vector.tensor_tensor(xn_l[:, c + 1, :], xn[:], xn_h[:, c + 1, :].bitcast(F32), ALU.subtract).then_inc(xn_low, 1)

                each_chunk(dve, step)
                dve.wait_ge(added, E * NG)
                for n in range(NT - GT, NT):
                    nc.vector.bn_stats(v.stat6[:, n, :], v.xa[:, n, :])

            @block.gpsimd
            def _(pool):
                def unit(c, e):
                    n, par = E * c + e, e % 2
                    pool.wait_ge(gated_done, n + 1)
                    pool.wait_ge(u_copied, n + 1)
                    if there(c - 1) or e >= 2:
                        pool.wait_ge(down_done, n - 1)
                    nc.gpsimd.tensor_tensor(hidden[par][:, 1], gated[par][:, 1], u_copy[par][:], ALU.mult).then_inc(hidden1_done, 1)

                def step(c):
                    for e in range(E):
                        if there(c):
                            unit(c, e)
                        if e == 7 and there(c + 1):
                            at = 2 * (c + 1)
                            pool.wait_ge(routing, ROUTE * (c + 2))
                            nc.gpsimd.tensor_tensor(w_best[1][:], w_best[0][:], ratio[:], ALU.mult).then_inc(weight_parts, 1)
                            nc.gpsimd.tensor_tensor(parts[0][:], chosen[0][:], w_best[0][:].broadcast_to([P, GT, E]), ALU.mult)
                            pool.wait_ge(weight_parts, at + 1)
                            nc.gpsimd.tensor_tensor(parts[1][:], chosen[1][:], w_best[1][:].broadcast_to([P, GT, E]), ALU.mult).then_inc(weight_parts, 1)
                            pool.wait_ge(weight_parts, at + 2)
                            nc.gpsimd.tensor_tensor(weight[:, bass.ds(GT * (c + 1), GT), :], parts[0][:], parts[1][:], ALU.add).then_inc(weight_ready, 1)

                each_chunk(pool, step)


def norms(nc, dve, v, stats, work, rstd, shift, steps, powed, at):
    mean, diff, var, rest, tmp = (work[:, i] for i in range(5))
    s, p = 5 * at, at
    nc.vector.tensor_tensor(mean, stats[:, :, 1], stats[:, :, 4], ALU.add)
    nc.vector.tensor_tensor(diff, stats[:, :, 1], stats[:, :, 4], ALU.subtract)
    nc.vector.tensor_tensor(rest, stats[:, :, 2], stats[:, :, 5], ALU.add).then_inc(steps, 1)
    dve.wait_ge(steps, s + 1)
    nc.vector.tensor_scalar(mean, mean, 0.5, None, ALU.mult)
    nc.vector.tensor_tensor(diff, diff, diff, ALU.mult)
    nc.vector.tensor_scalar(rest, rest, 1.0 / D, None, ALU.mult).then_inc(steps, 1)
    dve.wait_ge(steps, s + 2)
    nc.vector.scalar_tensor_tensor(var, diff, 0.25, rest, ALU.mult, ALU.add).then_inc(steps, 1)
    dve.wait_ge(steps, s + 3)
    nc.vector.tensor_scalar(tmp, var, LN_EPS, None, ALU.add).then_inc(steps, 1)
    dve.wait_ge(powed, p + 1)
    nc.vector.scalar_tensor_tensor(shift, mean, -1.0, rstd, ALU.mult, ALU.mult).then_inc(steps, 1)
    dve.wait_ge(steps, s + 5)
    return mean, var


def power(nc, pool, v, work, rstd, steps, powed, at):
    pool.wait_ge(steps, 5 * at + 4)
    nc.gpsimd.tensor_tensor(rstd, work[:, 4], v.minus_half[:], ALU.pow).then_inc(powed, 1)


def attention1(nc, v):
    with ExitStack() as ctx:
        sb = lambda name, shape, dt=F32: ctx.enter_context(nc.sbuf_tensor(name, shape, dt))
        w = Env()
        w.m_h, w.m_l = sb("c_m_h", [P, H, D], F32R), sb("c_m_l", [P, H, D], F32R)
        w.n_h, w.n_l = sb("c_n_h", [P, H, D], F32R), sb("c_n_l", [P, H, D], F32R)
        w.rstd, w.shift = sb("c_rstd", [P, NT]), sb("c_shift", [P, NT])
        w.ctx_rstd, w.ctx_shift = sb("c_ctx_rstd", [P, NT]), sb("c_ctx_shift", [P, NT])
        w.mask_bias = sb("c_mask_bias", [1, BATCH, SEQ], BF16)
        attention1_weights(nc, v, w)
        attention1_main(nc, v, w)


def attention1_weights(nc, v, w):
    with ExitStack() as ctx:
        sem = lambda name: ctx.enter_context(nc.semaphore(name))
        sb = lambda name, shape, dt=F32: ctx.enter_context(nc.sbuf_tensor(name, shape, dt))
        banks = [ctx.enter_context(nc.psum_tensor(f"cw_ps{i}", [P, 512], F32)) for i in range(4)]
        turned_w = sb("cw_turned", [P, 3, H // 2, D])
        ctx_stats, work, extra = sb("cw_ctx_stats", [P, NT, 6]), sb("cw_work", [P, 5, NT]), sb("cw_extra", [P, 2, NT])
        turned, copied = sem("turned"), sem("copied")
        product_done, high_done, low_done = sem("product_done"), sem("high_done"), sem("low_done")
        steps, powed, extra_steps, extra_powed, stats_done = sem("steps"), sem("powed"), sem("extra_steps"), sem("extra_powed"), sem("stats_done")
        TURNS, PRODUCTS = 6, 2 * H // 4
        first_head = lambda r: 8 * (r % 4 // 2) + r % 2
        heads_of = lambda r: slice(first_head(r), first_head(r) + 7, 2)
        with nc.Block() as block:

            @block.tensor
            def _(pe):
                pe.wait_ge(v.weights2_loaded, 128)
                for r in range(TURNS):
                    if r >= 4:
                        pe.wait_ge(copied, r - 3)
                    for i in range(4):
                        pair = 4 * (r % 2) + i
                        source = (v.wq1_raw, v.wkv1_raw, v.wkv1_raw)[r // 2]
                        at = pair * P + (H * HD1 if r // 2 == 2 else 0)
                        last = nc.tensor.transpose(banks[r % 4][:, i * P:(i + 1) * P], source[:, at:at + P], v.ident[:])
                    last.then_inc(turned, 1)
                pe.wait_ge(copied, TURNS)
                for r in range(PRODUCTS):
                    if r >= 4:
                        pe.wait_ge(low_done, r - 3)
                    for i in range(4):
                        h = first_head(r) + 2 * i
                        rows = slice(HD1 * (h % 2), HD1 * (h % 2 + 1))
                        left, right = ((turned_w[rows, 0, h // 2], turned_w[rows, 1, h // 2]) if r < 4
                                       else (turned_w[rows, 2, h // 2], v.wout1_raw[rows, h // 2]))
                        last = nc.tensor.matmul(banks[r % 4][:, i * P:(i + 1) * P], left, right, start=True, stop=True)
                    last.then_inc(product_done, 1)

            @block.scalar
            def _(act):
                for r in range(TURNS):
                    act.wait_ge(turned, r + 1)
                    nc.scalar.activation(turned_w[:, r // 2, 4 * (r % 2):4 * (r % 2) + 4], banks[r % 4][:].rearrange("p (i d) -> p i d", i=4),
                                         ACT.Copy).then_inc(copied, 1)
                for r in range(PRODUCTS):
                    act.wait_ge(product_done, r + 1)
                    high = (w.m_h, w.n_h)[r // 4][:, heads_of(r)]
                    nc.scalar.activation(high, banks[r % 4][:].rearrange("p (i d) -> p i d", i=4), ACT.Copy,
                                         scale=float(HD1) ** -0.5 if r < 4 else 1.0).then_inc(high_done, 1)

            @block.vector
            def _(dve):
                for n in range(NT):
                    last = nc.vector.bn_stats(ctx_stats[:, n], v.cx[:, n, :])
                last.then_inc(stats_done, 1)
                dve.wait_ge(v.weights2_loaded, 128)
                nc.vector.tensor_scalar(w.mask_bias[:], v.mask_u8[:].rearrange("a (b s) -> a b s", b=BATCH), -1.0, 3e38, ALU.add, ALU.mult)
                for r in range(PRODUCTS):
                    dve.wait_ge(high_done, r + 1)
                    high, low = ((w.m_h, w.m_l), (w.n_h, w.n_l))[r // 4]
                    nc.vector.scalar_tensor_tensor(low[:, heads_of(r)], banks[r % 4][:].rearrange("p (i d) -> p i d", i=4),
                                                   float(HD1) ** -0.5 if r < 4 else 1.0, high[:, heads_of(r)].bitcast(F32),
                                                   ALU.mult, ALU.subtract).then_inc(low_done, 1)
                dve.wait_ge(stats_done, 1)
                norms(nc, dve, v, ctx_stats, work, w.ctx_rstd[:], w.ctx_shift[:], steps, powed, 0)
                mean, var = norms(nc, dve, v, v.stat6, work, w.rstd[:], w.shift[:], steps, powed, 1)
                nc.vector.tensor_tensor(extra[:, 0], w.rstd[:], w.rstd[:], ALU.mult).then_inc(extra_steps, 1)
                dve.wait_ge(extra_steps, 1)
                nc.vector.tensor_tensor(extra[:, 0], extra[:, 0], var, ALU.mult).then_inc(extra_steps, 1)
                dve.wait_ge(extra_steps, 2)
                nc.vector.tensor_scalar(extra[:, 0], extra[:, 0], LN_EPS, None, ALU.add).then_inc(extra_steps, 1)
                dve.wait_ge(extra_powed, 1)
                nc.vector.tensor_tensor(w.rstd[:], w.rstd[:], extra[:, 1], ALU.mult)
                nc.vector.tensor_tensor(w.shift[:], w.shift[:], extra[:, 1], ALU.mult)

            @block.gpsimd
            def _(pool):
                power(nc, pool, v, work, w.ctx_rstd[:], steps, powed, 0)
                power(nc, pool, v, work, w.rstd[:], steps, powed, 1)
                pool.wait_ge(extra_steps, 3)
                nc.gpsimd.tensor_tensor(extra[:, 1], extra[:, 0], v.minus_half[:], ALU.pow).then_inc(extra_powed, 1)


def attention1_main(nc, v, w):
    C = GT * P
    U = 2 * GB
    HH = H // 2
    KEYS = 2 * SEQ
    with ExitStack() as ctx:
        sem = lambda name: ctx.enter_context(nc.semaphore(name))
        sb = lambda name, shape, dt=F32: ctx.enter_context(nc.sbuf_tensor(name, shape, dt))
        pb = lambda name, shape: ctx.enter_context(nc.psum_tensor(name, shape, F32))
        hat = sb("c_hat", [P, 2, GT, D])
        kv_t = [sb(f"c_kv_t{i}", [P, GB, KEYS]) for i in range(2)]
        kv_h = [sb(f"c_kv_h{i}", [P, GB, D], F32R) for i in range(2)]
        kv_l = [sb(f"c_kv_l{i}", [P, GB, D], F32R) for i in range(2)]
        lat_h = [sb(f"c_lat_h{i}", [P, GB, SEQ], F32R) for i in range(2)]
        lat_l = [sb(f"c_lat_l{i}", [P, GB, SEQ], F32R) for i in range(2)]
        q_t = sb("c_q_t", [P, GB, H, SEQ])
        neg_max, sums, recip = ([sb(f"c_{name}{i}", [P, 4]) for i in range(2)] for name in ("neg_max", "sums", "recip"))
        probs = [sb(f"c_probs{i}", [P, 4, KEYS]) for i in range(2)]
        normed = [sb(f"c_normed{i}", [P, 4, KEYS]) for i in range(2)]
        probs_h, probs_l = sb("c_probs_h", [P, 512], F32R), sb("c_probs_l", [P, 512], F32R)
        y_h, y_l = sb("c_y_h", [P, H, C], F32R), sb("c_y_l", [P, H, C], F32R)
        out_t = sb("c_out_t", [P, C])

        ps_s = [pb(f"c_ps_s{i}", [P, 4, KEYS]) for i in range(2)]
        ps_q = [pb(f"c_ps_q{i}", [P, 2, C]) for i in range(2)]
        ps_t, ps_y, ps_o, ps_x = (pb(f"c_ps_{n}", [P, 512]) for n in "tyox")

        hat_ready, hat_turned, kv_t_ready, lat_high, lat_low = (sem(n) for n in ("hat_ready", "hat_turned", "kv_t_ready", "lat_high", "lat_low"))
        kv_turned, kv_high, kv_low = sem("kv_turned"), sem("kv_high"), sem("kv_low")
        q_done, q_ready, scores_done, max_ready, exp_done, recip_ready, normed_ready = (
            sem(n) for n in ("q_done", "q_ready", "scores_done", "max_ready", "exp_done", "recip_ready", "normed_ready"))
        probs_turned, probs_high, probs_low = sem("probs_turned"), sem("probs_high"), sem("probs_low")
        y_done, y_high, y_low = sem("y_done"), sem("y_high"), sem("y_low")
        out_done, out_copied, out_turned, x3_ready = sem("out_done"), sem("out_copied"), sem("out_turned"), sem("x3_ready")

        with nc.Block() as block:

            def each_group(eng, step):
                for g in range(-2, 2):
                    step(g, g % 2)
                with eng.Fori(1, NG // 2 - 1) as i:
                    step(2 * i, 0)
                    step(2 * i + 1, 1)
                for g in range(NG - 2, NG + 1):
                    step(g, g % 2)

            def ahead(g, u, k):
                return (g, u + k, 0) if u + k < U else (g + 1, u + k - U, 1)

            def q_heads(g, u):
                return (g, 6 + u, 0) if u < 2 else (g + 1, u - 2, 1)

            def out_heads(g, u):
                return (g - 1, 3 + u) if u < 5 else (g, u - 5)

            def before(g, u):
                return (g, u - 1, 0) if u else (g - 1, U - 1, 1)

            @block.tensor
            def _(pe):
                def step(g, par):
                    for u in range(U):
                        n = U * g + u
                        if u == 0 and there(g + 1):
                            pe.wait_ge(hat_ready, g + 2)
                            if there(g - 2):
                                pe.wait_ge(x3_ready, g - 1)
                            for k in range(2):
                                for t in range(GT):
                                    last = nc.tensor.transpose(ps_x[:, (2 * k + t) * P:(2 * k + t + 1) * P], hat[:, k, t], v.ident[:])
                            last.then_inc(hat_turned, 1)
                        gq, pair, flip = q_heads(g, u)
                        if there(gq):
                            lat = par ^ flip
                            pe.wait_ge(lat_low, gq + 1)
                            if there(gq - 1) or pair >= 2:
                                pe.wait_ge(q_ready, 8 * gq + pair - 1)
                            for i in range(2):
                                h = 2 * pair + i
                                last = split_products(nc, ps_q[pair % 2][:, i], (w.m_h[:, h], w.m_l[:, h]),
                                                      (lat_h[lat][:].rearrange("p b s -> p (b s)"), lat_l[lat][:].rearrange("p b s -> p (b s)")), True, True)
                            last.then_inc(q_done, 1)
                        if u == 3 and there(g + 1):
                            pe.wait_ge(kv_t_ready, 2 * (g + 1) + 2)
                            pe.wait_ge(lat_low, g + 2)
                            for b in range(GB):
                                last = nc.tensor.transpose(ps_x[:, b * P:(b + 1) * P], kv_t[1 - par][:, b], v.ident[:])
                            last.then_inc(kv_turned, 1)
                        gb, ub, flip = before(g, u)
                        if there(gb):
                            pe.wait_ge(probs_low, n)
                            pe.wait_ge(kv_low, gb + 1)
                            if there(gb - 1) or ub:
                                pe.wait_ge(y_low, n - 1)
                            b, own = ub % GB, par ^ flip
                            split_products(nc, ps_y[:], (kv_h[own][:, b], kv_l[own][:, b]), (probs_h[:], probs_l[:]), True, True).then_inc(y_done, 1)
                        if there(g):
                            pe.wait_ge(normed_ready, n + 1)
                            if there(g - 1) or u:
                                pe.wait_ge(probs_low, n)
                            for i in range(4):
                                last = nc.tensor.transpose(ps_t[:, i * P:(i + 1) * P], normed[u % 2][:, i], v.ident[:])
                            last.then_inc(probs_turned, 1)
                        gs, us, flip = ahead(g, u, 2)
                        if there(gs):
                            b, half = us % GB, us // GB
                            pe.wait_ge(q_ready, 8 * gs + 4 * (half + 1))
                            pe.wait_ge(kv_t_ready, 2 * gs + 2)
                            if there(g):
                                pe.wait_ge(exp_done, n + 1)
                            bank = ps_s[us % 2]
                            for i in range(4):
                                h = HH * half + 2 * i
                                nc.tensor.matmul(bank[:, i], q_t[:, b, h:h + 2].rearrange("p h s -> p (h s)"), kv_t[par ^ flip][:, b],
                                                 start=i == 0, stop=False, skip_group_check=True)
                            nc.tensor.matmul(bank[:, :, 0:SEQ], v.ones_row[:], w.mask_bias[:, GB * gs + b, :].unsqueeze(1).broadcast_to([1, 4, SEQ]),
                                             start=False, stop=True, skip_group_check=True).then_inc(scores_done, 1)
                        if u == 6 and there(g - 1):
                            pe.wait_ge(out_copied, g)
                            if there(g + 1):
                                pe.wait_ge(kv_low, g + 2)
                            for t in range(GT):
                                last = nc.tensor.transpose(ps_x[:, t * P:(t + 1) * P], out_t[:, t * P:(t + 1) * P], v.ident[:])
                            last.then_inc(out_turned, 1)
                        go, pair = out_heads(g, u)
                        if there(go):
                            if pair == 0 and there(go - 1):
                                pe.wait_ge(out_copied, go)
                            pe.wait_ge(y_low, U * go + 4 * (pair // 4 + 1))
                            for h in (2 * pair, 2 * pair + 1):
                                last = split_products(nc, ps_o[:, 0:C], (w.n_h[:, h], w.n_l[:, h]), (y_h[:, h], y_l[:, h]), h == 0, h == H - 1)
                            if pair == 7:
                                last.then_inc(out_done, 1)

                each_group(pe, step)

            @block.scalar
            def _(act):
                def step(g, par):
                    for u in range(U):
                        n = U * g + u
                        if u == 0 and there(g + 1):
                            act.wait_ge(hat_turned, g + 2)
                            for k in range(2):
                                nc.scalar.activation(kv_t[1 - par][:, :, k * SEQ:(k + 1) * SEQ],
                                                     ps_x[:, k * C:(k + 1) * C].rearrange("p (b s) -> p b s", b=GB), ACT.Identity,
                                                     bias=v.vec2[:, 2 * k + 1:2 * k + 2], scale=v.vec2[:, 2 * k:2 * k + 1]).then_inc(kv_t_ready, 1)
                            act.wait_ge(kv_t_ready, 2 * (g + 1) + 2)
                            nc.scalar.activation(lat_h[1 - par][:], kv_t[1 - par][:, :, SEQ:KEYS], ACT.Copy).then_inc(lat_high, 1)
                        if u == 5 and there(g - 1):
                            act.wait_ge(out_done, g)
                            if there(g - 2):
                                act.wait_ge(out_turned, g - 1)
                            nc.scalar.activation(out_t[:], ps_o[:, 0:C], ACT.Copy).then_inc(out_copied, 1)
                        gb, ub, _ = before(g, u)
                        if there(gb):
                            act.wait_ge(y_done, n)
                            b, half = ub % GB, ub // GB
                            nc.scalar.activation(y_h[:, HH * half:HH * (half + 1), b * SEQ:(b + 1) * SEQ], ps_y[:].rearrange("p (h s) -> p h s", h=HH),
                                                 ACT.Copy).then_inc(y_high, 1)
                        if there(g):
                            act.wait_ge(probs_turned, n + 1)
                            if there(g - 1) or u:
                                act.wait_ge(y_done, n)
                            nc.scalar.activation(probs_h[:], ps_t[:], ACT.Copy).then_inc(probs_high, 1)
                        if u == 3 and there(g + 1):
                            act.wait_ge(kv_turned, g + 2)
                            nc.scalar.activation(kv_h[1 - par][:], ps_x[:].rearrange("p (b d) -> p b d", b=GB), ACT.Copy).then_inc(kv_high, 1)
                        gs, us, flip = ahead(g, u, 2)
                        if there(gs):
                            act.wait_ge(max_ready, U * gs + us + 1)
                            if there(g):
                                act.wait_ge(normed_ready, n + 1)
                            for i in range(4):
                                last = nc.scalar.activation(probs[us % 2][:, i], ps_s[us % 2][:, i], ACT.Exp, bias=neg_max[us % 2][:, i:i + 1],
                                                            accum_out=sums[us % 2][:, i:i + 1])
                            last.then_inc(exp_done, 1)

                each_group(act, step)

            @block.vector
            def _(dve):
                def step(g, par):
                    for u in range(U):
                        n = U * g + u
                        gq, pair, _ = q_heads(g, u)
                        if there(gq):
                            dve.wait_ge(q_done, 8 * gq + pair + 1)
                            nc.vector.tensor_copy(q_t[:, :, 2 * pair:2 * pair + 2].rearrange("p b h s -> p h b s"),
                                                  ps_q[pair % 2][:].rearrange("p h (b s) -> p h b s", b=GB)).then_inc(q_ready, 1)
                        g1, u1, _ = ahead(g, u, 1)
                        if there(g1):
                            n1 = U * g1 + u1
                            dve.wait_ge(exp_done, n1 + 1)
                            if there(g1 - 1) or u1 >= 2:
                                dve.wait_ge(normed_ready, n1 - 1)
                            nc.vector.reciprocal(recip[u1 % 2][:], sums[u1 % 2][:]).then_inc(recip_ready, 1)
                        if u == 0 and there(g + 1):
                            dve.wait_ge(lat_high, g + 2)
                            nc.vector.tensor_tensor(lat_l[1 - par][:], kv_t[1 - par][:, :, SEQ:KEYS], lat_h[1 - par][:].bitcast(F32), ALU.subtract
                                                    ).then_inc(lat_low, 1)
                        gb, ub, _ = before(g, u)
                        if there(gb):
                            b, half = ub % GB, ub // GB
                            dve.wait_ge(y_high, n)
                            nc.vector.tensor_tensor(y_l[:, HH * half:HH * (half + 1), b * SEQ:(b + 1) * SEQ], ps_y[:].rearrange("p (h s) -> p h s", h=HH),
                                                    y_h[:, HH * half:HH * (half + 1), b * SEQ:(b + 1) * SEQ].bitcast(F32), ALU.subtract).then_inc(y_low, 1)
                        gs, us, _ = ahead(g, u, 2)
                        if there(gs):
                            dve.wait_ge(scores_done, U * gs + us + 1)
                            nc.vector.tensor_reduce(neg_max[us % 2][:], ps_s[us % 2][:], AX.X, ALU.max, negate=True).then_inc(max_ready, 1)
                        if there(g):
                            dve.wait_ge(probs_high, n + 1)
                            nc.vector.tensor_tensor(probs_l[:], ps_t[:], probs_h[:].bitcast(F32), ALU.subtract).then_inc(probs_low, 1)
                        if u == 3 and there(g + 1):
                            dve.wait_ge(kv_high, g + 2)
                            nc.vector.tensor_tensor(kv_l[1 - par][:], ps_x[:].rearrange("p (b d) -> p b d", b=GB), kv_h[1 - par][:].bitcast(F32),
                                                    ALU.subtract).then_inc(kv_low, 1)
                        if u == 6 and there(g - 1):
                            residual(g - 1)
                        if u == 4 and there(g + 2):
                            if there(g + 1):
                                dve.wait_ge(hat_turned, g + 2)
                            for k, (source, rstd, shift) in enumerate(((v.cx, w.ctx_rstd, w.ctx_shift), (v.xa, w.rstd, w.shift))):
                                for t in range(GT):
                                    at = GT * (g + 2) + t
                                    last = nc.vector.tensor_scalar(hat[:, k, t], source[:, at, :], rstd[:, bass.ds(at, 1)], shift[:, bass.ds(at, 1)],
                                                                   ALU.mult, ALU.add)
                            last.then_inc(hat_ready, 1)

                def residual(g):
                    dve.wait_ge(out_turned, g + 1)
                    if there(g - 1):
                        dve.wait_ge(x3_ready, g)
                    for t in range(GT):
                        n = GT * g + t
                        last = nc.vector.scalar_tensor_tensor(v.xb[:, n, :], ps_x[:, t * P:(t + 1) * P], v.tgate[:, 1:2], v.xa[:, n, :], ALU.mult, ALU.add)
                    last.then_inc(x3_ready, 1)
                    if there(g - 1):
                        for t in range(GT):
                            nc.vector.bn_stats(v.stat6[:, GT * (g - 1) + t, :], v.xb[:, GT * (g - 1) + t, :])

                each_group(dve, step)
                dve.wait_ge(x3_ready, NG)
                for n in range(NT - GT, NT):
                    nc.vector.bn_stats(v.stat6[:, n, :], v.xb[:, n, :])

            @block.gpsimd
            def _(pool):
                def step(g, par):
                    for u in range(U):
                        g1, u1, _ = ahead(g, u, 1)
                        if not there(g1):
                            continue
                        n1 = U * g1 + u1
                        pool.wait_ge(recip_ready, n1 + 1)
                        if there(g1 - 1) or u1 >= 2:
                            pool.wait_ge(probs_turned, n1 - 1)
                        nc.gpsimd.tensor_tensor(normed[u1 % 2][:], probs[u1 % 2][:], recip[u1 % 2][:].unsqueeze(2).broadcast_to([P, 4, KEYS]), ALU.mult
                                                ).then_inc(normed_ready, 1)

                each_group(pool, step)


def mixture1(nc, v, out):
    with ExitStack() as ctx:
        sb = lambda name, shape, dt=F32: ctx.enter_context(nc.sbuf_tensor(name, shape, dt))
        w = Env()
        w.e_h, w.e_l, w.router = sb("d_e_h", [P, E * D], F32R), sb("d_e_l", [P, E * D], F32R), sb("d_router", [P, E])
        w.bias_pair, w.ones_pair = sb("d_bias_pair", [2, E * D], F32R), sb("d_ones_pair", [2, P], F32R)
        w.rstd, w.shift = sb("d_rstd", [P, NT]), sb("d_shift", [P, NT])
        mixture1_weights(nc, v, w)
        mixture1_main(nc, v, w, out)


def mixture1_weights(nc, v, w):
    with ExitStack() as ctx:
        sem = lambda name: ctx.enter_context(nc.semaphore(name))
        sb = lambda name, shape, dt=F32: ctx.enter_context(nc.sbuf_tensor(name, shape, dt))
        banks = [ctx.enter_context(nc.psum_tensor(f"dw_ps{i}", [P, 512], F32)) for i in range(3)]
        work = sb("dw_work", [P, 5, NT])
        bias_high, bias_low, bias_top = sb("dw_bias_high", [2, E * D], F32R), sb("dw_bias_low", [2, E * D]), sb("dw_bias_top", [2, E * D])
        turned, high_done, steps, powed, bias_steps = sem("turned"), sem("high_done"), sem("steps"), sem("powed"), sem("bias_steps")
        with nc.Block() as block:

            @block.tensor
            def _(pe):
                pe.wait_ge(v.weights3_loaded, 64)
                for r in range(2):
                    for i in range(4):
                        last = nc.tensor.transpose(banks[r][:, i * P:(i + 1) * P], v.expert_raw[:, 4 * r + i], v.ident[:])
                    last.then_inc(turned, 1)
                nc.tensor.transpose(banks[2][:, 0:E], v.router1_raw[:], v.ident[0:E, 0:E]).then_inc(turned, 1)

            @block.scalar
            def _(act):
                for r in range(2):
                    act.wait_ge(turned, r + 1)
                    nc.scalar.activation(w.e_h[:, r * 512:(r + 1) * 512], banks[r][:], ACT.Copy).then_inc(high_done, 1)
                act.wait_ge(turned, 3)
                nc.scalar.activation(w.router[:], banks[2][:, 0:E], ACT.Copy)

            @block.vector
            def _(dve):
                dve.wait_ge(v.weights3_loaded, 64)
                nc.vector.tensor_copy(w.ones_pair[:], v.ones_pair_f[:])
                nc.vector.tensor_copy(bias_high[:], v.expert_b_rows[:]).then_inc(bias_steps, 1)
                dve.wait_ge(bias_steps, 1)
                nc.vector.tensor_tensor(bias_low[:], v.expert_b_rows[:], bias_high[:].bitcast(F32), ALU.subtract)
                nc.vector.tensor_scalar(bias_top[:], bias_high[:].bitcast(F32), v.ident[0:2, 0:1], None, ALU.mult).then_inc(bias_steps, 1)
                dve.wait_ge(bias_steps, 2)
                nc.vector.scalar_tensor_tensor(w.bias_pair[:], bias_low[:], v.ident[0:2, 1:2], bias_top[:], ALU.mult, ALU.add)
                for r in range(2):
                    cols = slice(r * 512, (r + 1) * 512)
                    dve.wait_ge(high_done, r + 1)
                    nc.vector.tensor_tensor(w.e_l[:, cols], banks[r][:], w.e_h[:, cols].bitcast(F32), ALU.subtract)
                norms(nc, dve, v, v.stat6, work, w.rstd[:], w.shift[:], steps, powed, 0)

            @block.gpsimd
            def _(pool):
                power(nc, pool, v, work, w.rstd[:], steps, powed, 0)


def mixture1_main(nc, v, w, out):
    C = GT * P
    HALF = E // 2
    with ExitStack() as ctx:
        sem = lambda name: ctx.enter_context(nc.semaphore(name))
        sb = lambda name, shape, dt=F32: ctx.enter_context(nc.sbuf_tensor(name, shape, dt))
        pb = lambda name, shape: ctx.enter_context(nc.psum_tensor(name, shape, F32))
        hat = sb("d_hat", [P, GT, D])
        hat_t = sb("d_hat_t", [P, C])
        hat_h, hat_l = ([sb(f"d_hat_{n}{i}", [P, C], F32R) for i in range(2)] for n in "hl")
        logits, shifted, exps = sb("d_logits", [P, GT, E]), sb("d_shifted", [P, GT, E]), sb("d_exps", [P, GT, E])
        best, first, total = sb("d_best", [P, GT, 1]), sb("d_first", [P, GT, 1]), sb("d_total", [P, GT, 1])
        equal, ranked, chosen = sb("d_equal", [P, GT, E]), sb("d_ranked", [P, GT, E]), sb("d_chosen", [P, GT, E])
        weight = [sb(f"d_weight{i}", [P, GT, E]) for i in range(2)]
        scaled = [sb(f"d_scaled{i}", [P, HALF, D]) for i in range(2)]
        pairs, four = sb("d_pairs", [P, 2, D]), sb("d_four", [P, D])
        ps_lo, ps_hi = ([pb(f"d_ps_{n}{i}", [P, HALF, D]) for i in range(2)] for n in ("lo", "hi"))
        ps_x, ps_r = pb("d_ps_x", [P, 512]), pb("d_ps_r", [P, 512])
        hat_ready, turned, copied, high_done, low_done, routed, route = (
            sem(n) for n in ("hat_ready", "turned", "copied", "high_done", "low_done", "routed", "route"))
        shifted_ready, exps_ready, weight_ready = sem("shifted_ready"), sem("exps_ready"), sem("weight_ready")
        experts_done, added, scaled_done, pool_steps, tile_done, stored = (
            sem(n) for n in ("experts_done", "added", "scaled_done", "pool_steps", "tile_done", "stored"))
        ROUTE = 8

        with nc.Block() as block:

            def each_group(eng, step):
                for g in range(-2, 1):
                    step(g, g % 2)
                with eng.Fori(0, (NG - 4) // 2) as i:
                    step(2 * i + 1, 1)
                    step(2 * i + 2, 0)
                for g in range(NG - 3, NG):
                    step(g, g % 2)

            @block.sync
            def _(sp):
                rows = out.rearrange("(t c) s d -> (c s) t d", c=2)
                with sp.Fori(0, NG) as g:
                    sp.wait_ge(tile_done, GT * g + GT)
                    sp.dma_start(rows[:, bass.ds(GT * g, GT), :], v.xa[:, bass.ds(GT * g, GT), :]).then_inc(stored, 16)
                sp.wait_ge(stored, 16 * NG)

            @block.tensor
            def _(pe):
                def step(g, par):
                    for t in range(GT):
                        if there(g):
                            n = GT * g + t
                            pe.wait_ge(low_done, g + 1)
                            if there(g - 1):
                                pe.wait_ge(added, HALF * (n - 1))
                                pe.wait_ge(scaled_done, n - 1)
                            for half, bank in enumerate((ps_lo[t], ps_hi[t])):
                                cols = slice(half * 512, (half + 1) * 512)
                                flat = bank[:].rearrange("p e d -> p (e d)")
                                nc.tensor.matmul(flat, w.ones_pair[:], w.bias_pair[:, cols], start=True, stop=False)
                                last = split_products(nc, flat, (hat_h[par][:, t * P:(t + 1) * P], hat_l[par][:, t * P:(t + 1) * P]),
                                                      (w.e_h[:, cols], w.e_l[:, cols]), False, True)
                            last.then_inc(experts_done, 1)
                        if t == 1 and there(g + 1):
                            pe.wait_ge(copied, g + 2)
                            for s in range(GT):
                                last = nc.tensor.matmul(ps_r[:, s * E:(s + 1) * E], hat_t[:, s * P:(s + 1) * P], w.router[:], start=True, stop=True)
                            last.then_inc(routed, 1)
                        if t == 0 and there(g + 1):
                            pe.wait_ge(hat_ready, g + 2)
                            for s in range(GT):
                                last = nc.tensor.transpose(ps_x[:, s * P:(s + 1) * P], hat[:, s], v.ident[:])
                            last.then_inc(turned, 1)

                each_group(pe, step)

            @block.scalar
            def _(act):
                def step(g, par):
                    for t in range(GT):
                        if t == 0 and there(g + 1):
                            act.wait_ge(turned, g + 2)
                            if there(g):
                                act.wait_ge(routed, g + 1)
                                act.wait_ge(low_done, g + 1)
                            nc.scalar.activation(hat_t[:], ps_x[:, 0:C], ACT.Copy).then_inc(copied, 1)
                            act.wait_ge(copied, g + 2)
                            nc.scalar.activation(hat_h[1 - par][:], hat_t[:], ACT.Copy).then_inc(high_done, 1)
                        if there(g):
                            n = GT * g + t
                            act.wait_ge(experts_done, n + 1)
                            act.wait_ge(weight_ready, g + 1)
                            if there(g - 1):
                                act.wait_ge(pool_steps, 2 * (n - 2) + 1)
                            for e in range(HALF):
                                last = nc.scalar.activation(scaled[t][:, e], ps_hi[t][:, e], ACT.Copy, scale=weight[par][:, t, HALF + e:HALF + e + 1])
                            last.then_inc(scaled_done, 1)
                        if t == 1 and there(g + 1):
                            act.wait_ge(shifted_ready, g + 2)
                            nc.scalar.activation(exps[:], shifted[:], ACT.Exp).then_inc(exps_ready, 1)

                each_group(act, step)

            @block.vector
            def _(dve):
                def step(g, par):
                    for t in range(GT):
                        if t == 0 and there(g + 1):
                            dve.wait_ge(high_done, g + 2)
                            nc.vector.tensor_tensor(hat_l[1 - par][:], hat_t[:], hat_h[1 - par][:].bitcast(F32), ALU.subtract).then_inc(low_done, 1)
                        if there(g):
                            n = GT * g + t
                            for e in range(HALF):
                                if e == 0:
                                    dve.wait_ge(experts_done, n + 1)
                                    dve.wait_ge(weight_ready, g + 1)
                                else:
                                    dve.wait_ge(added, HALF * n + e)
                                before = v.xb[:, n, :] if e == 0 else v.xa[:, n, :]
                                nc.vector.scalar_tensor_tensor(v.xa[:, n, :], ps_lo[t][:, e], weight[par][:, t, e:e + 1], before, ALU.mult, ALU.add
                                                               ).then_inc(added, 1)
                        if t == 0 and there(g + 2):
                            if there(g + 1):
                                dve.wait_ge(turned, g + 2)
                            for s in range(GT):
                                at = GT * (g + 2) + s
                                last = nc.vector.tensor_scalar(hat[:, s], v.xb[:, at, :], w.rstd[:, bass.ds(at, 1)], w.shift[:, bass.ds(at, 1)],
                                                               ALU.mult, ALU.add)
                            last.then_inc(hat_ready, 1)
                        if t == 1 and there(g + 1):
                            choose(g + 1, 1 - par)

                def choose(g, par):
                    at = ROUTE * g
                    wide = [P, GT, E]
                    dve.wait_ge(routed, g + 1)
                    nc.vector.tensor_tensor(logits[:], ps_r[:, 0:GT * E].rearrange("p (t e) -> p t e", t=GT),
                                            v.router_b_row[:].unsqueeze(1).broadcast_to(wide), ALU.add).then_inc(route, 1)
                    dve.wait_ge(route, at + 1)
                    nc.vector.reduce_max(best[:, :, 0], logits[:], AX.X).then_inc(route, 1)
                    dve.wait_ge(route, at + 2)
                    nc.vector.tensor_tensor(shifted[:], logits[:], best[:].broadcast_to(wide), ALU.subtract).then_inc(shifted_ready, 1)
                    nc.vector.tensor_tensor(equal[:], logits[:], best[:].broadcast_to(wide), ALU.is_equal).then_inc(route, 1)
                    dve.wait_ge(route, at + 3)
                    nc.vector.tensor_tensor(ranked[:], equal[:], v.first_wins[:].unsqueeze(1).broadcast_to(wide), ALU.mult).then_inc(route, 1)
                    dve.wait_ge(route, at + 4)
                    nc.vector.reduce_max(first[:, :, 0], ranked[:], AX.X).then_inc(route, 1)
                    dve.wait_ge(route, at + 5)
                    nc.vector.tensor_tensor(chosen[:], ranked[:], first[:].broadcast_to(wide), ALU.is_equal).then_inc(route, 1)
                    dve.wait_ge(exps_ready, g + 1)
                    nc.vector.reduce_sum(total[:, :, 0], exps[:], AX.X).then_inc(route, 1)
                    dve.wait_ge(route, at + 7)
                    nc.vector.reciprocal(total[:], total[:]).then_inc(route, 1)
                    dve.wait_ge(route, at + 8)
                    nc.vector.tensor_scalar(total[:], total[:], v.tgate[:, 3:4], None, ALU.mult).then_inc(total_ready, 1)
                    dve.wait_ge(total_ready, g + 1)
                    nc.vector.tensor_tensor(weight[par][:], chosen[:], total[:].broadcast_to(wide), ALU.mult).then_inc(weight_ready, 1)

                total_ready = sem("total_ready")
                each_group(dve, step)

            @block.gpsimd
            def _(pool):
                def step(g, par):
                    for t in range(GT):
                        if there(g):
                            n = GT * g + t
                            pool.wait_ge(scaled_done, n + 1)
                            nc.gpsimd.tensor_tensor(pairs[:], scaled[t][:, 0:2], scaled[t][:, 2:4], ALU.add).then_inc(pool_steps, 1)
                            pool.wait_ge(pool_steps, 2 * n + 1)
                            nc.gpsimd.tensor_tensor(four[:], pairs[:, 0], pairs[:, 1], ALU.add).then_inc(pool_steps, 1)
                            pool.wait_ge(pool_steps, 2 * n + 2)
                            pool.wait_ge(added, HALF * (n + 1))
                            nc.gpsimd.tensor_tensor(v.xa[:, n, :], v.xa[:, n, :], four[:], ALU.add).then_inc(tile_done, 1)

                each_group(pool, step)


INPUTS = ["x", "ctx_1024", "mask_BxS2_bk0", "g_xattn", "g_ffn", "L0_xattn_Wq", "L0_xattn_bq", "L0_xattn_Wk", "L0_xattn_bk",
          "L0_xattn_Wv", "L0_xattn_bv", "L0_xattn_Wo", "L0_xattn_bo", "L0_ffn_norm_scale", "L0_ffn_w_router", "L0_ffn_w_up",
          "L0_ffn_w_down", "L1_xattn_g1", "L1_xattn_b1", "L1_xattn_g2", "L1_xattn_b2", "L1_xattn_Wq", "L1_xattn_Wkv",
          "L1_xattn_Wout", "L1_ffn_router_w", "L1_ffn_router_b", "L1_ffn_expert_w", "L1_ffn_expert_b"]


def build_program(nc, io, out):
    with ExitStack() as ctx:
        sem = lambda name: ctx.enter_context(nc.semaphore(name))
        sb = lambda name, shape, dt=F32: ctx.enter_context(nc.sbuf_tensor(name, shape, dt))
        v = Env()
        v.x_loaded, v.weights0_loaded, v.weights1_loaded = sem("x_loaded"), sem("weights0_loaded"), sem("weights1_loaded")
        v.weights2_loaded, v.weights3_loaded, v.gates_ready = sem("weights2_loaded"), sem("weights3_loaded"), sem("gates_ready")
        v.xa, v.xb, v.cx = sb("xa", [P, NT, D]), sb("xb", [P, NT, D]), sb("cx", [P, NT, D])
        v.stat6, v.norm_work = sb("stat6", [P, NT, 6]), sb("norm_work", [P, 8, GT])
        v.ident, v.minus_half = sb("ident", [P, P]), sb("minus_half", [P, NT])
        v.zeros = sb("zeros", [P, GT])
        v.ones_row, v.ones_pair_f = sb("ones_row", [1, P], BF16), sb("ones_pair_f", [2, P])
        v.first_wins = sb("first_wins", [P, E])
        v.head_in_four, v.four_rows, v.q_mask = sb("head_in_four", [P, 4]), sb("four_rows", [P, 4]), sb("q_mask", [P, 4])
        v.four_cols = sb("four_cols", [P, D])
        v.gate, v.tgate, v.half_gate = sb("gate", [P, 4]), sb("tgate", [P, 4]), sb("half_gate", [P, 1])
        v.wq1_raw, v.wkv1_raw, v.wout1_raw = sb("wq1_raw", [P, H * HD1]), sb("wkv1_raw", [P, 2 * H * HD1]), sb("wout1_raw", [P, H // 2, D])
        v.vec2, v.mask_u8 = sb("vec2", [P, 4]), sb("mask_u8", [1, BATCH * SEQ], mybir.dt.uint8)
        v.expert_raw, v.router1_raw = sb("expert_raw", [P, E, D]), sb("router1_raw", [E, D])
        v.router_b_row, v.expert_b_rows = sb("router_b_row", [P, E]), sb("expert_b_rows", [2, E * D])
        with ExitStack() as layer0:
            sb0 = lambda name, shape, dt=F32: layer0.enter_context(nc.sbuf_tensor(name, shape, dt))
            v.w_up_raw, v.w_down_raw = sb0("w_up_raw", [P, E * 4, D]), sb0("w_down_raw", [P, E, HID])
            v.router0_raw, v.vec1 = sb0("router0_raw", [E, D]), sb0("vec1", [P, 1])
            with ExitStack() as first:
                sb0 = lambda name, shape, dt=F32: first.enter_context(nc.sbuf_tensor(name, shape, dt))
                v.wq0, v.wk0, v.wv0, v.wo0 = (sb0(n, [P, D]) for n in ("wq0", "wk0", "wv0", "wo0"))
                v.wq0_h, v.wq0_l, v.wk0_h, v.wk0_l = (sb0(n, [P, D], F32R) for n in ("wq0_h", "wq0_l", "wk0_h", "wk0_l"))
                v.wo0_j, v.vec0, v.bk_four = sb0("wo0_j", [P, 4, D]), sb0("vec0", [P, 3]), sb0("bk_four", [P, 4])
                v.bo_row, v.gbo = sb0("bo_row", [P, D]), sb0("gbo", [P, D])
                setup(nc, v, io)
                attention0(nc, v)
            mixture0(nc, v)
        attention1(nc, v)
        mixture1(nc, v, out)


def kernel(**inputs):
    import numpy as _np
    import concourse.bacc as _bacc
    from concourse import mybir as _mybir
    from concourse.bass_utils import run_bass_kernel_spmd as _run

    nc = _bacc.Bacc("TRN2", target_bir_lowering=False, num_devices=1)
    arrays, io = {}, {}
    for name in INPUTS:
        a = _np.ascontiguousarray(_np.asarray(inputs[name]))
        arrays[f"in_{name}"] = a
        io[name] = nc.dram_tensor(f"in_{name}", a.shape, _mybir.dt.from_np(a.dtype), kind="ExternalInput").ap()
    out = nc.dram_tensor("out_tokens", (BATCH, SEQ, D), _mybir.dt.float32, kind="ExternalOutput").ap()
    build_program(nc, io, out)
    r = _run(nc, [arrays], core_ids=[0])
    return r.results[0]["out_tokens"]
```

```python
import concourse.bass as bass
from concourse import mybir
from contextlib import ExitStack

F32 = mybir.dt.float32
F32R = mybir.dt.float32r
BF16 = mybir.dt.bfloat16
ALU = mybir.AluOpType
ACT = mybir.ActivationFunctionType
AX = mybir.AxisListType

P = 128
BATCH, SEQ, D = 64, 64, 128
NT = BATCH * SEQ // P
GT = 2
NG = NT // GT
GB = GT * 2
H = 16
HD0 = D // H
CHUNK = 32
HD1 = 64
E = 8
HID = 256
FIRST_GROUPS = 4
LN_EPS = 1e-5
RMS_EPS = 1e-6
BIG = 1e30


class Env:
    pass


def there(g, n=NG):
    return not isinstance(g, int) or 0 <= g < n


def split_products(nc, out, lhs, rhs, start, stop):
    pairs = ((lhs[0], rhs[0]), (lhs[0], rhs[1]), (lhs[1], rhs[0]))
    for i, (a, b) in enumerate(pairs):
        last = nc.tensor.matmul(out, a, b, start=start and i == 0, stop=stop and i == 2)
    return last


def group_norm(nc, pool, v, stat6, rstd, shift, parts, done):
    w = v.norm_work
    twice_mean, diff, squares, diff2, rest, var4, half_rstd, product = (w[:, i] for i in range(8))
    nc.gpsimd.tensor_tensor(twice_mean, stat6[:, :, 1], stat6[:, :, 4], ALU.add)
    nc.gpsimd.tensor_tensor(diff, stat6[:, :, 1], stat6[:, :, 4], ALU.subtract)
    nc.gpsimd.tensor_tensor(squares, stat6[:, :, 2], stat6[:, :, 5], ALU.add).then_inc(parts, 1)
    pool.wait_ge(parts, done + 1)
    nc.gpsimd.tensor_tensor(diff2, diff, diff, ALU.mult)
    nc.gpsimd.tensor_scalar(rest, squares, 4.0 / D, 4 * LN_EPS, ALU.mult, ALU.add).then_inc(parts, 1)
    pool.wait_ge(parts, done + 2)
    nc.gpsimd.tensor_tensor(var4, diff2, rest, ALU.add).then_inc(parts, 1)
    pool.wait_ge(parts, done + 3)
    nc.gpsimd.tensor_tensor(half_rstd, var4, v.minus_half[:, 0:GT], ALU.pow).then_inc(parts, 1)
    pool.wait_ge(parts, done + 4)
    nc.gpsimd.tensor_tensor(product, twice_mean, half_rstd, ALU.mult)
    nc.gpsimd.tensor_scalar(rstd, half_rstd, 2.0, None, ALU.mult).then_inc(parts, 1)
    pool.wait_ge(parts, done + 5)
    return nc.gpsimd.tensor_tensor(shift, v.zeros[:, 0:GT], product, ALU.subtract)


NORM_STEPS, RMS_STEPS, TWICE_STEPS = 7, 9, 10


def norm_step(nc, pool, w, i, parts, done, stats, rstd, shift, second=None, rms=None, twice=None):
    twice_mean, diff, squares, rest, var4, var4_eps, half, product = (w.scratch[k] for k in range(8))
    square, mean_square, mean_square_eps, again = (w.scratch[8 + k][second] for k in range(4)) if second else (None,) * 4
    if i:
        pool.wait_ge(parts, done + i)
    if i == 0:
        nc.gpsimd.tensor_tensor(twice_mean, stats(1), stats(4), ALU.add)
        nc.gpsimd.tensor_tensor(diff, stats(1), stats(4), ALU.subtract)
        return nc.gpsimd.tensor_tensor(squares, stats(2), stats(5), ALU.add)
    if i == 1:
        nc.gpsimd.tensor_tensor(product, diff, diff, ALU.mult)
        return nc.gpsimd.tensor_scalar(rest, squares, 4.0 / D, None, ALU.mult)
    if i == 2:
        return nc.gpsimd.tensor_tensor(var4, product, rest, ALU.add)
    if i == 3:
        return nc.gpsimd.tensor_tensor(var4_eps, var4, w.four_eps, ALU.add)
    if i == 4:
        return nc.gpsimd.tensor_tensor(half, var4_eps, w.minus_half, ALU.pow)
    if i == 5:
        if second:
            nc.gpsimd.tensor_tensor(square, half[second], half[second], ALU.mult)
        nc.gpsimd.tensor_tensor(product, twice_mean, half, ALU.mult)
        return nc.gpsimd.tensor_tensor(rstd, half, half, ALU.add)
    if i == 6:
        if second:
            nc.gpsimd.tensor_tensor(mean_square, var4[second], square, ALU.mult)
        return nc.gpsimd.tensor_tensor(shift, w.zero, product, ALU.subtract)
    if i == 7:
        return nc.gpsimd.tensor_tensor(mean_square_eps, mean_square, w.second_eps[second], ALU.add)
    if i == 8:
        return nc.gpsimd.tensor_tensor(again if rms is None else rms, mean_square_eps, w.minus_half[second], ALU.pow)
    if i == 9:
        for scaled in twice:
            last = nc.gpsimd.tensor_tensor(scaled, scaled, again, ALU.mult)
        return last


def norm_constants(nc, w, tile, second_eps):
    w.scratch = [tile[:, k] for k in range(12)]
    w.four_eps, w.minus_half, w.zero, w.second_eps = (tile[:, k] for k in range(12, 16))
    for const, value in ((w.four_eps, 4 * LN_EPS), (w.minus_half, -0.5), (w.zero, 0.0), (w.second_eps, second_eps)):
        last = nc.gpsimd.memset(const, value)
    return last


def setup(nc, v, io):
    with ExitStack() as ctx:
        sem = lambda name: ctx.enter_context(nc.semaphore(name))
        sb = lambda name, shape, dt=F32: ctx.enter_context(nc.sbuf_tensor(name, shape, dt))
        consts_zeroed, consts_built = sem("consts_zeroed"), sem("consts_built")
        head_sums = sem("head_sums")
        head_rows = sb("head_rows", [P, 4, 4])
        with nc.Block() as block:

            @block.sync
            def _(sp):
                first = slice(0, FIRST_GROUPS * GT)
                for tile, tokens in ((v.xa, io["x"]), (v.cx, io["ctx_1024"])):
                    sp.dma_start(tile[:, first], tokens.rearrange("(t c) s d -> (c s) t d", c=2)[:, first]).then_inc(v.first_loaded, 16)

            @block.scalar
            def _(act):
                for name, tile in (("L0_xattn_Wq", v.wq0), ("L0_xattn_Wk", v.wk0), ("L0_xattn_Wv", v.wv0), ("L0_xattn_Wo", v.wo0)):
                    act.dma_start(tile[:], io[name]).then_inc(v.weights0_loaded, 16)
                for name, col in (("L0_xattn_bq", 0), ("L0_xattn_bk", 1), ("L0_xattn_bv", 2)):
                    act.dma_start(v.vec0[:, col:col + 1], io[name].rearrange("(d a) -> d a", a=1)).then_inc(v.weights0_loaded, 16)
                act.dma_start(v.bo_row[:], io["L0_xattn_bo"].rearrange("(a d) -> a d", a=1).broadcast_to([P, D])).then_inc(v.weights0_loaded, 16)
                for name, col in (("g_xattn", 0), ("g_ffn", 2)):
                    act.dma_start(v.gate[:, col:col + 2], io[name].rearrange("(a d) -> a d", a=1).broadcast_to([P, 2])).then_inc(v.weights0_loaded, 16)
                act.wait_ge(v.weights0_loaded, 160)
                nc.scalar.activation(v.tgate[:], v.gate[:], ACT.Tanh).then_inc(v.gates_ready, 1)

            @block.gpsimd
            def _(pool):
                nc.gpsimd.memset(v.ident[:], 0.0).then_inc(consts_zeroed, 1)
                nc.gpsimd.memset(head_rows[:], 1.0).then_inc(consts_zeroed, 1)
                nc.gpsimd.memset(v.minus_half[:], -0.5)
                nc.gpsimd.memset(v.zeros[:], 0.0)
                nc.gpsimd.memset(v.ones_row[:], 1.0)
                nc.gpsimd.memset(v.ones_pair_f[:], 1.0).then_inc(consts_zeroed, 1)
                for e in range(E):
                    last = nc.gpsimd.memset(v.first_wins[:, e:e + 1], float(E - e))
                last.then_inc(consts_zeroed, 1)
                pool.wait_ge(consts_zeroed, 4)
                nc.gpsimd.affine_select(out=v.ident[:], in_=v.ident[:], compare_op=ALU.not_equal, fill=1.0, base=0,
                                        pattern=[[-1, P]], channel_multiplier=1).then_inc(consts_built, 1)
                nc.gpsimd.affine_select(out=head_rows[:], in_=head_rows[:], compare_op=ALU.is_ge, fill=0.0, base=0,
                                        pattern=[[-4 * HD0, 4], [-HD0, 4]], channel_multiplier=1).then_inc(consts_built, 1)
                pool.wait_ge(consts_built, 2)
                nc.gpsimd.affine_select(out=head_rows[:], in_=head_rows[:], compare_op=ALU.is_ge, fill=0.0, base=HD0 - 1,
                                        pattern=[[4 * HD0, 4], [HD0, 4]], channel_multiplier=-1).then_inc(consts_built, 1)

            @block.vector
            def _(dve):
                dve.wait_ge(consts_built, 3)
                nc.vector.reduce_sum(v.head_in_four[:], head_rows[:].rearrange("p a j -> p j a"), AX.X).then_inc(head_sums, 1)
                nc.vector.reduce_sum(v.four_rows[:], head_rows[:], AX.X).then_inc(head_sums, 1)
                dve.wait_ge(head_sums, 2)
                nc.vector.tensor_scalar(v.q_mask[:], v.head_in_four[:], float(HD0) ** -0.5, None, ALU.mult).then_inc(head_sums, 1)
                nc.vector.tensor_copy(v.four_cols[:].rearrange("p (a c) -> p a c", a=4),
                                      v.four_rows[:].unsqueeze(2).broadcast_to([P, 4, 32])).then_inc(head_sums, 1)
                dve.wait_ge(v.weights0_loaded, 160)
                dve.wait_ge(v.gates_ready, 1)
                nc.vector.tensor_copy(v.wq0_h[:], v.wq0[:]).then_inc(head_sums, 1)
                nc.vector.tensor_copy(v.wk0_h[:], v.wk0[:]).then_inc(head_sums, 1)
                nc.vector.tensor_scalar(v.gbo[:], v.bo_row[:], v.tgate[:, 0:1], None, ALU.mult)
                for j in range(4):
                    nc.vector.tensor_scalar(v.wo0_j[:, j, :], v.wo0[:], v.head_in_four[:, j:j + 1], None, ALU.mult)
                nc.vector.tensor_scalar(v.bk_four[:], v.four_rows[:], v.vec0[:, 1:2], None, ALU.mult)
                nc.vector.tensor_scalar(v.half_gate[:], v.tgate[:, 2:3], 0.5, None, ALU.mult)
                dve.wait_ge(head_sums, 6)
                nc.vector.tensor_tensor(v.wq0_l[:], v.wq0[:], v.wq0_h[:].bitcast(F32), ALU.subtract)
                nc.vector.tensor_tensor(v.wk0_l[:], v.wk0[:], v.wk0_h[:].bitcast(F32), ALU.subtract)


def attention0(nc, v, io):
    with ExitStack() as ctx:
        sem = lambda name: ctx.enter_context(nc.semaphore(name))
        sb = lambda name, shape, dt=F32: ctx.enter_context(nc.sbuf_tensor(name, shape, dt))
        pb = lambda name, shape: ctx.enter_context(nc.psum_tensor(name, shape, F32))

        stat6 = sb("a_stat6", [P, GT, 6])
        rstd = sb("a_rstd", [P, GT])
        shift = sb("a_shift", [P, GT])
        x_hat = sb("a_x_hat", [P, GT, D])
        ctx_tile = sb("a_ctx_tile", [P, GT, D])
        xc = sb("a_xc", [P, 2, GT * P])
        xc_h = sb("a_xc_h", [P, 2, GT * P], F32R)
        xc_l = sb("a_xc_l", [P, 2, GT * P], F32R)
        ctx_rep = sb("a_ctx_rep", [P, 2 * GB, 4, CHUNK])
        q_flat = sb("a_q_flat", [P, 2 * GB, CHUNK])
        q_exp = [sb(f"a_q_exp{i}", [P, 2 * GB, 4, CHUNK]) for i in range(2)]
        k_exp = [sb(f"a_k_exp{i}", [P, 2 * GB, 4, CHUNK]) for i in range(2)]
        v_exp = [sb(f"a_v_exp{i}", [P, 2 * GB, D]) for i in range(2)]
        row_max = sb("a_row_max", [P, 2, 3, 4])
        row_max3 = sb("a_row_max3", [P, 2, 3, 4])
        shifted = sb("a_shifted", [P, 2, 384])
        probs = [sb(f"a_probs{i}", [P, 2, 384]) for i in range(2)]
        sums = sb("a_sums", [P, 2, 3, 4])
        sums_high = sb("a_sums_high", [P, 2, 4])
        recip = [sb(f"a_recip{i}", [P, 2, 3, 4]) for i in range(2)]
        normed = sb("a_normed", [P, 2, 384])
        probs_t = sb("a_probs_t", [P, 2, 384])
        heads_t = sb("a_heads_t", [P, 4, 4, CHUNK])

        ps_s = pb("a_ps_s", [P, 2, 512])
        ps_t = pb("a_ps_t", [P, 2, 512])
        ps_aux = pb("a_ps_aux", [P, 512])
        ps_qk = pb("a_ps_qk", [P, 512])
        ps_o = pb("a_ps_o", [P, 512])
        ps_y = pb("a_ps_y", [P, 512])

        stats_ready, rstd_ready, rstd_parts = sem("stats_ready"), sem("rstd_ready"), sem("rstd_parts")
        ctx_repeated = sem("ctx_repeated")
        xhat_ready, ctx_staged = sem("xhat_ready"), sem("ctx_staged")
        inputs_turned, xc_copied, xc_high, xc_low = sem("inputs_turned"), sem("xc_copied"), sem("xc_high"), sem("xc_low")
        qk_done, q_copied, k_ready, q_ready = sem("qk_done"), sem("q_copied"), sem("k_ready"), sem("q_ready")
        v_done, v_ready = sem("v_done"), sem("v_ready")
        scores_done, scores_maxed, max_spread, shifted_ready = sem("scores_done"), sem("scores_maxed"), sem("max_spread"), sem("shifted_ready")
        exp_done, sums_done, sums_added, recip_ready, normed_ready = sem("exp_done"), sem("sums_done"), sem("sums_added"), sem("recip_ready"), sem("normed_ready")
        probs_turned, probs_t_ready = sem("probs_turned"), sem("probs_t_ready")
        heads_done, heads_ready, projected, x1_ready = sem("heads_done"), sem("heads_ready"), sem("projected"), sem("x1_ready")
        base_ready = sem("base_ready")

        with nc.Block() as block:

            @block.sync
            def _(sp):
                rest = slice(FIRST_GROUPS * GT, NT)
                for tile, tokens in ((v.xa, io["x"]), (v.cx, io["ctx_1024"])):
                    sp.dma_start(tile[:, rest], tokens.rearrange("(t c) s d -> (c s) t d", c=2)[:, rest]).then_inc(v.x_loaded, 16)
                sp.dma_start(v.w_up_raw[:], io["L0_ffn_w_up"].rearrange("e (c p) d -> p (e c) d", p=P)).then_inc(v.weights1_loaded, 16)
                sp.dma_start(v.w_down_raw[:], io["L0_ffn_w_down"].rearrange("e o f -> o e f")).then_inc(v.weights1_loaded, 16)
                sp.dma_start(v.router0_raw[:], io["L0_ffn_w_router"]).then_inc(v.weights1_loaded, 16)
                sp.dma_start(v.vec1[:, 0:1], io["L0_ffn_norm_scale"].rearrange("(d a) -> d a", a=1)).then_inc(v.weights1_loaded, 16)
                sp.dma_start(v.wq1_raw[:], io["L1_xattn_Wq"]).then_inc(v.weights2_loaded, 16)
                sp.dma_start(v.wkv1_raw[:], io["L1_xattn_Wkv"]).then_inc(v.weights2_loaded, 16)
                sp.dma_start(v.wout1_raw[:], io["L1_xattn_Wout"].rearrange("(c p) d -> p c d", p=P)).then_inc(v.weights2_loaded, 16)
                for col, name in enumerate(("L1_xattn_g1", "L1_xattn_b1", "L1_xattn_g2", "L1_xattn_b2")):
                    sp.dma_start(v.vec2[:, col:col + 1], io[name].rearrange("(d a) -> d a", a=1)).then_inc(v.weights2_loaded, 16)
                sp.dma_start(v.mask_u8[:], io["mask_BxS2_bk0"].rearrange("(a b) s -> a (b s)", a=1)).then_inc(v.weights2_loaded, 16)
                sp.dma_start(v.expert_raw[:], io["L1_ffn_expert_w"].rearrange("e o d -> o e d")).then_inc(v.weights3_loaded, 16)
                sp.dma_start(v.router1_raw[:], io["L1_ffn_router_w"]).then_inc(v.weights3_loaded, 16)
                sp.dma_start(v.router_b_row[:], io["L1_ffn_router_b"].rearrange("(a e) -> a e", a=1).broadcast_to([P, E])).then_inc(v.weights3_loaded, 16)
                sp.dma_start(v.expert_b_rows[:], io["L1_ffn_expert_b"].rearrange("(a e) d -> a (e d)", a=1).broadcast_to([2, E * D])).then_inc(v.weights3_loaded, 16)

            def each_group(eng, step):
                for g in range(-3, FIRST_GROUPS - 3):
                    step(g, g % 2)
                if eng is not nc.tensor:
                    eng.wait_ge(v.x_loaded, 32)
                with eng.Fori(0, (NG - 4) // 2) as i:
                    step(2 * i + 1, 1)
                    step(2 * i + 2, 0)
                for g in range(NG - 3, NG + 1):
                    step(g, g % 2)

            @block.tensor
            def _(pe):
                def values(g, par, half, bank):
                    pe.wait_ge(ctx_repeated, g + 1)
                    pe.wait_ge(k_ready, g + 1)
                    for i in range(4):
                        c = 4 * half + i
                        last = nc.tensor.matmul(bank[:, i * P:(i + 1) * P], ctx_rep[:, c], v.wv0[:], start=True, stop=True)
                    last.then_inc(v_done, 1)

                def scores(g, par, k):
                    pe.wait_ge(q_ready, g + 1)
                    pe.wait_ge(k_ready, g + 1)
                    if there(g - 1) or k:
                        pe.wait_ge(shifted_ready, 2 * g + k)
                    for b in range(2):
                        c = 2 * (2 * k + b)
                        nc.tensor.matmul(ps_s[:, b, 0:128], q_exp[par][:, c], k_exp[par][:, c], start=True, stop=True)
                        last = nc.tensor.matmul(ps_s[:, b, 128:384], q_exp[par][:, c + 1], k_exp[par][:, c:c + 2], start=True, stop=True)
                    last.then_inc(scores_done, 1)

                def turn_probs(g, k):
                    pe.wait_ge(normed_ready, 2 * g + k + 1)
                    if there(g - 1) or k:
                        pe.wait_ge(probs_t_ready, 2 * g + k)
                    for b in range(2):
                        for n in range(3):
                            cols = slice(n * 128, (n + 1) * 128)
                            last = nc.tensor.transpose(ps_t[:, b, cols], normed[:, b, cols], v.ident[:])
                    last.then_inc(probs_turned, 1)

                def heads(g, par, k):
                    pe.wait_ge(probs_t_ready, 2 * g + k + 1)
                    pe.wait_ge(v_ready, 2 * g + 2)
                    if there(g - 1) or k:
                        pe.wait_ge(heads_ready, 2 * g + k)
                    for b in range(2):
                        c = 2 * (2 * k + b)
                        nc.tensor.matmul(ps_o[:, b * 256:b * 256 + 256], v_exp[par][:, c], probs_t[:, b, 0:256], start=True, stop=False)
                        last = nc.tensor.matmul(ps_o[:, b * 256 + 128:b * 256 + 256], v_exp[par][:, c + 1], probs_t[:, b, 256:384],
                                                start=False, stop=True)
                    last.then_inc(heads_done, 1)

                def project(g, k):
                    pe.wait_ge(heads_ready, 2 * g + k + 1)
                    if there(g - 1) or k:
                        pe.wait_ge(x1_ready, 2 * g + k)
                    for j in range(4):
                        last = nc.tensor.matmul(ps_y[:, 0:D], heads_t[:, j],
                                                v.wo0_j[:, j], start=j == 0, stop=j == 3)
                    last.then_inc(projected, 1)

                def step(g, par):
                    for k in range(2):
                        if there(g):
                            turn_probs(g, k)
                        if k == 0 and there(g + 1):
                            values(g + 1, 1 - par, 0, ps_qk)
                            values(g + 1, 1 - par, 1, ps_aux)
                        if k == 1 and there(g + 2):
                            pe.wait_ge(xc_low, g + 3)
                            pe.wait_ge(xc_high, g + 3)
                            if there(g + 1):
                                pe.wait_ge(v_ready, 2 * (g + 1) + 1)
                            x_pair, c_pair = ((xc_h[:, n], xc_l[:, n]) for n in range(2))
                            split_products(nc, ps_qk[:, 0:256], (v.wq0_h[:], v.wq0_l[:]), x_pair, True, True)
                            split_products(nc, ps_qk[:, 256:512], (v.wk0_h[:], v.wk0_l[:]), c_pair, True, True).then_inc(qk_done, 1)
                        if there(g + 1):
                            scores(g + 1, 1 - par, k)
                        if k == 0 and there(g + 2):
                            pe.wait_ge(xhat_ready, g + 3)
                            pe.wait_ge(ctx_staged, g + 3)
                            if there(g + 1):
                                pe.wait_ge(v_ready, 2 * (g + 1) + 2)
                            for t in range(GT):
                                nc.tensor.transpose(ps_aux[:, t * P:(t + 1) * P], x_hat[:, t], v.ident[:])
                            for t in range(GT):
                                last = nc.tensor.transpose(ps_aux[:, (GT + t) * P:(GT + t + 1) * P], ctx_tile[:, t], v.ident[:])
                            last.then_inc(inputs_turned, 1)
                        if k == 0 and there(g - 1):
                            project(g - 1, 1)
                        if k == 1 and there(g):
                            project(g, 0)
                        if there(g):
                            heads(g, par, k)

                pe.wait_ge(v.weights0_loaded, 160)
                each_group(pe, step)

            @block.scalar
            def _(act):
                def step(g, par):
                    for k in range(2):
                        if there(g):
                            act.wait_ge(probs_turned, 2 * g + k + 1)
                            if there(g - 1) or k:
                                act.wait_ge(heads_done, 2 * g + k)
                            nc.scalar.activation(probs_t[:], ps_t[:, :, 0:384], ACT.Copy).then_inc(probs_t_ready, 1)
                        if k == 1 and there(g + 2):
                            act.wait_ge(qk_done, g + 3)
                            if there(g + 1):
                                act.wait_ge(q_ready, g + 2)
                            nc.scalar.activation(q_flat[:], ps_qk[:, 0:256].rearrange("p (c q) -> p c q", q=CHUNK), ACT.Identity,
                                                 bias=v.vec0[:, 0:1]).then_inc(q_copied, 1)
                            if there(g):
                                act.wait_ge(scores_done, 2 * g + 2)
                            for a in range(4):
                                last = nc.scalar.activation(k_exp[par][:, :, a], ps_qk[:, 256:512].rearrange("p (c q) -> p c q", q=CHUNK),
                                                            ACT.Identity, bias=v.bk_four[:, a:a + 1], scale=v.four_rows[:, a:a + 1])
                            last.then_inc(k_ready, 1)
                        if k == 0 and there(g + 2):
                            act.wait_ge(inputs_turned, g + 3)
                            if there(g + 1):
                                act.wait_ge(xc_low, g + 2)
                            nc.scalar.activation(xc[:], ps_aux[:].rearrange("p (n t) -> p n t", n=2), ACT.Copy).then_inc(xc_copied, 1)
                            act.wait_ge(xc_copied, g + 3)
                            if there(g + 1):
                                act.wait_ge(qk_done, g + 2)
                            nc.scalar.activation(xc_h[:], xc[:], ACT.Copy).then_inc(xc_high, 1)
                            if there(g + 1):
                                act.wait_ge(v_done, 2 * (g + 1) + 2)
                            nc.scalar.activation(ctx_rep[:], xc[:, 1].rearrange("p (c k) -> p c k", k=CHUNK).unsqueeze(2)
                                                 .broadcast_to([P, 2 * GB, 4, CHUNK]), ACT.Copy).then_inc(ctx_repeated, 1)
                        if there(g + 1):
                            act.wait_ge(shifted_ready, 2 * (g + 1) + k + 1)
                            if there(g):
                                act.wait_ge(normed_ready, 2 * g + k + 1)
                            nc.scalar.activation(probs[k][:], shifted[:], ACT.Exp).then_inc(exp_done, 1)
                        if there(g):
                            act.wait_ge(heads_done, 2 * g + k + 1)
                            if there(g - 1) or k:
                                act.wait_ge(projected, 2 * g + k)
                            nc.scalar.activation(heads_t[:].rearrange("p j c q -> p c j q"), ps_o[:].rearrange("p (c j q) -> p c j q", c=4, j=4), ACT.Identity,
                                                 bias=v.vec0[:, 2:3]).then_inc(heads_ready, 1)
                        if k == 1 and there(g + 3):
                            if there(g + 2):
                                act.wait_ge(inputs_turned, g + 3)
                            nc.scalar.activation(ctx_tile[:], v.cx[:, bass.ds(GT * (g + 3), GT), :], ACT.Copy).then_inc(ctx_staged, 1)

                act.wait_ge(v.first_loaded, 32)
                each_group(act, step)

            @block.vector
            def _(dve):
                def step(g, par):
                    for k in range(2):
                        n = 2 * g + k + 1
                        if there(g) and k == 0 or there(g + 1) and k == 1:
                            kk = (k + 1) % 2
                            dve.wait_ge(exp_done, n + 1)
                            if k == 1 and there(g + 2):
                                dve.wait_ge(rstd_ready, g + 3)
                            nc.vector.reduce_sum(sums[:].rearrange("p b c a -> p b (c a)"),
                                                 probs[kk][:].rearrange("p b (c q) -> p b c q", q=CHUNK), AX.X).then_inc(sums_done, 1)
                            dve.wait_ge(sums_done, n + 1)
                            nc.vector.tensor_tensor(sums_high[:], sums[:, :, 1], sums[:, :, 2], ALU.add).then_inc(sums_added, 1)
                            nc.vector.reciprocal(recip[kk][:, :, 0], sums[:, :, 0])
                            dve.wait_ge(sums_added, n + 1)
                            nc.vector.reciprocal(recip[kk][:, :, 1:3], sums_high[:].unsqueeze(2).broadcast_to([P, 2, 2, 4])).then_inc(recip_ready, 1)
                        if k == 1 and there(g + 3):
                            for t in range(GT):
                                last = nc.vector.bn_stats(stat6[:, t], v.xa[:, GT * (g + 3) + t, :])
                            last.then_inc(stats_ready, 1)
                        if k == 0 and there(g + 1):
                            for half, bank in enumerate((ps_qk, ps_aux)):
                                dve.wait_ge(v_done, 2 * (g + 1) + half + 1)
                                if half == 0 and there(g - 1):
                                    dve.wait_ge(heads_done, 2 * (g - 1) + 2)
                                nc.vector.tensor_tensor(v_exp[1 - par][:, 4 * half:4 * half + 4], bank[:].rearrange("p (c d) -> p c d", c=4),
                                                        v.four_cols[:].unsqueeze(1).broadcast_to([P, 4, D]), ALU.mult).then_inc(v_ready, 1)
                        if k == 0 and there(g + 2):
                            dve.wait_ge(rstd_ready, g + 3)
                            if there(g + 1):
                                dve.wait_ge(inputs_turned, g + 2)
                            for t in range(GT):
                                last = nc.vector.tensor_scalar(x_hat[:, t], v.xa[:, GT * (g + 2) + t, :], rstd[:, t:t + 1], shift[:, t:t + 1],
                                                               ALU.mult, ALU.add)
                            last.then_inc(xhat_ready, 1)
                        if there(g + 1):
                            m = 2 * (g + 1) + k
                            dve.wait_ge(scores_done, m + 1)
                            nc.vector.reduce_max(row_max[:].rearrange("p b c a -> p b (c a)"),
                                                 ps_s[:, :, 0:384].rearrange("p b (c q) -> p b c q", q=CHUNK), AX.X).then_inc(scores_maxed, 1)
                            dve.wait_ge(scores_maxed, m + 1)
                            nc.vector.tensor_tensor(row_max3[:, :, 1:3], row_max[:, :, 1].unsqueeze(2).broadcast_to([P, 2, 2, 4]),
                                                    row_max[:, :, 2].unsqueeze(2).broadcast_to([P, 2, 2, 4]), ALU.max)
                            nc.vector.tensor_copy(row_max3[:, :, 0], row_max[:, :, 0]).then_inc(max_spread, 1)
                            dve.wait_ge(max_spread, m + 1)
                            if there(g) or k:
                                dve.wait_ge(exp_done, m)
                            nc.vector.tensor_tensor(shifted[:].rearrange("p b (c q) -> p b c q", q=CHUNK),
                                                    ps_s[:, :, 0:384].rearrange("p b (c q) -> p b c q", q=CHUNK),
                                                    row_max3[:].rearrange("p b c a -> p b (c a)").unsqueeze(3).broadcast_to([P, 2, 12, CHUNK]),
                                                    ALU.subtract).then_inc(shifted_ready, 1)
                        if k == 0 and there(g + 2):
                            dve.wait_ge(xc_high, g + 3)
                            nc.vector.tensor_tensor(xc_l[:], xc[:], xc_h[:].bitcast(F32), ALU.subtract).then_inc(xc_low, 1)
                        if k == 0 and there(g - 1):
                            residual(g - 1, 1)
                        if k == 1 and there(g):
                            residual(g, 0)
                            for t in range(GT):
                                nc.vector.bn_stats(v.ctx_stat6[:, GT * g + t, :], v.cx[:, GT * g + t, :])

                def residual(g, k):
                    n = 2 * g + k
                    dve.wait_ge(projected, n + 1)
                    dve.wait_ge(base_ready, g + 1)
                    if there(g - 1) or k:
                        dve.wait_ge(x1_ready, n)
                    nc.vector.scalar_tensor_tensor(v.xb[:, n, :], ps_y[:, 0:D], v.tgate[:, 0:1], v.xb[:, n, :], ALU.mult, ALU.add).then_inc(x1_ready, 1)
                    if there(g - 1) or k:
                        nc.vector.bn_stats(v.stat6[:, n - 1, :], v.xb[:, n - 1, :])

                dve.wait_ge(v.first_loaded, 32)
                each_group(dve, step)
                dve.wait_ge(x1_ready, NT)
                nc.vector.bn_stats(v.stat6[:, NT - 1, :], v.xb[:, NT - 1, :])

            @block.gpsimd
            def _(pool):
                def step(g, par):
                    for k in range(2):
                        n = 2 * g + k + 1
                        if there(g) and k == 0 or there(g + 1) and k == 1:
                            kk = (k + 1) % 2
                            pool.wait_ge(recip_ready, n + 1)
                            if there(g):
                                pool.wait_ge(probs_turned, n)
                            nc.gpsimd.tensor_tensor(normed[:].rearrange("p b (c q) -> p (b c) q", q=CHUNK),
                                                    probs[kk][:].rearrange("p b (c q) -> p (b c) q", q=CHUNK),
                                                    recip[kk][:].rearrange("p b c a -> p (b c a)").unsqueeze(2).broadcast_to([P, 24, CHUNK]),
                                                    ALU.mult).then_inc(normed_ready, 1)
                        if k == 1 and there(g + 2):
                            pool.wait_ge(q_copied, g + 3)
                            if there(g):
                                pool.wait_ge(scores_done, 2 * g + 2)
                            nc.gpsimd.tensor_tensor(q_exp[par][:], q_flat[:].unsqueeze(2).broadcast_to([P, 2 * GB, 4, CHUNK]),
                                                    v.q_mask[:].unsqueeze(1).unsqueeze(3).broadcast_to([P, 2 * GB, 4, CHUNK]), ALU.mult
                                                    ).then_inc(q_ready, 1)
                        if k == 1 and there(g + 3):
                            pool.wait_ge(stats_ready, g + 4)
                            if there(g + 2):
                                pool.wait_ge(xhat_ready, g + 3)
                            group_norm(nc, pool, v, stat6, rstd[:], shift[:], rstd_parts, 5 * (g + 3)).then_inc(rstd_ready, 1)
                        if k == 0 and there(g):
                            nc.gpsimd.tensor_tensor(v.xb[:, bass.ds(GT * g, GT), :], v.xa[:, bass.ds(GT * g, GT), :],
                                                    v.gbo[:].unsqueeze(1).broadcast_to([P, GT, D]), ALU.add).then_inc(base_ready, 1)

                pool.wait_ge(v.first_loaded, 32)
                each_group(pool, step)


def mixture0(nc, v):
    with ExitStack() as ctx:
        sb = lambda name, shape, dt=F32: ctx.enter_context(nc.sbuf_tensor(name, shape, dt))
        up_h, up_l = sb("b_up_h", [P, E, 2 * HID], F32R), sb("b_up_l", [P, E, 2 * HID], F32R)
        down_w, router_w = sb("b_down_w", [P, E, 2, D]), sb("b_router_w", [P, E])
        w = Env()
        w.rstd, w.shift, w.rms = sb("b_rstd", [P, NT]), sb("b_shift", [P, NT]), sb("b_rms", [P, NT])
        w.normed, w.norm_parts = ctx.enter_context(nc.semaphore("normed")), ctx.enter_context(nc.semaphore("norm_parts"))
        w.scratch_tile = sb("b_norm_scratch", [P, 16, GT])

        def norm_part(pool, c, i):
            tiles = slice(GT * c, GT * (c + 1)) if isinstance(c, int) else bass.ds(GT * c, GT)
            last = norm_step(nc, pool, w, i, w.norm_parts, (RMS_STEPS - 1) * c, lambda k: v.stat6[:, tiles, k], w.rstd[:, tiles], w.shift[:, tiles],
                             second=(slice(None),), rms=w.rms[:, tiles])
            last.then_inc(w.normed if i == RMS_STEPS - 1 else w.norm_parts, 1)

        w.norm_part = norm_part
        mixture0_weights(nc, v, w, up_h, up_l, down_w, router_w)
        mixture0_main(nc, v, w, up_h, up_l, down_w, router_w)


def mixture0_weights(nc, v, w, up_h, up_l, down_w, router_w):
    with ExitStack() as ctx:
        sem = lambda name: ctx.enter_context(nc.semaphore(name))
        banks = [ctx.enter_context(nc.psum_tensor(f"bw_ps{i}", [P, 512], F32)) for i in range(4)]
        turned, high_done, bank_free = sem("turned"), sem("high_done"), sem("bank_free")
        UP, DOWN = E, E // 2
        zeroed = sem("norm_constants")
        with nc.Block() as block:

            @block.tensor
            def _(pe):
                pe.wait_ge(v.weights1_loaded, 64)
                for r in range(UP + DOWN + 1):
                    if r >= 4:
                        pe.wait_ge(bank_free, r - 3)
                    bank = banks[r % 4]
                    if r < UP:
                        parts = [v.w_up_raw[:, 4 * r + i] for i in range(4)]
                    elif r < UP + DOWN:
                        parts = [v.w_down_raw[:, 2 * (r - UP) + i // 2, (i % 2) * P:(i % 2 + 1) * P] for i in range(4)]
                    else:
                        nc.tensor.transpose(bank[:, 0:E], v.router0_raw[:], v.ident[0:E, 0:E]).then_inc(turned, 1)
                        break
                    for i, part in enumerate(parts):
                        last = nc.tensor.transpose(bank[:, i * P:(i + 1) * P], part, v.ident[:])
                    last.then_inc(turned, 1)

            @block.scalar
            def _(act):
                for r in range(UP + DOWN + 1):
                    act.wait_ge(turned, r + 1)
                    bank = banks[r % 4]
                    if r < UP:
                        nc.scalar.activation(up_h[:, r], bank[:], ACT.Copy).then_inc(high_done, 1)
                    elif r < UP + DOWN:
                        e = 2 * (r - UP)
                        nc.scalar.activation(down_w[:, e:e + 2], bank[:].rearrange("p (e c d) -> p e c d", e=2, c=2), ACT.Copy).then_inc(bank_free, 1)
                    else:
                        nc.scalar.activation(router_w[:], bank[:, 0:E], ACT.Copy)
                    if r == UP - 1:
                        act.wait_ge(bank_free, UP)

            @block.vector
            def _(dve):
                for r in range(UP):
                    dve.wait_ge(high_done, r + 1)
                    nc.vector.tensor_tensor(up_l[:, r], banks[r % 4][:], up_h[:, r].bitcast(F32), ALU.subtract).then_inc(bank_free, 1)

            @block.gpsimd
            def _(pool):
                norm_constants(nc, w, w.scratch_tile, RMS_EPS).then_inc(zeroed, 1)
                pool.wait_ge(zeroed, 1)
                for i in range(RMS_STEPS):
                    w.norm_part(pool, 0, i)


def mixture0_main(nc, v, w, up_h, up_l, down_w, router_w):
    C = GT * P
    with ExitStack() as ctx:
        sem = lambda name: ctx.enter_context(nc.semaphore(name))
        sb = lambda name, shape, dt=F32: ctx.enter_context(nc.sbuf_tensor(name, shape, dt))
        pb = lambda name, shape: ctx.enter_context(nc.psum_tensor(name, shape, F32))
        lat, normed = sb("b_lat", [P, GT, D]), sb("b_normed", [P, GT, D])
        xn = sb("b_xn", [P, C])
        xn_h, xn_l = sb("b_xn_h", [P, NG, C], F32R), sb("b_xn_l", [P, NG, C], F32R)
        weight = sb("b_weight", [P, NT, E])
        scores = sb("b_scores", [P, GT, E])
        best = [sb(f"b_best{i}", [P, GT, 1]) for i in range(2)]
        equal, ranked, chosen = sb("b_equal", [P, GT, E]), sb("b_ranked", [P, GT, E]), [sb(f"b_chosen{i}", [P, GT, E]) for i in range(2)]
        first = sb("b_first", [P, GT, 1])
        gap, ratio, one_plus = sb("b_gap", [P, GT, 1]), sb("b_ratio", [P, GT, 1]), sb("b_one_plus", [P, GT, 1])
        w_best = [sb(f"b_w_best{i}", [P, GT, 1]) for i in range(2)]
        parts = [sb(f"b_part{i}", [P, GT, E]) for i in range(2)]
        tanh_t = [sb(f"b_tanh{i}", [P, 2, C]) for i in range(2)]
        gated = [sb(f"b_gated{i}", [P, 2, C]) for i in range(2)]
        u_copy = [sb(f"b_u_copy{i}", [P, C]) for i in range(2)]
        hidden = [sb(f"b_hidden{i}", [P, 2, C]) for i in range(2)]
        ps_u = [pb(f"b_ps_u{i}", [P, 2, C]) for i in range(2)]
        ps_g = [pb(f"b_ps_g{i}", [P, 2, C]) for i in range(2)]
        ps_d = [pb(f"b_ps_d{i}", [P, 512]) for i in range(2)]
        ps_x, ps_r = pb("b_ps_x", [P, 512]), pb("b_ps_r", [P, 512])

        lat_ready, normed_ready, base_ready = sem("lat_ready"), sem("normed_ready"), sem("base_ready")
        x_turned, xn_ready, xn_high, xn_low = sem("x_turned"), sem("xn_ready"), sem("xn_high"), sem("xn_low")
        routed, routing, ratio_ready, weight_ready, weight_parts = sem("routed"), sem("routing"), sem("ratio_ready"), sem("weight_ready"), sem("weight_parts")
        gate_done, up_done, tanh_done, u_copied, gated_done = sem("gate_done"), sem("up_done"), sem("tanh_done"), sem("u_copied"), sem("gated_done")
        hidden0_done, hidden1_done, down_done, added = sem("hidden0_done"), sem("hidden1_done"), sem("down_done"), sem("added")
        ROUTE = 16

        with nc.Block() as block:

            def each_chunk(eng, step):
                for c in range(-2, 1):
                    step(c)
                with eng.Fori(1, NG - 2) as c:
                    step(c)
                for c in range(NG - 2, NG):
                    step(c)

            @block.tensor
            def _(pe):
                def up(c, e, bank, at):
                    pair = (xn_h[:, c, :], xn_l[:, c, :])
                    for f in range(2):
                        cols = slice(at + f * P, at + (f + 1) * P)
                        last = split_products(nc, bank[:, f], (up_h[:, e, cols], up_l[:, e, cols]), pair, True, True)
                    return last

                def gates(c, e):
                    n, par = E * c + e, e % 2
                    pe.wait_ge(xn_low, c + 1)
                    pe.wait_ge(xn_high, c + 1)
                    if there(c - 1) or e >= 2:
                        pe.wait_ge(gated_done, n - 1)
                    up(c, e, ps_g[par], HID).then_inc(gate_done, 1)

                def values(c, e):
                    n, par = E * c + e, e % 2
                    if there(c - 1) or e >= 2:
                        pe.wait_ge(hidden0_done, n - 1)
                    up(c, e, ps_u[par], 0).then_inc(up_done, 1)

                def down(c, e):
                    n, par = E * c + e, e % 2
                    pe.wait_ge(hidden0_done, n + 1)
                    pe.wait_ge(hidden1_done, n + 1)
                    if there(c - 1) or e >= 2:
                        pe.wait_ge(added, n - 1)
                    for t in range(GT):
                        for f in range(2):
                            last = nc.tensor.matmul(ps_d[par][:, t * P:(t + 1) * P], hidden[par][:, f, t * P:(t + 1) * P], down_w[:, e, f],
                                                    start=f == 0, stop=f == 1)
                    last.then_inc(down_done, 1)

                def step(c):
                    for e in range(E):
                        ahead = (c, e + 2) if e + 2 < E else (c + 1, e + 2 - E)
                        if there(ahead[0]):
                            gates(*ahead)
                        if there(c):
                            down(c, e)
                        if e == 0 and there(c + 1):
                            pe.wait_ge(normed_ready, c + 2)
                            for t in range(GT):
                                last = nc.tensor.transpose(ps_x[:, t * P:(t + 1) * P], normed[:, t], v.ident[:])
                            last.then_inc(x_turned, 1)
                        if e == 1 and there(c + 1):
                            pe.wait_ge(xn_ready, c + 2)
                            for t in range(GT):
                                last = nc.tensor.matmul(ps_r[:, t * E:(t + 1) * E], xn[:, t * P:(t + 1) * P], router_w[:], start=True, stop=True)
                            last.then_inc(routed, 1)
                        if there(ahead[0]):
                            values(*ahead)

                each_chunk(pe, step)

            @block.scalar
            def _(act):
                def unit(c, e, between):
                    n, par = E * c + e, e % 2
                    if there(c):
                        act.wait_ge(gate_done, n + 1)
                        if there(c - 1) or e >= 2:
                            act.wait_ge(gated_done, n - 1)
                        nc.scalar.activation(tanh_t[par][:], ps_g[par][:], ACT.Tanh, scale=0.5).then_inc(tanh_done, 1)
                    between()
                    if there(c):
                        if there(c - 1) or e >= 2:
                            act.wait_ge(hidden1_done, n - 1)
                        act.wait_ge(up_done, n + 1)
                        nc.scalar.activation(u_copy[par][:], ps_u[par][:, 1], ACT.Copy).then_inc(u_copied, 1)

                def prepare(c, e):
                    if e == 1 and there(c + 1):
                        act.wait_ge(x_turned, c + 2)
                        if there(c):
                            act.wait_ge(routed, c + 1)
                            act.wait_ge(xn_low, c + 1)
                        nc.scalar.activation(xn[:], ps_x[:, 0:C], ACT.Copy, scale=v.vec1[:, 0:1]).then_inc(xn_ready, 1)
                        act.wait_ge(xn_ready, c + 2)
                        nc.scalar.activation(xn_h[:, c + 1, :], xn[:], ACT.Copy).then_inc(xn_high, 1)
                    if e == 6 and there(c + 2):
                        act.wait_ge(w.normed, c + 3)
                        if there(c + 1):
                            act.wait_ge(base_ready, c + 2)
                        for t in range(GT):
                            n = GT * (c + 2) + t
                            last = nc.scalar.activation(lat[:, t], v.xb[:, n, :], ACT.Identity, scale=w.rstd[:, bass.ds(n, 1)], bias=w.shift[:, bass.ds(n, 1)])
                        last.then_inc(lat_ready, 1)
                    if e == 7 and there(c + 2):
                        act.wait_ge(lat_ready, c + 3)
                        if there(c + 1):
                            act.wait_ge(x_turned, c + 2)
                        for t in range(GT):
                            last = nc.scalar.activation(normed[:, t], lat[:, t], ACT.Copy, scale=w.rms[:, bass.ds(GT * (c + 2) + t, 1)])
                        last.then_inc(normed_ready, 1)

                def step(c):
                    for e in range(E):
                        unit(*((c, e + 1) if e + 1 < E else (c + 1, 0)), lambda: prepare(c, e))
                        if e == 5 and there(c + 1):
                            act.wait_ge(routing, ROUTE * (c + 1) + 9)
                            nc.scalar.activation(ratio[:], gap[:], ACT.Exp).then_inc(ratio_ready, 1)

                each_chunk(act, step)

            @block.vector
            def _(dve):
                def unit(c, e, between):
                    n, par = E * c + e, e % 2
                    if there(c):
                        dve.wait_ge(tanh_done, n + 1)
                        if there(c - 1) or e >= 2:
                            dve.wait_ge(hidden1_done, n - 1)
                        nc.vector.scalar_tensor_tensor(gated[par][:], tanh_t[par][:], 1.0, ps_g[par][:], ALU.add, ALU.mult).then_inc(gated_done, 1)
                    between()
                    if there(c):
                        dve.wait_ge(u_copied, n + 1)
                        dve.wait_ge(gated_done, n + 1)
                        if there(c - 1) or e >= 2:
                            dve.wait_ge(down_done, n - 1)
                        nc.vector.tensor_tensor(hidden[par][:, 0], gated[par][:, 0], ps_u[par][:, 0], ALU.mult).then_inc(hidden0_done, 1)

                def add(c, e):
                    n, par = E * c + e, e % 2
                    dve.wait_ge(down_done, n + 1)
                    if e == 0:
                        dve.wait_ge(weight_ready, c + 1)
                        dve.wait_ge(base_ready, c + 1)
                    else:
                        dve.wait_ge(added, n)
                    for t in range(GT):
                        tile = v.xa[:, GT * c + t, :]
                        last = nc.vector.scalar_tensor_tensor(tile, ps_d[par][:, t * P:(t + 1) * P], weight[:, GT * c + t, e:e + 1], tile,
                                                              ALU.mult, ALU.add)
                    last.then_inc(added, 1)

                def pick(k, i):
                    if i == 0:
                        return nc.vector.reduce_max(best[k][:, :, 0], scores[:], AX.X)
                    if i == 1:
                        return nc.vector.tensor_tensor(equal[:], scores[:], best[k][:].broadcast_to([P, GT, E]), ALU.is_equal)
                    if i == 2:
                        return nc.vector.tensor_tensor(ranked[:], equal[:], v.first_wins[:].unsqueeze(1).broadcast_to([P, GT, E]), ALU.mult)
                    if i == 3:
                        return nc.vector.reduce_max(first[:, :, 0], ranked[:], AX.X)
                    return nc.vector.tensor_tensor(chosen[k][:], ranked[:], first[:].broadcast_to([P, GT, E]), ALU.is_equal)

                def route(c, i):
                    if not there(c) or not 0 <= i < ROUTE:
                        return
                    if i == 0:
                        dve.wait_ge(routed, c + 1)
                        if there(c - 1):
                            dve.wait_ge(weight_ready, c)
                        last = nc.vector.tensor_copy(scores[:], ps_r[:, 0:GT * E].rearrange("p (t e) -> p t e", t=GT))
                    else:
                        dve.wait_ge(routing, ROUTE * c + i)
                    if 1 <= i <= 5:
                        last = pick(0, i - 1)
                    if i == 6:
                        last = nc.vector.scalar_tensor_tensor(scores[:], chosen[0][:], -BIG, scores[:], ALU.mult, ALU.add)
                    if i == 7:
                        last = pick(1, 0)
                    if i == 8:
                        last = nc.vector.tensor_tensor(gap[:], best[1][:], best[0][:], ALU.subtract)
                    if 9 <= i <= 12:
                        last = pick(1, i - 8)
                    if i == 13:
                        dve.wait_ge(ratio_ready, c + 1)
                        last = nc.vector.tensor_scalar(one_plus[:], ratio[:], 1.0, None, ALU.add)
                    if i == 14:
                        last = nc.vector.reciprocal(one_plus[:], one_plus[:])
                    if i == 15:
                        last = nc.vector.tensor_scalar(w_best[0][:], one_plus[:], v.half_gate[:, 0:1], None, ALU.mult)
                    last.then_inc(routing, 1)

                def step(c):
                    for e in range(E):
                        at = 3 * (e - 2) + (1 if e > 4 else 0)
                        unit(*((c, e + 1) if e + 1 < E else (c + 1, 0)), lambda: route(c + 1, at))
                        route(c + 1, at + 1)
                        if there(c):
                            add(c, e)
                        route(c + 1, at + 2)
                        if e == 4:
                            route(c + 1, at + 3)
                        if e == 3 and there(c) and there(c - 1):
                            for t in range(GT):
                                nc.vector.bn_stats(v.stat6[:, GT * (c - 1) + t, :], v.xa[:, GT * (c - 1) + t, :])
                        if e == 0 and there(c + 1):
                            dve.wait_ge(lat_ready, c + 2)
                            nc.vector.scalar_tensor_tensor(v.xa[:, bass.ds(GT * (c + 1), GT), :], lat[:], v.tgate[:, 2:3],
                                                           v.xb[:, bass.ds(GT * (c + 1), GT), :], ALU.mult, ALU.add).then_inc(base_ready, 1)
                        if e == 1 and there(c + 1):
                            dve.wait_ge(xn_high, c + 2)
                            nc.vector.tensor_tensor(xn_l[:, c + 1, :], xn[:], xn_h[:, c + 1, :].bitcast(F32), ALU.subtract).then_inc(xn_low, 1)

                each_chunk(dve, step)
                dve.wait_ge(added, E * NG)
                for n in range(NT - GT, NT):
                    nc.vector.bn_stats(v.stat6[:, n, :], v.xa[:, n, :])

            @block.gpsimd
            def _(pool):
                def unit(c, e):
                    n, par = E * c + e, e % 2
                    pool.wait_ge(gated_done, n + 1)
                    pool.wait_ge(u_copied, n + 1)
                    if there(c - 1) or e >= 2:
                        pool.wait_ge(down_done, n - 1)
                    nc.gpsimd.tensor_tensor(hidden[par][:, 1], gated[par][:, 1], u_copy[par][:], ALU.mult).then_inc(hidden1_done, 1)

                def step(c):
                    for e in range(E):
                        if there(c):
                            unit(c, e)
                        if there(c + 2) and not (isinstance(c, int) and c == -2):
                            for i in {0: (0, 1), 1: (2, 3), 2: (4,), 3: (5, 6), 4: (7,), 5: (8,)}.get(e, ()):
                                w.norm_part(pool, c + 2, i)
                        if e == 7 and there(c + 1):
                            at = 2 * (c + 1)
                            pool.wait_ge(routing, ROUTE * (c + 2))
                            nc.gpsimd.tensor_tensor(w_best[1][:], w_best[0][:], ratio[:], ALU.mult).then_inc(weight_parts, 1)
                            nc.gpsimd.tensor_tensor(parts[0][:], chosen[0][:], w_best[0][:].broadcast_to([P, GT, E]), ALU.mult)
                            pool.wait_ge(weight_parts, at + 1)
                            nc.gpsimd.tensor_tensor(parts[1][:], chosen[1][:], w_best[1][:].broadcast_to([P, GT, E]), ALU.mult).then_inc(weight_parts, 1)
                            pool.wait_ge(weight_parts, at + 2)
                            nc.gpsimd.tensor_tensor(weight[:, bass.ds(GT * (c + 1), GT), :], parts[0][:], parts[1][:], ALU.add).then_inc(weight_ready, 1)

                each_chunk(pool, step)


def attention1(nc, v):
    with ExitStack() as ctx:
        sb = lambda name, shape, dt=F32: ctx.enter_context(nc.sbuf_tensor(name, shape, dt))
        w = Env()
        w.m_h, w.m_l = sb("c_m_h", [P, H, D], F32R), sb("c_m_l", [P, H, D], F32R)
        w.n_h, w.n_l = sb("c_n_h", [P, H, D], F32R), sb("c_n_l", [P, H, D], F32R)
        w.rstd, w.shift = sb("c_rstd", [P, 2, NT]), sb("c_shift", [P, 2, NT])
        w.normed, w.norm_parts = ctx.enter_context(nc.semaphore("normed_rows")), ctx.enter_context(nc.semaphore("norm_parts"))
        w.scratch_tile = sb("c_norm_scratch", [P, 16, 2, GT])

        def norm_part(pool, g, i):
            tiles = slice(GT * g, GT * (g + 1)) if isinstance(g, int) else bass.ds(GT * g, GT)
            last = norm_step(nc, pool, w, i, w.norm_parts, (TWICE_STEPS - 1) * g, lambda k: v.stats[:, :, tiles, k],
                             w.rstd[:, :, tiles], w.shift[:, :, tiles], second=(slice(None), 1), twice=(w.rstd[:, 1, tiles], w.shift[:, 1, tiles]))
            last.then_inc(w.normed if i == TWICE_STEPS - 1 else w.norm_parts, 1)

        w.norm_part = norm_part
        w.mask_bias = sb("c_mask_bias", [1, BATCH, SEQ], BF16)
        attention1_weights(nc, v, w)
        attention1_main(nc, v, w)


def attention1_weights(nc, v, w):
    with ExitStack() as ctx:
        sem = lambda name: ctx.enter_context(nc.semaphore(name))
        sb = lambda name, shape, dt=F32: ctx.enter_context(nc.sbuf_tensor(name, shape, dt))
        banks = [ctx.enter_context(nc.psum_tensor(f"cw_ps{i}", [P, 512], F32)) for i in range(4)]
        turned_w = sb("cw_turned", [P, 3, H // 2, D])
        turned, copied = sem("turned"), sem("copied")
        product_done, high_done, low_done = sem("product_done"), sem("high_done"), sem("low_done")
        zeroed = sem("norm_constants")
        TURNS, PRODUCTS = 6, 2 * H // 4
        first_head = lambda r: 8 * (r % 4 // 2) + r % 2
        heads_of = lambda r: slice(first_head(r), first_head(r) + 7, 2)
        with nc.Block() as block:

            @block.tensor
            def _(pe):
                pe.wait_ge(v.weights2_loaded, 128)
                for r in range(TURNS):
                    if r >= 4:
                        pe.wait_ge(copied, r - 3)
                    for i in range(4):
                        pair = 4 * (r % 2) + i
                        source = (v.wq1_raw, v.wkv1_raw, v.wkv1_raw)[r // 2]
                        at = pair * P + (H * HD1 if r // 2 == 2 else 0)
                        last = nc.tensor.transpose(banks[r % 4][:, i * P:(i + 1) * P], source[:, at:at + P], v.ident[:])
                    last.then_inc(turned, 1)
                pe.wait_ge(copied, TURNS)
                for r in range(PRODUCTS):
                    if r >= 4:
                        pe.wait_ge(low_done, r - 3)
                    for i in range(4):
                        h = first_head(r) + 2 * i
                        rows = slice(HD1 * (h % 2), HD1 * (h % 2 + 1))
                        left, right = ((turned_w[rows, 0, h // 2], turned_w[rows, 1, h // 2]) if r < 4
                                       else (turned_w[rows, 2, h // 2], v.wout1_raw[rows, h // 2]))
                        last = nc.tensor.matmul(banks[r % 4][:, i * P:(i + 1) * P], left, right, start=True, stop=True)
                    last.then_inc(product_done, 1)

            @block.scalar
            def _(act):
                for r in range(TURNS):
                    act.wait_ge(turned, r + 1)
                    nc.scalar.activation(turned_w[:, r // 2, 4 * (r % 2):4 * (r % 2) + 4], banks[r % 4][:].rearrange("p (i d) -> p i d", i=4),
                                         ACT.Copy).then_inc(copied, 1)
                for r in range(PRODUCTS):
                    act.wait_ge(product_done, r + 1)
                    high = (w.m_h, w.n_h)[r // 4][:, heads_of(r)]
                    nc.scalar.activation(high, banks[r % 4][:].rearrange("p (i d) -> p i d", i=4), ACT.Copy,
                                         scale=float(HD1) ** -0.5 if r < 4 else 1.0).then_inc(high_done, 1)

            @block.vector
            def _(dve):
                dve.wait_ge(v.weights2_loaded, 128)
                nc.vector.tensor_scalar(w.mask_bias[:], v.mask_u8[:].rearrange("a (b s) -> a b s", b=BATCH), -1.0, 3e38, ALU.add, ALU.mult)
                for r in range(PRODUCTS):
                    dve.wait_ge(high_done, r + 1)
                    high, low = ((w.m_h, w.m_l), (w.n_h, w.n_l))[r // 4]
                    nc.vector.scalar_tensor_tensor(low[:, heads_of(r)], banks[r % 4][:].rearrange("p (i d) -> p i d", i=4),
                                                   float(HD1) ** -0.5 if r < 4 else 1.0, high[:, heads_of(r)].bitcast(F32),
                                                   ALU.mult, ALU.subtract).then_inc(low_done, 1)

            @block.gpsimd
            def _(pool):
                norm_constants(nc, w, w.scratch_tile, LN_EPS).then_inc(zeroed, 1)
                pool.wait_ge(zeroed, 1)
                for i in range(TWICE_STEPS):
                    w.norm_part(pool, 0, i)


def attention1_main(nc, v, w):
    C = GT * P
    U = 2 * GB
    HH = H // 2
    KEYS = 2 * SEQ
    with ExitStack() as ctx:
        sem = lambda name: ctx.enter_context(nc.semaphore(name))
        sb = lambda name, shape, dt=F32: ctx.enter_context(nc.sbuf_tensor(name, shape, dt))
        pb = lambda name, shape: ctx.enter_context(nc.psum_tensor(name, shape, F32))
        hat = sb("c_hat", [P, 2, GT, D])
        kv_t = [sb(f"c_kv_t{i}", [P, GB, KEYS]) for i in range(2)]
        kv_h = [sb(f"c_kv_h{i}", [P, GB, D], F32R) for i in range(2)]
        kv_l = [sb(f"c_kv_l{i}", [P, GB, D], F32R) for i in range(2)]
        lat_h = [sb(f"c_lat_h{i}", [P, GB, SEQ], F32R) for i in range(2)]
        lat_l = [sb(f"c_lat_l{i}", [P, GB, SEQ], F32R) for i in range(2)]
        q_t = sb("c_q_t", [P, GB, H, SEQ])
        neg_max, sums, recip = ([sb(f"c_{name}{i}", [P, 4]) for i in range(2)] for name in ("neg_max", "sums", "recip"))
        probs = [sb(f"c_probs{i}", [P, 4, KEYS]) for i in range(2)]
        normed = [sb(f"c_normed{i}", [P, 4, KEYS]) for i in range(2)]
        probs_h, probs_l = sb("c_probs_h", [P, 512], F32R), sb("c_probs_l", [P, 512], F32R)
        y_h, y_l = sb("c_y_h", [P, H, C], F32R), sb("c_y_l", [P, H, C], F32R)
        out_t = sb("c_out_t", [P, C])

        ps_s = [pb(f"c_ps_s{i}", [P, 4, KEYS]) for i in range(2)]
        ps_q = [pb(f"c_ps_q{i}", [P, 2, C]) for i in range(2)]
        ps_t, ps_y, ps_o, ps_x = (pb(f"c_ps_{n}", [P, 512]) for n in "tyox")

        hat_ready, hat_turned, kv_t_ready, lat_high, lat_low = (sem(n) for n in ("hat_ready", "hat_turned", "kv_t_ready", "lat_high", "lat_low"))
        kv_turned, kv_high, kv_low = sem("kv_turned"), sem("kv_high"), sem("kv_low")
        q_done, q_ready, scores_done, max_ready, exp_done, recip_ready, normed_ready = (
            sem(n) for n in ("q_done", "q_ready", "scores_done", "max_ready", "exp_done", "recip_ready", "normed_ready"))
        probs_turned, probs_high, probs_low = sem("probs_turned"), sem("probs_high"), sem("probs_low")
        y_done, y_high, y_low = sem("y_done"), sem("y_high"), sem("y_low")
        x3_stats, x3_constants = sem("x3_stats"), sem("x3_norm_constants")
        out_done, out_copied, out_turned, x3_ready = sem("out_done"), sem("out_copied"), sem("out_turned"), sem("x3_ready")

        with nc.Block() as block:

            def each_group(eng, step):
                for g in range(-2, 4):
                    step(g, g % 2)
                with eng.Fori(2, NG // 2 - 1) as i:
                    step(2 * i, 0)
                    step(2 * i + 1, 1)
                for g in range(NG - 2, NG + 1):
                    step(g, g % 2)

            def ahead(g, u, k):
                return (g, u + k, 0) if u + k < U else (g + 1, u + k - U, 1)

            def q_heads(g, u):
                return (g, 7, 0) if u == 0 else (g + 1, u - 1, 1)

            def out_heads(g, u):
                return (g - 1, 3 + u) if u < 5 else (g, u - 5)

            def before(g, u):
                return (g, u - 1, 0) if u else (g - 1, U - 1, 1)

            @block.tensor
            def _(pe):
                def step(g, par):
                    for u in range(U):
                        n = U * g + u
                        gs, us, flip = ahead(g, u, 2)
                        if there(gs):
                            b, half = us % GB, us // GB
                            pe.wait_ge(q_ready, 8 * gs + 4 * (half + 1))
                            pe.wait_ge(kv_t_ready, 2 * gs + 2)
                            if there(g):
                                pe.wait_ge(exp_done, n + 1)
                            bank = ps_s[us % 2]
                            for i in range(4):
                                h = HH * half + 2 * i
                                nc.tensor.matmul(bank[:, i], q_t[:, b, h:h + 2].rearrange("p h s -> p (h s)"), kv_t[par ^ flip][:, b],
                                                 start=i == 0, stop=False, skip_group_check=True)
                            nc.tensor.matmul(bank[:, :, 0:SEQ], v.ones_row[:], w.mask_bias[:, GB * gs + b, :].unsqueeze(1).broadcast_to([1, 4, SEQ]),
                                             start=False, stop=True, skip_group_check=True).then_inc(scores_done, 1)
                        gb, ub, flip = before(g, u)
                        if there(gb):
                            pe.wait_ge(probs_low, n)
                            pe.wait_ge(kv_low, gb + 1)
                            if there(gb - 1) or ub:
                                pe.wait_ge(y_low, n - 1)
                            b, own = ub % GB, par ^ flip
                            split_products(nc, ps_y[:], (kv_h[own][:, b], kv_l[own][:, b]), (probs_h[:], probs_l[:]), True, True).then_inc(y_done, 1)
                        if there(g):
                            pe.wait_ge(normed_ready, n + 1)
                            if there(g - 1) or u:
                                pe.wait_ge(probs_low, n)
                            for i in range(4):
                                last = nc.tensor.transpose(ps_t[:, i * P:(i + 1) * P], normed[u % 2][:, i], v.ident[:])
                            last.then_inc(probs_turned, 1)
                        if u == 0 and there(g + 1):
                            pe.wait_ge(hat_ready, g + 2)
                            if there(g - 2):
                                pe.wait_ge(x3_ready, g - 1)
                            for k in range(2):
                                for t in range(GT):
                                    last = nc.tensor.transpose(ps_x[:, (2 * k + t) * P:(2 * k + t + 1) * P], hat[:, k, t], v.ident[:])
                            last.then_inc(hat_turned, 1)
                        if u == 3 and there(g + 1):
                            pe.wait_ge(kv_t_ready, 2 * (g + 1) + 2)
                            pe.wait_ge(lat_low, g + 2)
                            for b in range(GB):
                                last = nc.tensor.transpose(ps_x[:, b * P:(b + 1) * P], kv_t[1 - par][:, b], v.ident[:])
                            last.then_inc(kv_turned, 1)
                        if u == 6 and there(g - 1):
                            pe.wait_ge(out_copied, g)
                            if there(g + 1):
                                pe.wait_ge(kv_low, g + 2)
                            for t in range(GT):
                                last = nc.tensor.transpose(ps_x[:, t * P:(t + 1) * P], out_t[:, t * P:(t + 1) * P], v.ident[:])
                            last.then_inc(out_turned, 1)
                        go, pair = out_heads(g, u)
                        if there(go):
                            if pair == 0 and there(go - 1):
                                pe.wait_ge(out_copied, go)
                            pe.wait_ge(y_low, U * go + 4 * (pair // 4 + 1))
                            for h in (2 * pair, 2 * pair + 1):
                                last = split_products(nc, ps_o[:, 0:C], (w.n_h[:, h], w.n_l[:, h]), (y_h[:, h], y_l[:, h]), h == 0, h == H - 1)
                            if pair == 7:
                                last.then_inc(out_done, 1)
                        gq, pair, flip = q_heads(g, u)
                        if there(gq):
                            lat = par ^ flip
                            pe.wait_ge(lat_low, gq + 1)
                            if there(gq - 1) or pair >= 2:
                                pe.wait_ge(q_ready, 8 * gq + pair - 1)
                            for i in range(2):
                                h = 2 * pair + i
                                last = split_products(nc, ps_q[pair % 2][:, i], (w.m_h[:, h], w.m_l[:, h]),
                                                      (lat_h[lat][:].rearrange("p b s -> p (b s)"), lat_l[lat][:].rearrange("p b s -> p (b s)")), True, True)
                            last.then_inc(q_done, 1)

                each_group(pe, step)

            @block.scalar
            def _(act):
                def step(g, par):
                    for u in range(U):
                        n = U * g + u
                        if u == 5 and there(g - 1):
                            act.wait_ge(out_done, g)
                            if there(g - 2):
                                act.wait_ge(out_turned, g - 1)
                            nc.scalar.activation(out_t[:], ps_o[:, 0:C], ACT.Copy).then_inc(out_copied, 1)
                        gb, ub, _ = before(g, u)
                        if there(gb):
                            act.wait_ge(y_done, n)
                            b, half = ub % GB, ub // GB
                            nc.scalar.activation(y_h[:, HH * half:HH * (half + 1), b * SEQ:(b + 1) * SEQ], ps_y[:].rearrange("p (h s) -> p h s", h=HH),
                                                 ACT.Copy).then_inc(y_high, 1)
                        if there(g):
                            act.wait_ge(probs_turned, n + 1)
                            if there(g - 1) or u:
                                act.wait_ge(y_done, n)
                            nc.scalar.activation(probs_h[:], ps_t[:], ACT.Copy).then_inc(probs_high, 1)
                        gs, us, flip = ahead(g, u, 2)
                        if there(gs):
                            act.wait_ge(max_ready, U * gs + us + 1)
                            if there(g):
                                act.wait_ge(normed_ready, n + 1)
                            for i in range(4):
                                last = nc.scalar.activation(probs[us % 2][:, i], ps_s[us % 2][:, i], ACT.Exp, bias=neg_max[us % 2][:, i:i + 1],
                                                            accum_out=sums[us % 2][:, i:i + 1])
                            last.then_inc(exp_done, 1)
                        if u == 0 and there(g + 1):
                            act.wait_ge(hat_turned, g + 2)
                            for k in range(2):
                                nc.scalar.activation(kv_t[1 - par][:, :, k * SEQ:(k + 1) * SEQ],
                                                     ps_x[:, k * C:(k + 1) * C].rearrange("p (b s) -> p b s", b=GB), ACT.Identity,
                                                     bias=v.vec2[:, 2 * k + 1:2 * k + 2], scale=v.vec2[:, 2 * k:2 * k + 1]).then_inc(kv_t_ready, 1)
                            act.wait_ge(kv_t_ready, 2 * (g + 1) + 2)
                            nc.scalar.activation(lat_h[1 - par][:], kv_t[1 - par][:, :, SEQ:KEYS], ACT.Copy).then_inc(lat_high, 1)
                        if u == 3 and there(g + 1):
                            act.wait_ge(kv_turned, g + 2)
                            nc.scalar.activation(kv_h[1 - par][:], ps_x[:].rearrange("p (b d) -> p b d", b=GB), ACT.Copy).then_inc(kv_high, 1)

                each_group(act, step)

            @block.vector
            def _(dve):
                def step(g, par):
                    for u in range(U):
                        n = U * g + u
                        g1, u1, _ = ahead(g, u, 1)
                        if there(g1):
                            n1 = U * g1 + u1
                            dve.wait_ge(exp_done, n1 + 1)
                            if there(g1 - 1) or u1 >= 2:
                                dve.wait_ge(normed_ready, n1 - 1)
                            nc.vector.reciprocal(recip[u1 % 2][:], sums[u1 % 2][:]).then_inc(recip_ready, 1)
                        gs, us, _ = ahead(g, u, 2)
                        if there(gs):
                            dve.wait_ge(scores_done, U * gs + us + 1)
                            nc.vector.tensor_reduce(neg_max[us % 2][:], ps_s[us % 2][:], AX.X, ALU.max, negate=True).then_inc(max_ready, 1)
                        gb, ub, _ = before(g, u)
                        if there(gb):
                            b, half = ub % GB, ub // GB
                            dve.wait_ge(y_high, n)
                            nc.vector.tensor_tensor(y_l[:, HH * half:HH * (half + 1), b * SEQ:(b + 1) * SEQ], ps_y[:].rearrange("p (h s) -> p h s", h=HH),
                                                    y_h[:, HH * half:HH * (half + 1), b * SEQ:(b + 1) * SEQ].bitcast(F32), ALU.subtract).then_inc(y_low, 1)
                        if there(g):
                            dve.wait_ge(probs_high, n + 1)
                            nc.vector.tensor_tensor(probs_l[:], ps_t[:], probs_h[:].bitcast(F32), ALU.subtract).then_inc(probs_low, 1)
                        gq, pair, _ = q_heads(g, u)
                        if there(gq):
                            dve.wait_ge(q_done, 8 * gq + pair + 1)
                            nc.vector.tensor_copy(q_t[:, :, 2 * pair:2 * pair + 2].rearrange("p b h s -> p h b s"),
                                                  ps_q[pair % 2][:].rearrange("p h (b s) -> p h b s", b=GB)).then_inc(q_ready, 1)
                        if u == 0 and there(g + 1):
                            dve.wait_ge(lat_high, g + 2)
                            nc.vector.tensor_tensor(lat_l[1 - par][:], kv_t[1 - par][:, :, SEQ:KEYS], lat_h[1 - par][:].bitcast(F32), ALU.subtract
                                                    ).then_inc(lat_low, 1)
                        if u == 3 and there(g + 1):
                            dve.wait_ge(kv_high, g + 2)
                            nc.vector.tensor_tensor(kv_l[1 - par][:], ps_x[:].rearrange("p (b d) -> p b d", b=GB), kv_h[1 - par][:].bitcast(F32),
                                                    ALU.subtract).then_inc(kv_low, 1)
                        if u == 6 and there(g - 1):
                            residual(g - 1)
                        if u == 6 and there(g + 2):
                            dve.wait_ge(w.normed, g + 3)
                            if there(g + 1):
                                dve.wait_ge(hat_turned, g + 2)
                            for k, source in enumerate((v.cx, v.xa)):
                                for t in range(GT):
                                    at = GT * (g + 2) + t
                                    last = nc.vector.tensor_scalar(hat[:, k, t], source[:, at, :], w.rstd[:, k, bass.ds(at, 1)], w.shift[:, k, bass.ds(at, 1)],
                                                                   ALU.mult, ALU.add)
                            last.then_inc(hat_ready, 1)

                def residual(g):
                    dve.wait_ge(out_turned, g + 1)
                    if there(g - 1):
                        dve.wait_ge(x3_ready, g)
                    for t in range(GT):
                        n = GT * g + t
                        last = nc.vector.scalar_tensor_tensor(v.xb[:, n, :], ps_x[:, t * P:(t + 1) * P], v.tgate[:, 1:2], v.xa[:, n, :], ALU.mult, ALU.add)
                    last.then_inc(x3_ready, 1)
                    if there(g - 1):
                        for t in range(GT):
                            last = nc.vector.bn_stats(v.stat6[:, GT * (g - 1) + t, :], v.xb[:, GT * (g - 1) + t, :])
                        last.then_inc(x3_stats, 1)

                each_group(dve, step)
                dve.wait_ge(x3_ready, NG)
                for n in range(NT - GT, NT):
                    nc.vector.bn_stats(v.stat6[:, n, :], v.xb[:, n, :])

            @block.gpsimd
            def _(pool):
                norm_constants(nc, v.norm3, v.norm3_tile, 0.0).then_inc(x3_constants, 1)
                pool.wait_ge(x3_constants, 1)

                def step(g, par):
                    for u in range(U):
                        if there(g + 2) and not (isinstance(g, int) and g == -2):
                            for i in {0: (0, 1), 1: (2, 3), 2: (4,), 3: (5, 6), 4: (7, 8), 5: (9,)}.get(u, ()):
                                w.norm_part(pool, g + 2, i)
                        if there(g - 3) and u >= 6:
                            if u == 6:
                                pool.wait_ge(x3_stats, g - 2)
                            for i in ((0, 1, 2, 3), (4, 5, 6))[u - 6]:
                                v.norm3_part(pool, g - 3, i)
                        g1, u1, _ = ahead(g, u, 1)
                        if not there(g1):
                            continue
                        n1 = U * g1 + u1
                        pool.wait_ge(recip_ready, n1 + 1)
                        if there(g1 - 1) or u1 >= 2:
                            pool.wait_ge(probs_turned, n1 - 1)
                        nc.gpsimd.tensor_tensor(normed[u1 % 2][:], probs[u1 % 2][:], recip[u1 % 2][:].unsqueeze(2).broadcast_to([P, 4, KEYS]), ALU.mult
                                                ).then_inc(normed_ready, 1)

                each_group(pool, step)


def mixture1(nc, v, out):
    with ExitStack() as ctx:
        sb = lambda name, shape, dt=F32: ctx.enter_context(nc.sbuf_tensor(name, shape, dt))
        w = Env()
        w.e_h, w.e_l, w.router = sb("d_e_h", [P, E * D], F32R), sb("d_e_l", [P, E * D], F32R), sb("d_router", [P, E])
        w.bias_pair, w.ones_pair = sb("d_bias_pair", [2, E * D], F32R), sb("d_ones_pair", [2, P], F32R)
        mixture1_weights(nc, v, w)
        mixture1_main(nc, v, w, out)


def mixture1_weights(nc, v, w):
    with ExitStack() as ctx:
        sem = lambda name: ctx.enter_context(nc.semaphore(name))
        sb = lambda name, shape, dt=F32: ctx.enter_context(nc.sbuf_tensor(name, shape, dt))
        banks = [ctx.enter_context(nc.psum_tensor(f"dw_ps{i}", [P, 512], F32)) for i in range(3)]
        bias_high, bias_low, bias_top = sb("dw_bias_high", [2, E * D], F32R), sb("dw_bias_low", [2, E * D]), sb("dw_bias_top", [2, E * D])
        turned, high_done, bias_steps = sem("turned"), sem("high_done"), sem("bias_steps")
        with nc.Block() as block:

            @block.tensor
            def _(pe):
                pe.wait_ge(v.weights3_loaded, 64)
                for r in range(2):
                    for i in range(4):
                        last = nc.tensor.transpose(banks[r][:, i * P:(i + 1) * P], v.expert_raw[:, 4 * r + i], v.ident[:])
                    last.then_inc(turned, 1)
                nc.tensor.transpose(banks[2][:, 0:E], v.router1_raw[:], v.ident[0:E, 0:E]).then_inc(turned, 1)

            @block.scalar
            def _(act):
                for r in range(2):
                    act.wait_ge(turned, r + 1)
                    nc.scalar.activation(w.e_h[:, r * 512:(r + 1) * 512], banks[r][:], ACT.Copy).then_inc(high_done, 1)
                act.wait_ge(turned, 3)
                nc.scalar.activation(w.router[:], banks[2][:, 0:E], ACT.Copy)

            @block.vector
            def _(dve):
                dve.wait_ge(v.weights3_loaded, 64)
                nc.vector.tensor_copy(w.ones_pair[:], v.ones_pair_f[:])
                nc.vector.tensor_copy(bias_high[:], v.expert_b_rows[:]).then_inc(bias_steps, 1)
                dve.wait_ge(bias_steps, 1)
                nc.vector.tensor_tensor(bias_low[:], v.expert_b_rows[:], bias_high[:].bitcast(F32), ALU.subtract)
                nc.vector.tensor_scalar(bias_top[:], bias_high[:].bitcast(F32), v.ident[0:2, 0:1], None, ALU.mult).then_inc(bias_steps, 1)
                dve.wait_ge(bias_steps, 2)
                nc.vector.scalar_tensor_tensor(w.bias_pair[:], bias_low[:], v.ident[0:2, 1:2], bias_top[:], ALU.mult, ALU.add)
                for r in range(2):
                    cols = slice(r * 512, (r + 1) * 512)
                    dve.wait_ge(high_done, r + 1)
                    nc.vector.tensor_tensor(w.e_l[:, cols], banks[r][:], w.e_h[:, cols].bitcast(F32), ALU.subtract)


def mixture1_main(nc, v, w, out):
    C = GT * P
    HALF = E // 2
    with ExitStack() as ctx:
        sem = lambda name: ctx.enter_context(nc.semaphore(name))
        sb = lambda name, shape, dt=F32: ctx.enter_context(nc.sbuf_tensor(name, shape, dt))
        pb = lambda name, shape: ctx.enter_context(nc.psum_tensor(name, shape, F32))
        hat = sb("d_hat", [P, GT, D])
        hat_t = sb("d_hat_t", [P, C])
        hat_h, hat_l = ([sb(f"d_hat_{n}{i}", [P, C], F32R) for i in range(2)] for n in "hl")
        logits, shifted, exps = sb("d_logits", [P, GT, E]), sb("d_shifted", [P, GT, E]), sb("d_exps", [P, GT, E])
        best, first, total = sb("d_best", [P, GT, 1]), sb("d_first", [P, GT, 1]), sb("d_total", [P, GT, 1])
        equal, ranked, chosen = sb("d_equal", [P, GT, E]), sb("d_ranked", [P, GT, E]), sb("d_chosen", [P, GT, E])
        weight = [sb(f"d_weight{i}", [P, GT, E]) for i in range(2)]
        scaled = [sb(f"d_scaled{i}", [P, HALF, D]) for i in range(2)]
        pairs, four = sb("d_pairs", [P, 2, D]), sb("d_four", [P, D])
        ps_lo, ps_hi = ([pb(f"d_ps_{n}{i}", [P, HALF, D]) for i in range(2)] for n in ("lo", "hi"))
        ps_x, ps_r = pb("d_ps_x", [P, 512]), pb("d_ps_r", [P, 512])
        hat_ready, turned, copied, high_done, low_done, routed, route = (
            sem(n) for n in ("hat_ready", "turned", "copied", "high_done", "low_done", "routed", "route"))
        shifted_ready, exps_ready, weight_ready = sem("shifted_ready"), sem("exps_ready"), sem("weight_ready")
        experts_done, added, scaled_done, pool_steps, tile_done, stored = (
            sem(n) for n in ("experts_done", "added", "scaled_done", "pool_steps", "tile_done", "stored"))
        ROUTE = 8

        with nc.Block() as block:

            def each_group(eng, step):
                for g in range(-2, 1):
                    step(g, g % 2)
                with eng.Fori(0, (NG - 4) // 2) as i:
                    step(2 * i + 1, 1)
                    step(2 * i + 2, 0)
                for g in range(NG - 3, NG):
                    step(g, g % 2)

            @block.sync
            def _(sp):
                rows = out.rearrange("(t c) s d -> (c s) t d", c=2)
                with sp.Fori(0, NG) as g:
                    sp.wait_ge(tile_done, GT * g + GT)
                    sp.dma_start(rows[:, bass.ds(GT * g, GT), :], v.xa[:, bass.ds(GT * g, GT), :]).then_inc(stored, 16)
                sp.wait_ge(stored, 16 * NG)

            @block.tensor
            def _(pe):
                def step(g, par):
                    for t in range(GT):
                        if there(g):
                            n = GT * g + t
                            pe.wait_ge(low_done, g + 1)
                            if there(g - 1):
                                pe.wait_ge(added, HALF * (n - 1))
                                pe.wait_ge(scaled_done, n - 1)
                            for half, bank in enumerate((ps_lo[t], ps_hi[t])):
                                cols = slice(half * 512, (half + 1) * 512)
                                flat = bank[:].rearrange("p e d -> p (e d)")
                                nc.tensor.matmul(flat, w.ones_pair[:], w.bias_pair[:, cols], start=True, stop=False)
                                last = split_products(nc, flat, (hat_h[par][:, t * P:(t + 1) * P], hat_l[par][:, t * P:(t + 1) * P]),
                                                      (w.e_h[:, cols], w.e_l[:, cols]), False, True)
                            last.then_inc(experts_done, 1)
                        if t == 1 and there(g + 1):
                            pe.wait_ge(copied, g + 2)
                            for s in range(GT):
                                last = nc.tensor.matmul(ps_r[:, s * E:(s + 1) * E], hat_t[:, s * P:(s + 1) * P], w.router[:], start=True, stop=True)
                            last.then_inc(routed, 1)
                        if t == 0 and there(g + 1):
                            pe.wait_ge(hat_ready, g + 2)
                            for s in range(GT):
                                last = nc.tensor.transpose(ps_x[:, s * P:(s + 1) * P], hat[:, s], v.ident[:])
                            last.then_inc(turned, 1)

                each_group(pe, step)

            @block.scalar
            def _(act):
                def step(g, par):
                    for t in range(GT):
                        if t == 0 and there(g + 1):
                            act.wait_ge(turned, g + 2)
                            if there(g):
                                act.wait_ge(routed, g + 1)
                                act.wait_ge(low_done, g + 1)
                            nc.scalar.activation(hat_t[:], ps_x[:, 0:C], ACT.Copy).then_inc(copied, 1)
                            act.wait_ge(copied, g + 2)
                            nc.scalar.activation(hat_h[1 - par][:], hat_t[:], ACT.Copy).then_inc(high_done, 1)
                        if there(g):
                            n = GT * g + t
                            act.wait_ge(experts_done, n + 1)
                            act.wait_ge(weight_ready, g + 1)
                            if there(g - 1):
                                act.wait_ge(pool_steps, 2 * (n - 2) + 1)
                            for e in range(HALF):
                                last = nc.scalar.activation(scaled[t][:, e], ps_hi[t][:, e], ACT.Copy, scale=weight[par][:, t, HALF + e:HALF + e + 1])
                            last.then_inc(scaled_done, 1)
                        if t == 1 and there(g + 1):
                            act.wait_ge(shifted_ready, g + 2)
                            nc.scalar.activation(exps[:], shifted[:], ACT.Exp).then_inc(exps_ready, 1)

                each_group(act, step)

            @block.vector
            def _(dve):
                def step(g, par):
                    for t in range(GT):
                        if t == 0 and there(g + 1):
                            dve.wait_ge(high_done, g + 2)
                            nc.vector.tensor_tensor(hat_l[1 - par][:], hat_t[:], hat_h[1 - par][:].bitcast(F32), ALU.subtract).then_inc(low_done, 1)
                        if there(g):
                            n = GT * g + t
                            for e in range(HALF):
                                if e == 0:
                                    dve.wait_ge(experts_done, n + 1)
                                    dve.wait_ge(weight_ready, g + 1)
                                else:
                                    dve.wait_ge(added, HALF * n + e)
                                before = v.xb[:, n, :] if e == 0 else v.xa[:, n, :]
                                nc.vector.scalar_tensor_tensor(v.xa[:, n, :], ps_lo[t][:, e], weight[par][:, t, e:e + 1], before, ALU.mult, ALU.add
                                                               ).then_inc(added, 1)
                        if t == 0 and there(g + 2):
                            if not isinstance(g, int) or g >= NG - 4:
                                dve.wait_ge(v.normed3, NG)
                            if there(g + 1):
                                dve.wait_ge(turned, g + 2)
                            for s in range(GT):
                                at = GT * (g + 2) + s
                                last = nc.vector.tensor_scalar(hat[:, s], v.xb[:, at, :], v.rstd3[:, bass.ds(at, 1)], v.shift3[:, bass.ds(at, 1)],
                                                               ALU.mult, ALU.add)
                            last.then_inc(hat_ready, 1)
                        if t == 1 and there(g + 1):
                            choose(g + 1, 1 - par)

                def choose(g, par):
                    at = ROUTE * g
                    wide = [P, GT, E]
                    dve.wait_ge(routed, g + 1)
                    nc.vector.tensor_tensor(logits[:], ps_r[:, 0:GT * E].rearrange("p (t e) -> p t e", t=GT),
                                            v.router_b_row[:].unsqueeze(1).broadcast_to(wide), ALU.add).then_inc(route, 1)
                    dve.wait_ge(route, at + 1)
                    nc.vector.reduce_max(best[:, :, 0], logits[:], AX.X).then_inc(route, 1)
                    dve.wait_ge(route, at + 2)
                    nc.vector.tensor_tensor(shifted[:], logits[:], best[:].broadcast_to(wide), ALU.subtract).then_inc(shifted_ready, 1)
                    nc.vector.tensor_tensor(equal[:], logits[:], best[:].broadcast_to(wide), ALU.is_equal).then_inc(route, 1)
                    dve.wait_ge(route, at + 3)
                    nc.vector.tensor_tensor(ranked[:], equal[:], v.first_wins[:].unsqueeze(1).broadcast_to(wide), ALU.mult).then_inc(route, 1)
                    dve.wait_ge(route, at + 4)
                    nc.vector.reduce_max(first[:, :, 0], ranked[:], AX.X).then_inc(route, 1)
                    dve.wait_ge(route, at + 5)
                    nc.vector.tensor_tensor(chosen[:], ranked[:], first[:].broadcast_to(wide), ALU.is_equal).then_inc(route, 1)
                    dve.wait_ge(exps_ready, g + 1)
                    nc.vector.reduce_sum(total[:, :, 0], exps[:], AX.X).then_inc(route, 1)
                    dve.wait_ge(route, at + 7)
                    nc.vector.reciprocal(total[:], total[:]).then_inc(route, 1)
                    dve.wait_ge(route, at + 8)
                    nc.vector.tensor_scalar(total[:], total[:], v.tgate[:, 3:4], None, ALU.mult).then_inc(total_ready, 1)
                    dve.wait_ge(total_ready, g + 1)
                    nc.vector.tensor_tensor(weight[par][:], chosen[:], total[:].broadcast_to(wide), ALU.mult).then_inc(weight_ready, 1)

                total_ready = sem("total_ready")
                each_group(dve, step)

            @block.gpsimd
            def _(pool):
                for g in range(NG - 2, NG):
                    for i in range(NORM_STEPS):
                        v.norm3_part(pool, g, i)

                def step(g, par):
                    for t in range(GT):
                        if there(g):
                            n = GT * g + t
                            pool.wait_ge(scaled_done, n + 1)
                            nc.gpsimd.tensor_tensor(pairs[:], scaled[t][:, 0:2], scaled[t][:, 2:4], ALU.add).then_inc(pool_steps, 1)
                            pool.wait_ge(pool_steps, 2 * n + 1)
                            nc.gpsimd.tensor_tensor(four[:], pairs[:, 0], pairs[:, 1], ALU.add).then_inc(pool_steps, 1)
                            pool.wait_ge(pool_steps, 2 * n + 2)
                            pool.wait_ge(added, HALF * (n + 1))
                            nc.gpsimd.tensor_tensor(v.xa[:, n, :], v.xa[:, n, :], four[:], ALU.add).then_inc(tile_done, 1)

                each_group(pool, step)


INPUTS = ["x", "ctx_1024", "mask_BxS2_bk0", "g_xattn", "g_ffn", "L0_xattn_Wq", "L0_xattn_bq", "L0_xattn_Wk", "L0_xattn_bk",
          "L0_xattn_Wv", "L0_xattn_bv", "L0_xattn_Wo", "L0_xattn_bo", "L0_ffn_norm_scale", "L0_ffn_w_router", "L0_ffn_w_up",
          "L0_ffn_w_down", "L1_xattn_g1", "L1_xattn_b1", "L1_xattn_g2", "L1_xattn_b2", "L1_xattn_Wq", "L1_xattn_Wkv",
          "L1_xattn_Wout", "L1_ffn_router_w", "L1_ffn_router_b", "L1_ffn_expert_w", "L1_ffn_expert_b"]


def build_program(nc, io, out):
    with ExitStack() as ctx:
        sem = lambda name: ctx.enter_context(nc.semaphore(name))
        sb = lambda name, shape, dt=F32: ctx.enter_context(nc.sbuf_tensor(name, shape, dt))
        v = Env()
        v.first_loaded, v.x_loaded, v.weights0_loaded, v.weights1_loaded = sem("first_loaded"), sem("x_loaded"), sem("weights0_loaded"), sem("weights1_loaded")
        v.weights2_loaded, v.weights3_loaded, v.gates_ready = sem("weights2_loaded"), sem("weights3_loaded"), sem("gates_ready")
        v.xa, v.xb, v.cx = sb("xa", [P, NT, D]), sb("xb", [P, NT, D]), sb("cx", [P, NT, D])
        v.stats, v.norm_work = sb("stats", [P, 2, NT, 6]), sb("norm_work", [P, 8, GT])
        v.ctx_stat6, v.stat6 = v.stats[:, 0], v.stats[:, 1]
        v.rstd3, v.shift3, v.norm3_tile = sb("rstd3", [P, NT]), sb("shift3", [P, NT]), sb("norm3_scratch", [P, 16, GT])
        v.norm3, v.normed3, v.norm3_parts = Env(), sem("normed3"), sem("norm3_parts")

        def norm3_part(pool, g, i):
            tiles = slice(GT * g, GT * (g + 1)) if isinstance(g, int) else bass.ds(GT * g, GT)
            last = norm_step(nc, pool, v.norm3, i, v.norm3_parts, (NORM_STEPS - 1) * g, lambda k: v.stat6[:, tiles, k], v.rstd3[:, tiles],
                             v.shift3[:, tiles])
            last.then_inc(v.normed3 if i == NORM_STEPS - 1 else v.norm3_parts, 1)

        v.norm3_part = norm3_part
        v.ident, v.minus_half = sb("ident", [P, P]), sb("minus_half", [P, NT])
        v.zeros = sb("zeros", [P, GT])
        v.ones_row, v.ones_pair_f = sb("ones_row", [1, P], BF16), sb("ones_pair_f", [2, P])
        v.first_wins = sb("first_wins", [P, E])
        v.head_in_four, v.four_rows, v.q_mask = sb("head_in_four", [P, 4]), sb("four_rows", [P, 4]), sb("q_mask", [P, 4])
        v.four_cols = sb("four_cols", [P, D])
        v.gate, v.tgate, v.half_gate = sb("gate", [P, 4]), sb("tgate", [P, 4]), sb("half_gate", [P, 1])
        v.wq1_raw, v.wkv1_raw, v.wout1_raw = sb("wq1_raw", [P, H * HD1]), sb("wkv1_raw", [P, 2 * H * HD1]), sb("wout1_raw", [P, H // 2, D])
        v.vec2, v.mask_u8 = sb("vec2", [P, 4]), sb("mask_u8", [1, BATCH * SEQ], mybir.dt.uint8)
        v.expert_raw, v.router1_raw = sb("expert_raw", [P, E, D]), sb("router1_raw", [E, D])
        v.router_b_row, v.expert_b_rows = sb("router_b_row", [P, E]), sb("expert_b_rows", [2, E * D])
        with ExitStack() as layer0:
            sb0 = lambda name, shape, dt=F32: layer0.enter_context(nc.sbuf_tensor(name, shape, dt))
            v.w_up_raw, v.w_down_raw = sb0("w_up_raw", [P, E * 4, D]), sb0("w_down_raw", [P, E, HID])
            v.router0_raw, v.vec1 = sb0("router0_raw", [E, D]), sb0("vec1", [P, 1])
            with ExitStack() as first:
                sb0 = lambda name, shape, dt=F32: first.enter_context(nc.sbuf_tensor(name, shape, dt))
                v.wq0, v.wk0, v.wv0, v.wo0 = (sb0(n, [P, D]) for n in ("wq0", "wk0", "wv0", "wo0"))
                v.wq0_h, v.wq0_l, v.wk0_h, v.wk0_l = (sb0(n, [P, D], F32R) for n in ("wq0_h", "wq0_l", "wk0_h", "wk0_l"))
                v.wo0_j, v.vec0, v.bk_four = sb0("wo0_j", [P, 4, D]), sb0("vec0", [P, 3]), sb0("bk_four", [P, 4])
                v.bo_row, v.gbo = sb0("bo_row", [P, D]), sb0("gbo", [P, D])
                setup(nc, v, io)
                attention0(nc, v, io)
            mixture0(nc, v)
        attention1(nc, v)
        mixture1(nc, v, out)


def kernel(**inputs):
    import numpy as _np
    import concourse.bacc as _bacc
    from concourse import mybir as _mybir
    from concourse.bass_utils import run_bass_kernel_spmd as _run

    nc = _bacc.Bacc("TRN2", target_bir_lowering=False, num_devices=1)
    arrays, io = {}, {}
    for name in INPUTS:
        a = _np.ascontiguousarray(_np.asarray(inputs[name]))
        arrays[f"in_{name}"] = a
        io[name] = nc.dram_tensor(f"in_{name}", a.shape, _mybir.dt.from_np(a.dtype), kind="ExternalInput").ap()
    out = nc.dram_tensor("out_tokens", (BATCH, SEQ, D), _mybir.dt.float32, kind="ExternalOutput").ap()
    build_program(nc, io, out)
    r = _run(nc, [arrays], core_ids=[0])
    return r.results[0]["out_tokens"]
```

```python
import concourse.bass as bass
from concourse import mybir
from contextlib import ExitStack

F32 = mybir.dt.float32
F32R = mybir.dt.float32r
BF16 = mybir.dt.bfloat16
ALU = mybir.AluOpType
ACT = mybir.ActivationFunctionType
AX = mybir.AxisListType

P = 128
BATCH, SEQ, D = 64, 64, 128
NT = BATCH * SEQ // P
GT = 2
NG = NT // GT
GB = GT * 2
H = 16
HD0 = D // H
CHUNK = 32
HD1 = 64
E = 8
HID = 256
FIRST_GROUPS = 4
LN_EPS = 1e-5
RMS_EPS = 1e-6
BIG = 1e30


class Env:
    pass


def there(g, n=NG):
    return not isinstance(g, int) or 0 <= g < n


def split_products(nc, out, lhs, rhs, start, stop):
    pairs = ((lhs[0], rhs[0]), (lhs[0], rhs[1]), (lhs[1], rhs[0]))
    for i, (a, b) in enumerate(pairs):
        last = nc.tensor.matmul(out, a, b, start=start and i == 0, stop=stop and i == 2)
    return last


def group_norm(nc, pool, v, stat6, rstd, shift, parts, done):
    w = v.norm_work
    twice_mean, diff, squares, diff2, rest, var4, half_rstd, product = (w[:, i] for i in range(8))
    nc.gpsimd.tensor_tensor(twice_mean, stat6[:, :, 1], stat6[:, :, 4], ALU.add)
    nc.gpsimd.tensor_tensor(diff, stat6[:, :, 1], stat6[:, :, 4], ALU.subtract)
    nc.gpsimd.tensor_tensor(squares, stat6[:, :, 2], stat6[:, :, 5], ALU.add).then_inc(parts, 1)
    pool.wait_ge(parts, done + 1)
    nc.gpsimd.tensor_tensor(diff2, diff, diff, ALU.mult)
    nc.gpsimd.tensor_scalar(rest, squares, 4.0 / D, 4 * LN_EPS, ALU.mult, ALU.add).then_inc(parts, 1)
    pool.wait_ge(parts, done + 2)
    nc.gpsimd.tensor_tensor(var4, diff2, rest, ALU.add).then_inc(parts, 1)
    pool.wait_ge(parts, done + 3)
    nc.gpsimd.tensor_tensor(half_rstd, var4, v.minus_half[:, 0:GT], ALU.pow).then_inc(parts, 1)
    pool.wait_ge(parts, done + 4)
    nc.gpsimd.tensor_tensor(product, twice_mean, half_rstd, ALU.mult)
    nc.gpsimd.tensor_scalar(rstd, half_rstd, 2.0, None, ALU.mult).then_inc(parts, 1)
    pool.wait_ge(parts, done + 5)
    return nc.gpsimd.tensor_tensor(shift, v.zeros[:, 0:GT], product, ALU.subtract)


NORM_STEPS, RMS_STEPS, TWICE_STEPS = 7, 9, 10


def norm_step(nc, pool, w, i, parts, done, stats, rstd, shift, second=None, rms=None, twice=None):
    twice_mean, diff, squares, rest, var4, var4_eps, half, product = (w.scratch[k] for k in range(8))
    square, mean_square, mean_square_eps, again = (w.scratch[8 + k][second] for k in range(4)) if second else (None,) * 4
    if i:
        pool.wait_ge(parts, done + i)
    if i == 0:
        nc.gpsimd.tensor_tensor(twice_mean, stats(1), stats(4), ALU.add)
        nc.gpsimd.tensor_tensor(diff, stats(1), stats(4), ALU.subtract)
        return nc.gpsimd.tensor_tensor(squares, stats(2), stats(5), ALU.add)
    if i == 1:
        nc.gpsimd.tensor_tensor(product, diff, diff, ALU.mult)
        return nc.gpsimd.tensor_scalar(rest, squares, 4.0 / D, None, ALU.mult)
    if i == 2:
        return nc.gpsimd.tensor_tensor(var4, product, rest, ALU.add)
    if i == 3:
        return nc.gpsimd.tensor_tensor(var4_eps, var4, w.four_eps, ALU.add)
    if i == 4:
        return nc.gpsimd.tensor_tensor(half, var4_eps, w.minus_half, ALU.pow)
    if i == 5:
        if second:
            nc.gpsimd.tensor_tensor(square, half[second], half[second], ALU.mult)
        nc.gpsimd.tensor_tensor(product, twice_mean, half, ALU.mult)
        return nc.gpsimd.tensor_tensor(rstd, half, half, ALU.add)
    if i == 6:
        if second:
            nc.gpsimd.tensor_tensor(mean_square, var4[second], square, ALU.mult)
        return nc.gpsimd.tensor_tensor(shift, w.zero, product, ALU.subtract)
    if i == 7:
        return nc.gpsimd.tensor_tensor(mean_square_eps, mean_square, w.second_eps[second], ALU.add)
    if i == 8:
        return nc.gpsimd.tensor_tensor(again if rms is None else rms, mean_square_eps, w.minus_half[second], ALU.pow)
    if i == 9:
        for scaled in twice:
            last = nc.gpsimd.tensor_tensor(scaled, scaled, again, ALU.mult)
        return last


def norm_constants(nc, w, tile, second_eps):
    w.scratch = [tile[:, k] for k in range(12)]
    w.four_eps, w.minus_half, w.zero, w.second_eps = (tile[:, k] for k in range(12, 16))
    for const, value in ((w.four_eps, 4 * LN_EPS), (w.minus_half, -0.5), (w.zero, 0.0), (w.second_eps, second_eps)):
        last = nc.gpsimd.memset(const, value)
    return last


def setup(nc, v, io):
    with ExitStack() as ctx:
        sem = lambda name: ctx.enter_context(nc.semaphore(name))
        sb = lambda name, shape, dt=F32: ctx.enter_context(nc.sbuf_tensor(name, shape, dt))
        consts_zeroed, consts_built = sem("consts_zeroed"), sem("consts_built")
        head_sums = sem("head_sums")
        head_rows = sb("head_rows", [P, 4, 4])
        with nc.Block() as block:

            @block.sync
            def _(sp):
                first = slice(0, FIRST_GROUPS * GT)
                for tile, tokens in ((v.xa, io["x"]), (v.cx, io["ctx_1024"])):
                    sp.dma_start(tile[:, first], tokens.rearrange("(t c) s d -> (c s) t d", c=2)[:, first]).then_inc(v.first_loaded, 16)

            @block.scalar
            def _(act):
                for name, tile in (("L0_xattn_Wq", v.wq0), ("L0_xattn_Wk", v.wk0), ("L0_xattn_Wv", v.wv0), ("L0_xattn_Wo", v.wo0)):
                    act.dma_start(tile[:], io[name]).then_inc(v.weights0_loaded, 16)
                for name, col in (("L0_xattn_bq", 0), ("L0_xattn_bk", 1), ("L0_xattn_bv", 2)):
                    act.dma_start(v.vec0[:, col:col + 1], io[name].rearrange("(d a) -> d a", a=1)).then_inc(v.weights0_loaded, 16)
                act.dma_start(v.bo_row[:], io["L0_xattn_bo"].rearrange("(a d) -> a d", a=1).broadcast_to([P, D])).then_inc(v.weights0_loaded, 16)
                for name, col in (("g_xattn", 0), ("g_ffn", 2)):
                    act.dma_start(v.gate[:, col:col + 2], io[name].rearrange("(a d) -> a d", a=1).broadcast_to([P, 2])).then_inc(v.weights0_loaded, 16)

            @block.gpsimd
            def _(pool):
                nc.gpsimd.memset(v.ident[:], 0.0).then_inc(consts_zeroed, 1)
                nc.gpsimd.memset(head_rows[:], 1.0).then_inc(consts_zeroed, 1)
                nc.gpsimd.memset(v.minus_half[:], -0.5)
                nc.gpsimd.memset(v.zeros[:], 0.0)
                nc.gpsimd.memset(v.ones_row[:], 1.0).then_inc(consts_zeroed, 1)
                for e in range(E):
                    last = nc.gpsimd.memset(v.first_wins[:, e:e + 1], float(E - e))
                last.then_inc(consts_zeroed, 1)
                pool.wait_ge(consts_zeroed, 4)
                nc.gpsimd.affine_select(out=v.ident[:], in_=v.ident[:], compare_op=ALU.not_equal, fill=1.0, base=0,
                                        pattern=[[-1, P]], channel_multiplier=1).then_inc(consts_built, 1)
                nc.gpsimd.affine_select(out=head_rows[:], in_=head_rows[:], compare_op=ALU.is_ge, fill=0.0, base=0,
                                        pattern=[[-4 * HD0, 4], [-HD0, 4]], channel_multiplier=1).then_inc(consts_built, 1)
                pool.wait_ge(consts_built, 2)
                nc.gpsimd.affine_select(out=head_rows[:], in_=head_rows[:], compare_op=ALU.is_ge, fill=0.0, base=HD0 - 1,
                                        pattern=[[4 * HD0, 4], [HD0, 4]], channel_multiplier=-1).then_inc(consts_built, 1)

            @block.vector
            def _(dve):
                dve.wait_ge(consts_built, 3)
                nc.vector.reduce_sum(v.four_rows[:], head_rows[:].rearrange("p j a -> p a j"), AX.X).then_inc(head_sums, 1)
                nc.vector.reduce_sum(v.head_in_four[:], head_rows[:], AX.X).then_inc(head_sums, 1)
                dve.wait_ge(head_sums, 2)
                nc.vector.tensor_scalar(v.q_mask[:], v.head_in_four[:], float(HD0) ** -0.5, None, ALU.mult).then_inc(head_sums, 1)
                nc.vector.tensor_copy(v.four_cols[:].rearrange("p (j a d) -> p j a d", j=4, a=4),
                                      v.head_in_four[:].unsqueeze(1).unsqueeze(3).broadcast_to([P, 4, 4, HD0])).then_inc(head_sums, 1)


def attention0(nc, v, io):
    with ExitStack() as ctx:
        sem = lambda name: ctx.enter_context(nc.semaphore(name))
        sb = lambda name, shape, dt=F32: ctx.enter_context(nc.sbuf_tensor(name, shape, dt))
        pb = lambda name, shape: ctx.enter_context(nc.psum_tensor(name, shape, F32))

        stat6 = sb("a_stat6", [P, GT, 6])
        rstd = sb("a_rstd", [P, GT])
        shift = sb("a_shift", [P, GT])
        x_hat = sb("a_x_hat", [P, GT, D])
        ctx_tile = sb("a_ctx_tile", [P, GT, D])
        xc = sb("a_xc", [P, 2, GT * P])
        xc_h = sb("a_xc_h", [P, 2, GT * P], F32R)
        xc_l = sb("a_xc_l", [P, 2, GT * P], F32R)
        ctx_rep = sb("a_ctx_rep", [P, 2 * GB, 4, CHUNK])
        q_flat = sb("a_q_flat", [P, 2 * GB, CHUNK])
        q_exp = [sb(f"a_q_exp{i}", [P, 2 * GB, 4, CHUNK]) for i in range(2)]
        k_exp = [sb(f"a_k_exp{i}", [P, 2 * GB, 4, CHUNK]) for i in range(2)]
        v_exp = [sb(f"a_v_exp{i}", [P, 2 * GB, D]) for i in range(2)]
        row_max = sb("a_row_max", [P, 2, 3, 4])
        row_max3 = sb("a_row_max3", [P, 2, 3, 4])
        shifted = sb("a_shifted", [P, 2, 384])
        probs = [sb(f"a_probs{i}", [P, 2, 384]) for i in range(2)]
        sums = sb("a_sums", [P, 2, 3, 4])
        sums_high = sb("a_sums_high", [P, 2, 4])
        recip = [sb(f"a_recip{i}", [P, 2, 3, 4]) for i in range(2)]
        normed = sb("a_normed", [P, 2, 384])
        probs_t = sb("a_probs_t", [P, 2, 384])
        heads_t = sb("a_heads_t", [P, P])
        reorder, wo, wv, vec = sb("a_reorder", [P, P]), sb("a_wo", [P, D]), sb("a_wv", [P, D]), sb("a_vec", [P, 3])

        ps_s = pb("a_ps_s", [P, 2, 512])
        ps_t = pb("a_ps_t", [P, 2, 512])
        ps_aux = pb("a_ps_aux", [P, 512])
        ps_qk = pb("a_ps_qk", [P, 512])
        ps_o = pb("a_ps_o", [P, 512])
        ps_y = pb("a_ps_y", [P, 512])

        stats_ready, rstd_ready, rstd_parts = sem("stats_ready"), sem("rstd_ready"), sem("rstd_parts")
        ctx_repeated = sem("ctx_repeated")
        xhat_ready, ctx_staged = sem("xhat_ready"), sem("ctx_staged")
        inputs_turned, xc_copied, xc_high, xc_low = sem("inputs_turned"), sem("xc_copied"), sem("xc_high"), sem("xc_low")
        qk_done, q_copied, k_ready, q_ready = sem("qk_done"), sem("q_copied"), sem("k_ready"), sem("q_ready")
        v_done, v_ready = sem("v_done"), sem("v_ready")
        scores_done, scores_maxed, max_spread, shifted_ready = sem("scores_done"), sem("scores_maxed"), sem("max_spread"), sem("shifted_ready")
        exp_done, sums_done, sums_added, recip_ready, normed_ready = sem("exp_done"), sem("sums_done"), sem("sums_added"), sem("recip_ready"), sem("normed_ready")
        probs_turned, probs_t_ready = sem("probs_turned"), sem("probs_t_ready")
        heads_done, heads_ready, projected, x1_ready = sem("heads_done"), sem("heads_ready"), sem("projected"), sem("x1_ready")
        base_ready, weights_high, weights_ready = sem("base_ready"), sem("weights_high"), sem("weights_ready")
        reorder_ready, reordered = sem("reorder_ready"), sem("reordered")

        with nc.Block() as block:

            @block.sync
            def _(sp):
                rest = slice(FIRST_GROUPS * GT, NT)
                for tile, tokens in ((v.xa, io["x"]), (v.cx, io["ctx_1024"])):
                    sp.dma_start(tile[:, rest], tokens.rearrange("(t c) s d -> (c s) t d", c=2)[:, rest]).then_inc(v.x_loaded, 16)
                sp.dma_start(v.w_up_raw[:], io["L0_ffn_w_up"].rearrange("e (c p) d -> p (e c) d", p=P)).then_inc(v.weights1_loaded, 16)
                sp.dma_start(v.w_down_raw[:], io["L0_ffn_w_down"].rearrange("e o f -> o e f")).then_inc(v.weights1_loaded, 16)
                sp.dma_start(v.router0_raw[:], io["L0_ffn_w_router"]).then_inc(v.weights1_loaded, 16)
                sp.dma_start(v.vec1[:, 0:1], io["L0_ffn_norm_scale"].rearrange("(d a) -> d a", a=1)).then_inc(v.weights1_loaded, 16)
                sp.dma_start(v.wq1_raw[:], io["L1_xattn_Wq"]).then_inc(v.weights2_loaded, 16)
                sp.dma_start(v.wkv1_raw[:], io["L1_xattn_Wkv"]).then_inc(v.weights2_loaded, 16)
                sp.dma_start(v.wout1_raw[:], io["L1_xattn_Wout"].rearrange("(c p) d -> p c d", p=P)).then_inc(v.weights2_loaded, 16)
                for col, name in enumerate(("L1_xattn_g1", "L1_xattn_b1", "L1_xattn_g2", "L1_xattn_b2")):
                    sp.dma_start(v.vec2[:, col:col + 1], io[name].rearrange("(d a) -> d a", a=1)).then_inc(v.weights2_loaded, 16)
                sp.dma_start(v.expert_raw[:], io["L1_ffn_expert_w"].rearrange("e o d -> o e d")).then_inc(v.weights3_loaded, 16)
                sp.dma_start(v.router1_raw[:], io["L1_ffn_router_w"]).then_inc(v.weights3_loaded, 16)
                sp.dma_start(v.router_b_row[:], io["L1_ffn_router_b"].rearrange("(a e) -> a e", a=1).broadcast_to([P, E])).then_inc(v.weights3_loaded, 16)

            def each_group(eng, step, weights):
                for g in range(-4, 1):
                    if g == FIRST_GROUPS - 4 and eng is not nc.tensor:
                        eng.wait_ge(v.x_loaded, 32)
                    step(g, g % 2)
                    if g == -3:
                        weights()
                with eng.Fori(0, (NG - 6) // 2) as i:
                    step(2 * i + 1, 1)
                    step(2 * i + 2, 0)
                for g in range(NG - 5, NG + 1):
                    step(g, g % 2)

            @block.tensor
            def _(pe):
                def values(g, par, half, bank):
                    pe.wait_ge(ctx_repeated, g + 1)
                    pe.wait_ge(k_ready, g + 1)
                    for i in range(4):
                        c = 4 * half + i
                        last = nc.tensor.matmul(bank[:, i * P:(i + 1) * P], ctx_rep[:, c], wv[:], start=True, stop=True)
                    last.then_inc(v_done, 1)

                def scores(g, par, k):
                    pe.wait_ge(q_ready, g + 1)
                    pe.wait_ge(k_ready, g + 1)
                    if there(g - 1) or k:
                        pe.wait_ge(shifted_ready, 2 * g + k)
                    for b in range(2):
                        c = 2 * (2 * k + b)
                        nc.tensor.matmul(ps_s[:, b, 0:128], q_exp[par][:, c], k_exp[par][:, c], start=True, stop=True)
                        last = nc.tensor.matmul(ps_s[:, b, 128:384], q_exp[par][:, c + 1], k_exp[par][:, c:c + 2], start=True, stop=True)
                    last.then_inc(scores_done, 1)

                def turn_probs(g, k):
                    pe.wait_ge(normed_ready, 2 * g + k + 1)
                    if there(g - 1) or k:
                        pe.wait_ge(probs_t_ready, 2 * g + k)
                    for b in range(2):
                        for n in range(3):
                            cols = slice(n * 128, (n + 1) * 128)
                            last = nc.tensor.transpose(ps_t[:, b, cols], normed[:, b, cols], v.ident[:])
                    last.then_inc(probs_turned, 1)

                def heads(g, par, k):
                    pe.wait_ge(probs_t_ready, 2 * g + k + 1)
                    pe.wait_ge(v_ready, 2 * g + 2)
                    if there(g - 1) or k:
                        pe.wait_ge(heads_ready, 2 * g + k)
                    for b in range(2):
                        c = 2 * (2 * k + b)
                        nc.tensor.matmul(ps_o[:, b * 256:b * 256 + 256], v_exp[par][:, c], probs_t[:, b, 0:256], start=True, stop=False)
                        last = nc.tensor.matmul(ps_o[:, b * 256 + 128:b * 256 + 256], v_exp[par][:, c + 1], probs_t[:, b, 256:384],
                                                start=False, stop=True)
                    last.then_inc(heads_done, 1)

                def project(g, k):
                    pe.wait_ge(heads_ready, 2 * g + k + 1)
                    if there(g - 1) or k:
                        pe.wait_ge(x1_ready, 2 * g + k)
                    nc.tensor.matmul(ps_y[:, 0:D], heads_t[:], wo[:], start=True, stop=True).then_inc(projected, 1)

                def step(g, par):
                    for k in range(2):
                        if there(g):
                            turn_probs(g, k)
                        if k == 0 and there(g + 1):
                            values(g + 1, 1 - par, 0, ps_qk)
                            values(g + 1, 1 - par, 1, ps_aux)
                        if k == 1 and there(g + 2):
                            pe.wait_ge(xc_low, g + 3)
                            pe.wait_ge(xc_high, g + 3)
                            if there(g + 1):
                                pe.wait_ge(v_ready, 2 * (g + 1) + 1)
                            x_pair, c_pair = ((xc_h[:, n], xc_l[:, n]) for n in range(2))
                            split_products(nc, ps_qk[:, 0:256], (v.wq0_h[:], v.wq0_l[:]), x_pair, True, True)
                            split_products(nc, ps_qk[:, 256:512], (v.wk0_h[:], v.wk0_l[:]), c_pair, True, True).then_inc(qk_done, 1)
                        if there(g + 1):
                            scores(g + 1, 1 - par, k)
                        if k == 0 and there(g + 2):
                            pe.wait_ge(xhat_ready, g + 3)
                            pe.wait_ge(ctx_staged, g + 3)
                            if there(g + 1):
                                pe.wait_ge(v_ready, 2 * (g + 1) + 2)
                            for t in range(GT):
                                nc.tensor.transpose(ps_aux[:, t * P:(t + 1) * P], x_hat[:, t], v.ident[:])
                            for t in range(GT):
                                last = nc.tensor.transpose(ps_aux[:, (GT + t) * P:(GT + t + 1) * P], ctx_tile[:, t], v.ident[:])
                            last.then_inc(inputs_turned, 1)
                        if k == 0 and there(g - 1):
                            project(g - 1, 1)
                        if k == 1 and there(g):
                            project(g, 0)
                        if there(g):
                            heads(g, par, k)


                def weights():
                    pe.wait_ge(v.weights0_loaded, 160)
                    pe.wait_ge(reorder_ready, 1)
                    nc.tensor.matmul(ps_y[:, 0:D], reorder[:], v.wo0[:], start=True, stop=True)
                    nc.tensor.matmul(ps_y[:, D:D + 3], reorder[:], v.vec0[:], start=True, stop=True).then_inc(reordered, 1)
                    pe.wait_ge(weights_ready, 2)

                each_group(pe, step, weights)

            @block.scalar
            def _(act):
                def step(g, par):
                    for k in range(2):
                        if there(g):
                            act.wait_ge(probs_turned, 2 * g + k + 1)
                            if there(g - 1) or k:
                                act.wait_ge(heads_done, 2 * g + k)
                            nc.scalar.activation(probs_t[:], ps_t[:, :, 0:384], ACT.Copy).then_inc(probs_t_ready, 1)
                        if k == 1 and there(g + 2):
                            act.wait_ge(qk_done, g + 3)
                            if there(g + 1):
                                act.wait_ge(q_ready, g + 2)
                            nc.scalar.activation(q_flat[:], ps_qk[:, 0:256].rearrange("p (c q) -> p c q", q=CHUNK), ACT.Identity,
                                                 bias=vec[:, 0:1]).then_inc(q_copied, 1)
                            if there(g):
                                act.wait_ge(scores_done, 2 * g + 2)
                            for a in range(4):
                                last = nc.scalar.activation(k_exp[par][:, :, a], ps_qk[:, 256:512].rearrange("p (c q) -> p c q", q=CHUNK),
                                                            ACT.Identity, bias=v.bk_four[:, a:a + 1], scale=v.four_rows[:, a:a + 1])
                            last.then_inc(k_ready, 1)
                        if k == 0 and there(g + 2):
                            act.wait_ge(inputs_turned, g + 3)
                            if there(g + 1):
                                act.wait_ge(xc_low, g + 2)
                            nc.scalar.activation(xc[:], ps_aux[:].rearrange("p (n t) -> p n t", n=2), ACT.Copy).then_inc(xc_copied, 1)
                            act.wait_ge(xc_copied, g + 3)
                            if there(g + 1):
                                act.wait_ge(qk_done, g + 2)
                            nc.scalar.activation(xc_h[:], xc[:], ACT.Copy).then_inc(xc_high, 1)
                            if there(g + 1):
                                act.wait_ge(v_done, 2 * (g + 1) + 2)
                            nc.scalar.activation(ctx_rep[:], xc[:, 1].rearrange("p (c k) -> p c k", k=CHUNK).unsqueeze(2)
                                                 .broadcast_to([P, 2 * GB, 4, CHUNK]), ACT.Copy).then_inc(ctx_repeated, 1)
                        if there(g + 1):
                            act.wait_ge(shifted_ready, 2 * (g + 1) + k + 1)
                            if there(g):
                                act.wait_ge(normed_ready, 2 * g + k + 1)
                            nc.scalar.activation(probs[k][:], shifted[:], ACT.Exp).then_inc(exp_done, 1)
                        if there(g):
                            act.wait_ge(heads_done, 2 * g + k + 1)
                            if there(g - 1) or k:
                                act.wait_ge(projected, 2 * g + k)
                            for j in range(4):
                                rows = slice(32 * j, 32 * (j + 1))
                                last = nc.scalar.activation(heads_t[rows].rearrange("p (c q) -> p c q", c=4),
                                                            ps_o[rows].rearrange("p (c j q) -> p c j q", c=4, j=4)[:, :, j], ACT.Identity, bias=vec[rows, 2:3])
                            last.then_inc(heads_ready, 1)
                        if k == 1 and there(g + 3):
                            if there(g + 2):
                                act.wait_ge(inputs_turned, g + 3)
                            nc.scalar.activation(ctx_tile[:], v.cx[:, bass.ds(GT * (g + 3), GT), :], ACT.Copy).then_inc(ctx_staged, 1)

                act.wait_ge(v.first_loaded, 32)

                def weights():
                    act.wait_ge(v.weights0_loaded, 160)
                    nc.scalar.activation(v.tgate[:], v.gate[:], ACT.Tanh).then_inc(v.gates_ready, 1)
                    act.wait_ge(weights_ready, 2)

                each_group(act, step, weights)

            @block.vector
            def _(dve):
                def step(g, par):
                    for k in range(2):
                        if k == 0 and there(g + 1):
                            masked_values(g, par, 0)
                        n = 2 * g + k + 1
                        summed = there(g) and k == 0 or there(g + 1) and k == 1
                        kk = (k + 1) % 2
                        if summed:
                            dve.wait_ge(exp_done, n + 1)
                            nc.vector.reduce_sum(sums[:].rearrange("p b c a -> p b (c a)"),
                                                 probs[kk][:].rearrange("p b (c q) -> p b c q", q=CHUNK), AX.X).then_inc(sums_done, 1)
                        if k == 0 and there(g + 1):
                            masked_values(g, par, 1)
                        if summed:
                            dve.wait_ge(sums_done, n + 1)
                            nc.vector.tensor_tensor(sums_high[:], sums[:, :, 1], sums[:, :, 2], ALU.add).then_inc(sums_added, 1)
                            nc.vector.reciprocal(recip[kk][:, :, 0], sums[:, :, 0])
                            dve.wait_ge(sums_added, n + 1)
                            nc.vector.reciprocal(recip[kk][:, :, 1:3], sums_high[:].unsqueeze(2).broadcast_to([P, 2, 2, 4])).then_inc(recip_ready, 1)
                        if there(g + 1):
                            m = 2 * (g + 1) + k
                            dve.wait_ge(scores_done, m + 1)
                            nc.vector.reduce_max(row_max[:].rearrange("p b c a -> p b (c a)"),
                                                 ps_s[:, :, 0:384].rearrange("p b (c q) -> p b c q", q=CHUNK), AX.X).then_inc(scores_maxed, 1)
                            dve.wait_ge(scores_maxed, m + 1)
                            nc.vector.tensor_tensor(row_max3[:, :, 1:3], row_max[:, :, 1].unsqueeze(2).broadcast_to([P, 2, 2, 4]),
                                                    row_max[:, :, 2].unsqueeze(2).broadcast_to([P, 2, 2, 4]), ALU.max)
                            nc.vector.tensor_copy(row_max3[:, :, 0], row_max[:, :, 0]).then_inc(max_spread, 1)
                            dve.wait_ge(max_spread, m + 1)
                            if there(g) or k:
                                dve.wait_ge(exp_done, m)
                            nc.vector.tensor_tensor(shifted[:].rearrange("p b (c q) -> p b c q", q=CHUNK),
                                                    ps_s[:, :, 0:384].rearrange("p b (c q) -> p b c q", q=CHUNK),
                                                    row_max3[:].rearrange("p b c a -> p b (c a)").unsqueeze(3).broadcast_to([P, 2, 12, CHUNK]),
                                                    ALU.subtract).then_inc(shifted_ready, 1)
                        if k == 0 and there(g + 2):
                            dve.wait_ge(xc_high, g + 3)
                            nc.vector.tensor_tensor(xc_l[:], xc[:], xc_h[:].bitcast(F32), ALU.subtract).then_inc(xc_low, 1)
                        if k == 0 and there(g - 1):
                            residual(g - 1, 1)
                        if k == 1 and there(g):
                            residual(g, 0)
                        if k == 1 and there(g + 3):
                            dve.wait_ge(rstd_ready, g + 4)
                            if there(g + 2):
                                dve.wait_ge(inputs_turned, g + 3)
                            for t in range(GT):
                                last = nc.vector.tensor_scalar(x_hat[:, t], v.xa[:, GT * (g + 3) + t, :], rstd[:, t:t + 1], shift[:, t:t + 1],
                                                               ALU.mult, ALU.add)
                            last.then_inc(xhat_ready, 1)
                        if k == 1 and there(g + 4):
                            if there(g + 3):
                                dve.wait_ge(rstd_ready, g + 4)
                            for t in range(GT):
                                last = nc.vector.bn_stats(stat6[:, t], v.xa[:, GT * (g + 4) + t, :])
                            last.then_inc(stats_ready, 1)

                def masked_values(g, par, half):
                    dve.wait_ge(v_done, 2 * (g + 1) + half + 1)
                    if half == 0 and there(g - 1):
                        dve.wait_ge(heads_done, 2 * (g - 1) + 2)
                    nc.vector.tensor_tensor(v_exp[1 - par][:, 4 * half:4 * half + 4], (ps_qk, ps_aux)[half][:].rearrange("p (c d) -> p c d", c=4),
                                            v.four_cols[:].unsqueeze(1).broadcast_to([P, 4, D]), ALU.mult).then_inc(v_ready, 1)

                def residual(g, k):
                    n = 2 * g + k
                    dve.wait_ge(projected, n + 1)
                    dve.wait_ge(base_ready, g + 1)
                    if there(g - 1) or k:
                        dve.wait_ge(x1_ready, n)
                    nc.vector.scalar_tensor_tensor(v.xb[:, n, :], ps_y[:, 0:D], v.tgate[:, 0:1], v.xb[:, n, :], ALU.mult, ALU.add).then_inc(x1_ready, 1)
                    if there(g - 1) or k:
                        nc.vector.bn_stats(v.stat6[:, n - 1, :], v.xb[:, n - 1, :])

                dve.wait_ge(v.first_loaded, 32)

                def weights():
                    dve.wait_ge(v.weights0_loaded, 160)
                    by_slot = lambda t: t.rearrange("p (a j d) -> p j a d", a=4, j=4)
                    own = lambda t: t.rearrange("p (j a d) -> p j a d", a=4, j=4)
                    nc.vector.tensor_copy(own(reorder[:]), by_slot(v.ident[:])).then_inc(reorder_ready, 1)
                    nc.vector.tensor_copy(own(v.wq0_h[:]), by_slot(v.wq0[:])).then_inc(weights_high, 1)
                    nc.vector.tensor_copy(own(v.wk0_h[:]), by_slot(v.wk0[:])).then_inc(weights_high, 1)
                    nc.vector.tensor_copy(own(wv[:]), by_slot(v.wv0[:]))
                    dve.wait_ge(v.gates_ready, 1)
                    nc.vector.tensor_scalar(v.gbo[:], v.bo_row[:], v.tgate[:, 0:1], None, ALU.mult)
                    nc.vector.tensor_scalar(v.half_gate[:], v.tgate[:, 2:3], 0.5, None, ALU.mult)
                    dve.wait_ge(weights_high, 2)
                    nc.vector.tensor_tensor(own(v.wq0_l[:]), by_slot(v.wq0[:]), own(v.wq0_h[:]).bitcast(F32), ALU.subtract)
                    nc.vector.tensor_tensor(own(v.wk0_l[:]), by_slot(v.wk0[:]), own(v.wk0_h[:]).bitcast(F32), ALU.subtract).then_inc(weights_ready, 1)
                    dve.wait_ge(reordered, 1)
                    nc.vector.tensor_copy(wo[:], ps_y[:, 0:D])
                    nc.vector.tensor_copy(vec[:], ps_y[:, D:D + 3]).then_inc(weights_high, 1)
                    dve.wait_ge(weights_high, 3)
                    nc.vector.tensor_scalar(v.bk_four[:], v.four_rows[:], vec[:, 1:2], None, ALU.mult).then_inc(weights_ready, 1)

                each_group(dve, step, weights)
                dve.wait_ge(x1_ready, NT)
                nc.vector.bn_stats(v.stat6[:, NT - 1, :], v.xb[:, NT - 1, :])

            @block.gpsimd
            def _(pool):
                def step(g, par):
                    for k in range(2):
                        n = 2 * g + k + 1
                        if there(g) and k == 0 or there(g + 1) and k == 1:
                            kk = (k + 1) % 2
                            pool.wait_ge(recip_ready, n + 1)
                            if there(g):
                                pool.wait_ge(probs_turned, n)
                            nc.gpsimd.tensor_tensor(normed[:].rearrange("p b (c q) -> p (b c) q", q=CHUNK),
                                                    probs[kk][:].rearrange("p b (c q) -> p (b c) q", q=CHUNK),
                                                    recip[kk][:].rearrange("p b c a -> p (b c a)").unsqueeze(2).broadcast_to([P, 24, CHUNK]),
                                                    ALU.mult).then_inc(normed_ready, 1)
                        if k == 1 and there(g + 2):
                            pool.wait_ge(q_copied, g + 3)
                            if there(g):
                                pool.wait_ge(scores_done, 2 * g + 2)
                            nc.gpsimd.tensor_tensor(q_exp[par][:], q_flat[:].unsqueeze(2).broadcast_to([P, 2 * GB, 4, CHUNK]),
                                                    v.q_mask[:].unsqueeze(1).unsqueeze(3).broadcast_to([P, 2 * GB, 4, CHUNK]), ALU.mult
                                                    ).then_inc(q_ready, 1)
                        if k == 0 and there(g):
                            nc.gpsimd.tensor_tensor(v.xb[:, bass.ds(GT * g, GT), :], v.xa[:, bass.ds(GT * g, GT), :],
                                                    v.gbo[:].unsqueeze(1).broadcast_to([P, GT, D]), ALU.add).then_inc(base_ready, 1)

                        if k == 0 and there(g + 3):
                            pool.wait_ge(stats_ready, g + 4)
                            if there(g + 2):
                                pool.wait_ge(xhat_ready, g + 3)
                            group_norm(nc, pool, v, stat6, rstd[:], shift[:], rstd_parts, 5 * (g + 3)).then_inc(rstd_ready, 1)

                pool.wait_ge(v.first_loaded, 32)

                def weights():
                    pool.wait_ge(weights_ready, 1)

                each_group(pool, step, weights)


def mixture0(nc, v):
    with ExitStack() as ctx:
        sb = lambda name, shape, dt=F32: ctx.enter_context(nc.sbuf_tensor(name, shape, dt))
        up_h, up_l = sb("b_up_h", [P, E, 2 * HID], F32R), sb("b_up_l", [P, E, 2 * HID], F32R)
        down_w, router_w = sb("b_down_w", [P, E, 2, D]), sb("b_router_w", [P, E])
        w = Env()
        w.rstd, w.shift, w.rms = sb("b_rstd", [P, NT]), sb("b_shift", [P, NT]), sb("b_rms", [P, NT])
        w.normed, w.norm_parts = ctx.enter_context(nc.semaphore("normed")), ctx.enter_context(nc.semaphore("norm_parts"))
        w.scratch_tile = sb("b_norm_scratch", [P, 16, GT])

        def norm_part(pool, c, i):
            tiles = slice(GT * c, GT * (c + 1)) if isinstance(c, int) else bass.ds(GT * c, GT)
            last = norm_step(nc, pool, w, i, w.norm_parts, (RMS_STEPS - 1) * c, lambda k: v.stat6[:, tiles, k], w.rstd[:, tiles], w.shift[:, tiles],
                             second=(slice(None),), rms=w.rms[:, tiles])
            last.then_inc(w.normed if i == RMS_STEPS - 1 else w.norm_parts, 1)

        w.norm_part = norm_part
        mixture0_weights(nc, v, w, up_h, up_l, down_w, router_w)
        mixture0_main(nc, v, w, up_h, up_l, down_w, router_w)


def mixture0_weights(nc, v, w, up_h, up_l, down_w, router_w):
    with ExitStack() as ctx:
        sem = lambda name: ctx.enter_context(nc.semaphore(name))
        banks = [ctx.enter_context(nc.psum_tensor(f"bw_ps{i}", [P, 512], F32)) for i in range(4)]
        turned, high_done, bank_free = sem("turned"), sem("high_done"), sem("bank_free")
        UP, DOWN = E, E // 2
        zeroed = sem("norm_constants")
        with nc.Block() as block:

            @block.tensor
            def _(pe):
                pe.wait_ge(v.weights1_loaded, 64)
                for r in range(UP + DOWN + 1):
                    if r >= 4:
                        pe.wait_ge(bank_free, r - 3)
                    bank = banks[r % 4]
                    if r < UP:
                        parts = [v.w_up_raw[:, 4 * r + i] for i in range(4)]
                    elif r < UP + DOWN:
                        parts = [v.w_down_raw[:, 2 * (r - UP) + i // 2, (i % 2) * P:(i % 2 + 1) * P] for i in range(4)]
                    else:
                        nc.tensor.transpose(bank[:, 0:E], v.router0_raw[:], v.ident[0:E, 0:E]).then_inc(turned, 1)
                        break
                    for i, part in enumerate(parts):
                        last = nc.tensor.transpose(bank[:, i * P:(i + 1) * P], part, v.ident[:])
                    last.then_inc(turned, 1)

            @block.scalar
            def _(act):
                for r in range(UP + DOWN + 1):
                    act.wait_ge(turned, r + 1)
                    bank = banks[r % 4]
                    if r < UP:
                        nc.scalar.activation(up_h[:, r], bank[:], ACT.Copy).then_inc(high_done, 1)
                    elif r < UP + DOWN:
                        e = 2 * (r - UP)
                        nc.scalar.activation(down_w[:, e:e + 2], bank[:].rearrange("p (e c d) -> p e c d", e=2, c=2), ACT.Copy).then_inc(bank_free, 1)
                    else:
                        nc.scalar.activation(router_w[:], bank[:, 0:E], ACT.Copy)
                    if r == UP - 1:
                        act.wait_ge(bank_free, UP)

            @block.vector
            def _(dve):
                for r in range(UP):
                    dve.wait_ge(high_done, r + 1)
                    nc.vector.tensor_tensor(up_l[:, r], banks[r % 4][:], up_h[:, r].bitcast(F32), ALU.subtract).then_inc(bank_free, 1)

            @block.gpsimd
            def _(pool):
                norm_constants(nc, w, w.scratch_tile, RMS_EPS).then_inc(zeroed, 1)
                pool.wait_ge(zeroed, 1)
                for i in range(RMS_STEPS):
                    w.norm_part(pool, 0, i)


def mixture0_main(nc, v, w, up_h, up_l, down_w, router_w):
    C = GT * P
    with ExitStack() as ctx:
        sem = lambda name: ctx.enter_context(nc.semaphore(name))
        sb = lambda name, shape, dt=F32: ctx.enter_context(nc.sbuf_tensor(name, shape, dt))
        pb = lambda name, shape: ctx.enter_context(nc.psum_tensor(name, shape, F32))
        lat, normed = sb("b_lat", [P, GT, D]), sb("b_normed", [P, GT, D])
        xn = sb("b_xn", [P, C])
        xn_h, xn_l = sb("b_xn_h", [P, NG, C], F32R), sb("b_xn_l", [P, NG, C], F32R)
        weight = sb("b_weight", [P, NT, E])
        scores = sb("b_scores", [P, GT, E])
        best = [sb(f"b_best{i}", [P, GT, 1]) for i in range(2)]
        equal, ranked, chosen = sb("b_equal", [P, GT, E]), sb("b_ranked", [P, GT, E]), [sb(f"b_chosen{i}", [P, GT, E]) for i in range(2)]
        first = sb("b_first", [P, GT, 1])
        gap, ratio, one_plus = sb("b_gap", [P, GT, 1]), sb("b_ratio", [P, GT, 1]), sb("b_one_plus", [P, GT, 1])
        w_best = [sb(f"b_w_best{i}", [P, GT, 1]) for i in range(2)]
        parts = [sb(f"b_part{i}", [P, GT, E]) for i in range(2)]
        tanh_t = [sb(f"b_tanh{i}", [P, 2, C]) for i in range(2)]
        gated = [sb(f"b_gated{i}", [P, 2, C]) for i in range(2)]
        u_copy = [sb(f"b_u_copy{i}", [P, C]) for i in range(2)]
        hidden = [sb(f"b_hidden{i}", [P, 2, C]) for i in range(2)]
        ps_u = [pb(f"b_ps_u{i}", [P, 2, C]) for i in range(2)]
        ps_g = [pb(f"b_ps_g{i}", [P, 2, C]) for i in range(2)]
        ps_d = [pb(f"b_ps_d{i}", [P, 512]) for i in range(2)]
        ps_x, ps_r = pb("b_ps_x", [P, 512]), pb("b_ps_r", [P, 512])

        lat_ready, normed_ready, base_ready = sem("lat_ready"), sem("normed_ready"), sem("base_ready")
        x_turned, xn_ready, xn_high, xn_low = sem("x_turned"), sem("xn_ready"), sem("xn_high"), sem("xn_low")
        routed, routing, ratio_ready, weight_ready, weight_parts = sem("routed"), sem("routing"), sem("ratio_ready"), sem("weight_ready"), sem("weight_parts")
        gate_done, up_done, tanh_done, u_copied, gated_done = sem("gate_done"), sem("up_done"), sem("tanh_done"), sem("u_copied"), sem("gated_done")
        hidden0_done, hidden1_done, down_done, added = sem("hidden0_done"), sem("hidden1_done"), sem("down_done"), sem("added")
        ROUTE = 16

        with nc.Block() as block:

            def each_chunk(eng, step):
                for c in range(-2, 1):
                    step(c)
                with eng.Fori(1, NG - 2) as c:
                    step(c)
                for c in range(NG - 2, NG):
                    step(c)

            @block.tensor
            def _(pe):
                def up(c, e, bank, at):
                    pair = (xn_h[:, c, :], xn_l[:, c, :])
                    for f in range(2):
                        cols = slice(at + f * P, at + (f + 1) * P)
                        last = split_products(nc, bank[:, f], (up_h[:, e, cols], up_l[:, e, cols]), pair, True, True)
                    return last

                def gates(c, e):
                    n, par = E * c + e, e % 2
                    pe.wait_ge(xn_low, c + 1)
                    pe.wait_ge(xn_high, c + 1)
                    if there(c - 1) or e >= 2:
                        pe.wait_ge(gated_done, n - 1)
                    up(c, e, ps_g[par], HID).then_inc(gate_done, 1)

                def values(c, e):
                    n, par = E * c + e, e % 2
                    if there(c - 1) or e >= 2:
                        pe.wait_ge(hidden0_done, n - 1)
                    up(c, e, ps_u[par], 0).then_inc(up_done, 1)

                def down(c, e):
                    n, par = E * c + e, e % 2
                    pe.wait_ge(hidden0_done, n + 1)
                    pe.wait_ge(hidden1_done, n + 1)
                    if there(c - 1) or e >= 2:
                        pe.wait_ge(added, n - 1)
                    for t in range(GT):
                        for f in range(2):
                            last = nc.tensor.matmul(ps_d[par][:, t * P:(t + 1) * P], hidden[par][:, f, t * P:(t + 1) * P], down_w[:, e, f],
                                                    start=f == 0, stop=f == 1)
                    last.then_inc(down_done, 1)

                def step(c):
                    for e in range(E):
                        ahead = (c, e + 2) if e + 2 < E else (c + 1, e + 2 - E)
                        if there(ahead[0]):
                            gates(*ahead)
                        if there(c):
                            down(c, e)
                        if e == 0 and there(c + 1):
                            pe.wait_ge(normed_ready, c + 2)
                            for t in range(GT):
                                last = nc.tensor.transpose(ps_x[:, t * P:(t + 1) * P], normed[:, t], v.ident[:])
                            last.then_inc(x_turned, 1)
                        if e == 1 and there(c + 1):
                            pe.wait_ge(xn_ready, c + 2)
                            for t in range(GT):
                                last = nc.tensor.matmul(ps_r[:, t * E:(t + 1) * E], xn[:, t * P:(t + 1) * P], router_w[:], start=True, stop=True)
                            last.then_inc(routed, 1)
                        if there(ahead[0]):
                            values(*ahead)

                each_chunk(pe, step)

            @block.scalar
            def _(act):
                def unit(c, e, between):
                    n, par = E * c + e, e % 2
                    if there(c):
                        act.wait_ge(gate_done, n + 1)
                        if there(c - 1) or e >= 2:
                            act.wait_ge(gated_done, n - 1)
                        nc.scalar.activation(tanh_t[par][:], ps_g[par][:], ACT.Tanh, scale=0.5).then_inc(tanh_done, 1)
                    between()
                    if there(c):
                        if there(c - 1) or e >= 2:
                            act.wait_ge(hidden1_done, n - 1)
                        act.wait_ge(up_done, n + 1)
                        nc.scalar.activation(u_copy[par][:], ps_u[par][:, 1], ACT.Copy).then_inc(u_copied, 1)

                def prepare(c, e):
                    if e == 1 and there(c + 1):
                        act.wait_ge(x_turned, c + 2)
                        if there(c):
                            act.wait_ge(routed, c + 1)
                            act.wait_ge(xn_low, c + 1)
                        nc.scalar.activation(xn[:], ps_x[:, 0:C], ACT.Copy, scale=v.vec1[:, 0:1]).then_inc(xn_ready, 1)
                        act.wait_ge(xn_ready, c + 2)
                        nc.scalar.activation(xn_h[:, c + 1, :], xn[:], ACT.Copy).then_inc(xn_high, 1)
                    if e == 6 and there(c + 2):
                        act.wait_ge(w.normed, c + 3)
                        if there(c + 1):
                            act.wait_ge(base_ready, c + 2)
                        for t in range(GT):
                            n = GT * (c + 2) + t
                            last = nc.scalar.activation(lat[:, t], v.xb[:, n, :], ACT.Identity, scale=w.rstd[:, bass.ds(n, 1)], bias=w.shift[:, bass.ds(n, 1)])
                        last.then_inc(lat_ready, 1)
                    if e == 7 and there(c + 2):
                        act.wait_ge(lat_ready, c + 3)
                        if there(c + 1):
                            act.wait_ge(x_turned, c + 2)
                        for t in range(GT):
                            last = nc.scalar.activation(normed[:, t], lat[:, t], ACT.Copy, scale=w.rms[:, bass.ds(GT * (c + 2) + t, 1)])
                        last.then_inc(normed_ready, 1)

                def step(c):
                    for e in range(E):
                        unit(*((c, e + 1) if e + 1 < E else (c + 1, 0)), lambda: prepare(c, e))
                        if e == 5 and there(c + 1):
                            act.wait_ge(routing, ROUTE * (c + 1) + 9)
                            nc.scalar.activation(ratio[:], gap[:], ACT.Exp).then_inc(ratio_ready, 1)

                each_chunk(act, step)

            @block.vector
            def _(dve):
                def unit(c, e, between):
                    n, par = E * c + e, e % 2
                    if there(c):
                        dve.wait_ge(tanh_done, n + 1)
                        if there(c - 1) or e >= 2:
                            dve.wait_ge(hidden1_done, n - 1)
                        nc.vector.scalar_tensor_tensor(gated[par][:], tanh_t[par][:], 1.0, ps_g[par][:], ALU.add, ALU.mult).then_inc(gated_done, 1)
                    between()
                    if there(c):
                        dve.wait_ge(u_copied, n + 1)
                        dve.wait_ge(gated_done, n + 1)
                        if there(c - 1) or e >= 2:
                            dve.wait_ge(down_done, n - 1)
                        nc.vector.tensor_tensor(hidden[par][:, 0], gated[par][:, 0], ps_u[par][:, 0], ALU.mult).then_inc(hidden0_done, 1)

                def add(c, e):
                    n, par = E * c + e, e % 2
                    dve.wait_ge(down_done, n + 1)
                    if e == 0:
                        dve.wait_ge(weight_ready, c + 1)
                        dve.wait_ge(base_ready, c + 1)
                    else:
                        dve.wait_ge(added, n)
                    for t in range(GT):
                        tile = v.xa[:, GT * c + t, :]
                        last = nc.vector.scalar_tensor_tensor(tile, ps_d[par][:, t * P:(t + 1) * P], weight[:, GT * c + t, e:e + 1], tile,
                                                              ALU.mult, ALU.add)
                    last.then_inc(added, 1)

                def pick(k, i):
                    if i == 0:
                        return nc.vector.reduce_max(best[k][:, :, 0], scores[:], AX.X)
                    if i == 1:
                        return nc.vector.tensor_tensor(equal[:], scores[:], best[k][:].broadcast_to([P, GT, E]), ALU.is_equal)
                    if i == 2:
                        return nc.vector.tensor_tensor(ranked[:], equal[:], v.first_wins[:].unsqueeze(1).broadcast_to([P, GT, E]), ALU.mult)
                    if i == 3:
                        return nc.vector.reduce_max(first[:, :, 0], ranked[:], AX.X)
                    return nc.vector.tensor_tensor(chosen[k][:], ranked[:], first[:].broadcast_to([P, GT, E]), ALU.is_equal)

                def route(c, i):
                    if not there(c) or not 0 <= i < ROUTE:
                        return
                    if i == 0:
                        dve.wait_ge(routed, c + 1)
                        if there(c - 1):
                            dve.wait_ge(weight_ready, c)
                        last = nc.vector.tensor_copy(scores[:], ps_r[:, 0:GT * E].rearrange("p (t e) -> p t e", t=GT))
                    else:
                        dve.wait_ge(routing, ROUTE * c + i)
                    if 1 <= i <= 5:
                        last = pick(0, i - 1)
                    if i == 6:
                        last = nc.vector.scalar_tensor_tensor(scores[:], chosen[0][:], -BIG, scores[:], ALU.mult, ALU.add)
                    if i == 7:
                        last = pick(1, 0)
                    if i == 8:
                        last = nc.vector.tensor_tensor(gap[:], best[1][:], best[0][:], ALU.subtract)
                    if 9 <= i <= 12:
                        last = pick(1, i - 8)
                    if i == 13:
                        dve.wait_ge(ratio_ready, c + 1)
                        last = nc.vector.tensor_scalar(one_plus[:], ratio[:], 1.0, None, ALU.add)
                    if i == 14:
                        last = nc.vector.reciprocal(one_plus[:], one_plus[:])
                    if i == 15:
                        last = nc.vector.tensor_scalar(w_best[0][:], one_plus[:], v.half_gate[:, 0:1], None, ALU.mult)
                    last.then_inc(routing, 1)

                def step(c):
                    for e in range(E):
                        at = 3 * (e - 2) + (1 if e > 4 else 0)
                        unit(*((c, e + 1) if e + 1 < E else (c + 1, 0)), lambda: route(c + 1, at))
                        route(c + 1, at + 1)
                        if there(c):
                            add(c, e)
                        route(c + 1, at + 2)
                        if e == 4:
                            route(c + 1, at + 3)
                        if e == 3 and there(c) and there(c - 1):
                            for t in range(GT):
                                nc.vector.bn_stats(v.stat6[:, GT * (c - 1) + t, :], v.xa[:, GT * (c - 1) + t, :])
                        if e == 2 and there(c):
                            for t in range(GT):
                                nc.vector.bn_stats(v.ctx_stat6[:, GT * c + t, :], v.cx[:, GT * c + t, :])
                        if e == 0 and there(c + 1):
                            dve.wait_ge(lat_ready, c + 2)
                            nc.vector.scalar_tensor_tensor(v.xa[:, bass.ds(GT * (c + 1), GT), :], lat[:], v.tgate[:, 2:3],
                                                           v.xb[:, bass.ds(GT * (c + 1), GT), :], ALU.mult, ALU.add).then_inc(base_ready, 1)
                        if e == 1 and there(c + 1):
                            dve.wait_ge(xn_high, c + 2)
                            nc.vector.tensor_tensor(xn_l[:, c + 1, :], xn[:], xn_h[:, c + 1, :].bitcast(F32), ALU.subtract).then_inc(xn_low, 1)

                each_chunk(dve, step)
                dve.wait_ge(added, E * NG)
                for n in range(NT - GT, NT):
                    nc.vector.bn_stats(v.stat6[:, n, :], v.xa[:, n, :])

            @block.gpsimd
            def _(pool):
                def unit(c, e):
                    n, par = E * c + e, e % 2
                    pool.wait_ge(gated_done, n + 1)
                    pool.wait_ge(u_copied, n + 1)
                    if there(c - 1) or e >= 2:
                        pool.wait_ge(down_done, n - 1)
                    nc.gpsimd.tensor_tensor(hidden[par][:, 1], gated[par][:, 1], u_copy[par][:], ALU.mult).then_inc(hidden1_done, 1)

                def step(c):
                    for e in range(E):
                        if there(c):
                            unit(c, e)
                        if there(c + 2) and not (isinstance(c, int) and c == -2):
                            for i in {0: (0, 1), 1: (2, 3), 2: (4,), 3: (5, 6), 4: (7,), 5: (8,)}.get(e, ()):
                                w.norm_part(pool, c + 2, i)
                        if e == 7 and there(c + 1):
                            at = 2 * (c + 1)
                            pool.wait_ge(routing, ROUTE * (c + 2))
                            nc.gpsimd.tensor_tensor(w_best[1][:], w_best[0][:], ratio[:], ALU.mult).then_inc(weight_parts, 1)
                            nc.gpsimd.tensor_tensor(parts[0][:], chosen[0][:], w_best[0][:].broadcast_to([P, GT, E]), ALU.mult)
                            pool.wait_ge(weight_parts, at + 1)
                            nc.gpsimd.tensor_tensor(parts[1][:], chosen[1][:], w_best[1][:].broadcast_to([P, GT, E]), ALU.mult).then_inc(weight_parts, 1)
                            pool.wait_ge(weight_parts, at + 2)
                            nc.gpsimd.tensor_tensor(weight[:, bass.ds(GT * (c + 1), GT), :], parts[0][:], parts[1][:], ALU.add).then_inc(weight_ready, 1)

                each_chunk(pool, step)


def attention1(nc, v, io, last_stage):
    with ExitStack() as ctx:
        sb = lambda name, shape, dt=F32: ctx.enter_context(nc.sbuf_tensor(name, shape, dt))
        w = Env()
        w.m_h, w.m_l = sb("c_m_h", [P, H, D], F32R), sb("c_m_l", [P, H, D], F32R)
        w.n_h, w.n_l = sb("c_n_h", [P, H, D], F32R), sb("c_n_l", [P, H, D], F32R)
        w.rstd, w.shift = sb("c_rstd", [P, 2, NT]), sb("c_shift", [P, 2, NT])
        w.normed, w.norm_parts = ctx.enter_context(nc.semaphore("normed_rows")), ctx.enter_context(nc.semaphore("norm_parts"))
        w.scratch_tile = sb("c_norm_scratch", [P, 16, 2, GT])

        def norm_part(pool, g, i):
            tiles = slice(GT * g, GT * (g + 1)) if isinstance(g, int) else bass.ds(GT * g, GT)
            last = norm_step(nc, pool, w, i, w.norm_parts, (TWICE_STEPS - 1) * g, lambda k: v.stats[:, :, tiles, k],
                             w.rstd[:, :, tiles], w.shift[:, :, tiles], second=(slice(None), 1), twice=(w.rstd[:, 1, tiles], w.shift[:, 1, tiles]))
            last.then_inc(w.normed if i == TWICE_STEPS - 1 else w.norm_parts, 1)

        w.norm_part = norm_part
        w.mask_bias = sb("c_mask_bias", [1, BATCH, SEQ], BF16)
        attention1_weights(nc, v, w, io, last_stage)
        attention1_main(nc, v, w)


def attention1_weights(nc, v, w, io, last_stage):
    with ExitStack() as ctx:
        sem = lambda name: ctx.enter_context(nc.semaphore(name))
        sb = lambda name, shape, dt=F32: ctx.enter_context(nc.sbuf_tensor(name, shape, dt))
        banks = [ctx.enter_context(nc.psum_tensor(f"cw_ps{i}", [P, 512], F32)) for i in range(4)]
        turned_w = sb("cw_turned", [P, 3, H // 2, D])
        turned, copied = sem("turned"), sem("copied")
        product_done, high_done, low_done = sem("product_done"), sem("high_done"), sem("low_done")
        zeroed, bias_steps = sem("norm_constants"), sem("bias_steps")
        bias_high, minus_low = sb("cw_bias_high", [2, E * D], F32R), sb("cw_minus_low", [2, 1])
        EXPERTS = 2
        TURNS, PRODUCTS = 6, 2 * H // 4
        first_head = lambda r: 8 * (r % 4 // 2) + r % 2
        heads_of = lambda r: slice(first_head(r), first_head(r) + 7, 2)
        mask_u8, mask_loaded = sb("cw_mask_u8", [1, BATCH * SEQ], mybir.dt.uint8), sem("mask_loaded")
        expert_b_rows, bias_loaded = sb("cw_expert_b_rows", [2, E * D]), sem("bias_loaded")
        with nc.Block() as block:

            @block.sync
            def _(sp):
                sp.dma_start(mask_u8[:], io["mask_BxS2_bk0"].rearrange("(a b) s -> a (b s)", a=1)).then_inc(mask_loaded, 16)
                sp.dma_start(expert_b_rows[:], io["L1_ffn_expert_b"].rearrange("(a e) d -> a (e d)", a=1).broadcast_to([2, E * D])).then_inc(bias_loaded, 16)

            @block.tensor
            def _(pe):
                pe.wait_ge(v.weights2_loaded, 112)
                for r in range(TURNS):
                    if r >= 4:
                        pe.wait_ge(copied, r - 3)
                    for i in range(4):
                        pair = 4 * (r % 2) + i
                        source = (v.wq1_raw, v.wkv1_raw, v.wkv1_raw)[r // 2]
                        at = pair * P + (H * HD1 if r // 2 == 2 else 0)
                        last = nc.tensor.transpose(banks[r % 4][:, i * P:(i + 1) * P], source[:, at:at + P], v.ident[:])
                    last.then_inc(turned, 1)
                pe.wait_ge(copied, TURNS)
                for r in range(PRODUCTS):
                    if r >= 4:
                        pe.wait_ge(low_done, r - 3)
                    for i in range(4):
                        h = first_head(r) + 2 * i
                        rows = slice(HD1 * (h % 2), HD1 * (h % 2 + 1))
                        left, right = ((turned_w[rows, 0, h // 2], turned_w[rows, 1, h // 2]) if r < 4
                                       else (turned_w[rows, 2, h // 2], v.wout1_raw[rows, h // 2]))
                        last = nc.tensor.matmul(banks[r % 4][:, i * P:(i + 1) * P], left, right, start=True, stop=True)
                    last.then_inc(product_done, 1)
                pe.wait_ge(v.weights3_loaded, 48)
                for r in range(PRODUCTS, PRODUCTS + EXPERTS):
                    pe.wait_ge(low_done, r - 3)
                    for i in range(4):
                        last = nc.tensor.transpose(banks[r % 4][:, i * P:(i + 1) * P], v.expert_raw[:, 4 * (r - PRODUCTS) + i], v.ident[:])
                    last.then_inc(product_done, 1)
                pe.wait_ge(low_done, PRODUCTS - 1)
                nc.tensor.transpose(banks[2][:, 0:E], v.router1_raw[:], v.ident[0:E, 0:E]).then_inc(product_done, 1)

            @block.scalar
            def _(act):
                for r in range(TURNS):
                    act.wait_ge(turned, r + 1)
                    nc.scalar.activation(turned_w[:, r // 2, 4 * (r % 2):4 * (r % 2) + 4], banks[r % 4][:].rearrange("p (i d) -> p i d", i=4),
                                         ACT.Copy).then_inc(copied, 1)
                for r in range(PRODUCTS):
                    act.wait_ge(product_done, r + 1)
                    high = (w.m_h, w.n_h)[r // 4][:, heads_of(r)]
                    nc.scalar.activation(high, banks[r % 4][:].rearrange("p (i d) -> p i d", i=4), ACT.Copy,
                                         scale=float(HD1) ** -0.5 if r < 4 else 1.0).then_inc(high_done, 1)
                for r in range(PRODUCTS, PRODUCTS + EXPERTS):
                    act.wait_ge(product_done, r + 1)
                    at = (r - PRODUCTS) * 512
                    nc.scalar.activation(last_stage.e_h[:, at:at + 512], banks[r % 4][:], ACT.Copy).then_inc(high_done, 1)
                act.wait_ge(product_done, PRODUCTS + EXPERTS + 1)
                nc.scalar.activation(last_stage.router[:], banks[2][:, 0:E], ACT.Copy)

            @block.vector
            def _(dve):
                dve.wait_ge(mask_loaded, 16)
                nc.vector.tensor_scalar(w.mask_bias[:], mask_u8[:].rearrange("a (b s) -> a b s", b=BATCH), -1.0, 3e38, ALU.add, ALU.mult)
                dve.wait_ge(bias_loaded, 16)
                dve.wait_ge(v.weights3_loaded, 48)
                nc.vector.tensor_scalar(last_stage.ones_pair[:], v.ident[0:2, :], 0.0, 1.0, ALU.mult, ALU.add)
                nc.vector.tensor_scalar(minus_low[:], v.ident[0:2, 1:2], -1.0, None, ALU.mult)
                nc.vector.tensor_copy(bias_high[:], expert_b_rows[:]).then_inc(bias_steps, 1)
                dve.wait_ge(bias_steps, 1)
                nc.vector.scalar_tensor_tensor(last_stage.bias_pair[:], bias_high[:].bitcast(F32), minus_low[:, 0:1], expert_b_rows[:], ALU.mult, ALU.add)
                for r in range(PRODUCTS):
                    dve.wait_ge(high_done, r + 1)
                    high, low = ((w.m_h, w.m_l), (w.n_h, w.n_l))[r // 4]
                    nc.vector.scalar_tensor_tensor(low[:, heads_of(r)], banks[r % 4][:].rearrange("p (i d) -> p i d", i=4),
                                                   float(HD1) ** -0.5 if r < 4 else 1.0, high[:, heads_of(r)].bitcast(F32),
                                                   ALU.mult, ALU.subtract).then_inc(low_done, 1)
                for r in range(PRODUCTS, PRODUCTS + EXPERTS):
                    dve.wait_ge(high_done, r + 1)
                    cols = slice((r - PRODUCTS) * 512, (r - PRODUCTS + 1) * 512)
                    nc.vector.tensor_tensor(last_stage.e_l[:, cols], banks[r % 4][:], last_stage.e_h[:, cols].bitcast(F32), ALU.subtract)

            @block.gpsimd
            def _(pool):
                norm_constants(nc, w, w.scratch_tile, LN_EPS).then_inc(zeroed, 1)
                pool.wait_ge(zeroed, 1)
                for i in range(TWICE_STEPS):
                    w.norm_part(pool, 0, i)


def attention1_main(nc, v, w):
    C = GT * P
    U = 2 * GB
    HH = H // 2
    KEYS = 2 * SEQ
    with ExitStack() as ctx:
        sem = lambda name: ctx.enter_context(nc.semaphore(name))
        sb = lambda name, shape, dt=F32: ctx.enter_context(nc.sbuf_tensor(name, shape, dt))
        pb = lambda name, shape: ctx.enter_context(nc.psum_tensor(name, shape, F32))
        hat = sb("c_hat", [P, 2, GT, D])
        kv_t = [sb(f"c_kv_t{i}", [P, GB, KEYS]) for i in range(2)]
        kv_h = [sb(f"c_kv_h{i}", [P, GB, D], F32R) for i in range(2)]
        kv_l = [sb(f"c_kv_l{i}", [P, GB, D], F32R) for i in range(2)]
        lat_h = [sb(f"c_lat_h{i}", [P, GB, SEQ], F32R) for i in range(2)]
        lat_l = [sb(f"c_lat_l{i}", [P, GB, SEQ], F32R) for i in range(2)]
        q_t = sb("c_q_t", [P, GB, H, SEQ])
        neg_max, sums, recip = ([sb(f"c_{name}{i}", [P, 4]) for i in range(2)] for name in ("neg_max", "sums", "recip"))
        probs = [sb(f"c_probs{i}", [P, 4, KEYS]) for i in range(2)]
        normed = [sb(f"c_normed{i}", [P, 4, KEYS]) for i in range(2)]
        probs_h, probs_l = sb("c_probs_h", [P, 512], F32R), sb("c_probs_l", [P, 512], F32R)
        y_h, y_l = sb("c_y_h", [P, H, C], F32R), sb("c_y_l", [P, H, C], F32R)
        out_t = sb("c_out_t", [P, C])

        ps_s = [pb(f"c_ps_s{i}", [P, 4, KEYS]) for i in range(2)]
        ps_q = [pb(f"c_ps_q{i}", [P, 2, C]) for i in range(2)]
        ps_t, ps_y, ps_o, ps_x = (pb(f"c_ps_{n}", [P, 512]) for n in "tyox")

        hat_ready, hat_turned, kv_t_ready, lat_high, lat_low = (sem(n) for n in ("hat_ready", "hat_turned", "kv_t_ready", "lat_high", "lat_low"))
        kv_turned, kv_high, kv_low = sem("kv_turned"), sem("kv_high"), sem("kv_low")
        q_done, q_ready, scores_done, max_ready, exp_done, recip_ready, normed_ready = (
            sem(n) for n in ("q_done", "q_ready", "scores_done", "max_ready", "exp_done", "recip_ready", "normed_ready"))
        probs_turned, probs_high, probs_low = sem("probs_turned"), sem("probs_high"), sem("probs_low")
        y_done, y_high, y_low = sem("y_done"), sem("y_high"), sem("y_low")
        x3_stats, x3_constants = sem("x3_stats"), sem("x3_norm_constants")
        out_done, out_copied, out_turned, x3_ready = sem("out_done"), sem("out_copied"), sem("out_turned"), sem("x3_ready")

        with nc.Block() as block:

            def each_group(eng, step):
                for g in range(-2, 4):
                    step(g, g % 2)
                with eng.Fori(2, NG // 2 - 1) as i:
                    step(2 * i, 0)
                    step(2 * i + 1, 1)
                for g in range(NG - 2, NG + 1):
                    step(g, g % 2)

            def ahead(g, u, k):
                return (g, u + k, 0) if u + k < U else (g + 1, u + k - U, 1)

            def q_heads(g, u):
                return (g, 7, 0) if u == 0 else (g + 1, u - 1, 1)

            def out_heads(g, u):
                return (g - 1, 3 + u) if u < 5 else (g, u - 5)

            def before(g, u):
                return (g, u - 1, 0) if u else (g - 1, U - 1, 1)

            @block.tensor
            def _(pe):
                def step(g, par):
                    for u in range(U):
                        n = U * g + u
                        gs, us, flip = ahead(g, u, 2)
                        if there(gs):
                            b, half = us % GB, us // GB
                            pe.wait_ge(q_ready, 8 * gs + 4 * (half + 1))
                            pe.wait_ge(kv_t_ready, 2 * gs + 2)
                            if there(g):
                                pe.wait_ge(exp_done, n + 1)
                            bank = ps_s[us % 2]
                            for i in range(4):
                                h = HH * half + 2 * i
                                nc.tensor.matmul(bank[:, i], q_t[:, b, h:h + 2].rearrange("p h s -> p (h s)"), kv_t[par ^ flip][:, b],
                                                 start=i == 0, stop=False, skip_group_check=True)
                            nc.tensor.matmul(bank[:, :, 0:SEQ], v.ones_row[:], w.mask_bias[:, GB * gs + b, :].unsqueeze(1).broadcast_to([1, 4, SEQ]),
                                             start=False, stop=True, skip_group_check=True).then_inc(scores_done, 1)
                        gb, ub, flip = before(g, u)
                        if there(gb):
                            pe.wait_ge(probs_low, n)
                            pe.wait_ge(kv_low, gb + 1)
                            if there(gb - 1) or ub:
                                pe.wait_ge(y_low, n - 1)
                            b, own = ub % GB, par ^ flip
                            split_products(nc, ps_y[:], (kv_h[own][:, b], kv_l[own][:, b]), (probs_h[:], probs_l[:]), True, True).then_inc(y_done, 1)
                        if there(g):
                            pe.wait_ge(normed_ready, n + 1)
                            if there(g - 1) or u:
                                pe.wait_ge(probs_low, n)
                            for i in range(4):
                                last = nc.tensor.transpose(ps_t[:, i * P:(i + 1) * P], normed[u % 2][:, i], v.ident[:])
                            last.then_inc(probs_turned, 1)
                        if u == 0 and there(g + 1):
                            pe.wait_ge(hat_ready, g + 2)
                            if there(g - 2):
                                pe.wait_ge(x3_ready, g - 1)
                            for k in range(2):
                                for t in range(GT):
                                    last = nc.tensor.transpose(ps_x[:, (2 * k + t) * P:(2 * k + t + 1) * P], hat[:, k, t], v.ident[:])
                            last.then_inc(hat_turned, 1)
                        if u == 3 and there(g + 1):
                            pe.wait_ge(kv_t_ready, 2 * (g + 1) + 2)
                            pe.wait_ge(lat_low, g + 2)
                            for b in range(GB):
                                last = nc.tensor.transpose(ps_x[:, b * P:(b + 1) * P], kv_t[1 - par][:, b], v.ident[:])
                            last.then_inc(kv_turned, 1)
                        if u == 6 and there(g - 1):
                            pe.wait_ge(out_copied, g)
                            if there(g + 1):
                                pe.wait_ge(kv_low, g + 2)
                            for t in range(GT):
                                last = nc.tensor.transpose(ps_x[:, t * P:(t + 1) * P], out_t[:, t * P:(t + 1) * P], v.ident[:])
                            last.then_inc(out_turned, 1)
                        go, pair = out_heads(g, u)
                        if there(go):
                            if pair == 0 and there(go - 1):
                                pe.wait_ge(out_copied, go)
                            pe.wait_ge(y_low, U * go + 4 * (pair // 4 + 1))
                            for h in (2 * pair, 2 * pair + 1):
                                last = split_products(nc, ps_o[:, 0:C], (w.n_h[:, h], w.n_l[:, h]), (y_h[:, h], y_l[:, h]), h == 0, h == H - 1)
                            if pair == 7:
                                last.then_inc(out_done, 1)
                        gq, pair, flip = q_heads(g, u)
                        if there(gq):
                            lat = par ^ flip
                            pe.wait_ge(lat_low, gq + 1)
                            if there(gq - 1) or pair >= 2:
                                pe.wait_ge(q_ready, 8 * gq + pair - 1)
                            for i in range(2):
                                h = 2 * pair + i
                                last = split_products(nc, ps_q[pair % 2][:, i], (w.m_h[:, h], w.m_l[:, h]),
                                                      (lat_h[lat][:].rearrange("p b s -> p (b s)"), lat_l[lat][:].rearrange("p b s -> p (b s)")), True, True)
                            last.then_inc(q_done, 1)

                each_group(pe, step)

            @block.scalar
            def _(act):
                def step(g, par):
                    for u in range(U):
                        n = U * g + u
                        if u == 5 and there(g - 1):
                            act.wait_ge(out_done, g)
                            if there(g - 2):
                                act.wait_ge(out_turned, g - 1)
                            nc.scalar.activation(out_t[:], ps_o[:, 0:C], ACT.Copy).then_inc(out_copied, 1)
                        gb, ub, _ = before(g, u)
                        if there(gb):
                            act.wait_ge(y_done, n)
                            b, half = ub % GB, ub // GB
                            nc.scalar.activation(y_h[:, HH * half:HH * (half + 1), b * SEQ:(b + 1) * SEQ], ps_y[:].rearrange("p (h s) -> p h s", h=HH),
                                                 ACT.Copy).then_inc(y_high, 1)
                        if there(g):
                            act.wait_ge(probs_turned, n + 1)
                            if there(g - 1) or u:
                                act.wait_ge(y_done, n)
                            nc.scalar.activation(probs_h[:], ps_t[:], ACT.Copy).then_inc(probs_high, 1)
                        gs, us, flip = ahead(g, u, 2)
                        if there(gs):
                            act.wait_ge(max_ready, U * gs + us + 1)
                            if there(g):
                                act.wait_ge(normed_ready, n + 1)
                            for i in range(4):
                                last = nc.scalar.activation(probs[us % 2][:, i], ps_s[us % 2][:, i], ACT.Exp, bias=neg_max[us % 2][:, i:i + 1],
                                                            accum_out=sums[us % 2][:, i:i + 1])
                            last.then_inc(exp_done, 1)
                        if u == 0 and there(g + 1):
                            act.wait_ge(hat_turned, g + 2)
                            for k in range(2):
                                nc.scalar.activation(kv_t[1 - par][:, :, k * SEQ:(k + 1) * SEQ],
                                                     ps_x[:, k * C:(k + 1) * C].rearrange("p (b s) -> p b s", b=GB), ACT.Identity,
                                                     bias=v.vec2[:, 2 * k + 1:2 * k + 2], scale=v.vec2[:, 2 * k:2 * k + 1]).then_inc(kv_t_ready, 1)
                            act.wait_ge(kv_t_ready, 2 * (g + 1) + 2)
                            nc.scalar.activation(lat_h[1 - par][:], kv_t[1 - par][:, :, SEQ:KEYS], ACT.Copy).then_inc(lat_high, 1)
                        if u == 3 and there(g + 1):
                            act.wait_ge(kv_turned, g + 2)
                            nc.scalar.activation(kv_h[1 - par][:], ps_x[:].rearrange("p (b d) -> p b d", b=GB), ACT.Copy).then_inc(kv_high, 1)

                each_group(act, step)

            @block.vector
            def _(dve):
                def step(g, par):
                    for u in range(U):
                        n = U * g + u
                        g1, u1, _ = ahead(g, u, 1)
                        if there(g1):
                            n1 = U * g1 + u1
                            dve.wait_ge(exp_done, n1 + 1)
                            if there(g1 - 1) or u1 >= 2:
                                dve.wait_ge(normed_ready, n1 - 1)
                            nc.vector.reciprocal(recip[u1 % 2][:], sums[u1 % 2][:]).then_inc(recip_ready, 1)
                        gs, us, _ = ahead(g, u, 2)
                        if there(gs):
                            dve.wait_ge(scores_done, U * gs + us + 1)
                            nc.vector.tensor_reduce(neg_max[us % 2][:], ps_s[us % 2][:], AX.X, ALU.max, negate=True).then_inc(max_ready, 1)
                        gb, ub, _ = before(g, u)
                        if there(gb):
                            b, half = ub % GB, ub // GB
                            dve.wait_ge(y_high, n)
                            nc.vector.tensor_tensor(y_l[:, HH * half:HH * (half + 1), b * SEQ:(b + 1) * SEQ], ps_y[:].rearrange("p (h s) -> p h s", h=HH),
                                                    y_h[:, HH * half:HH * (half + 1), b * SEQ:(b + 1) * SEQ].bitcast(F32), ALU.subtract).then_inc(y_low, 1)
                        if there(g):
                            dve.wait_ge(probs_high, n + 1)
                            nc.vector.tensor_tensor(probs_l[:], ps_t[:], probs_h[:].bitcast(F32), ALU.subtract).then_inc(probs_low, 1)
                        gq, pair, _ = q_heads(g, u)
                        if there(gq):
                            dve.wait_ge(q_done, 8 * gq + pair + 1)
                            nc.vector.tensor_copy(q_t[:, :, 2 * pair:2 * pair + 2].rearrange("p b h s -> p h b s"),
                                                  ps_q[pair % 2][:].rearrange("p h (b s) -> p h b s", b=GB)).then_inc(q_ready, 1)
                        if u == 0 and there(g + 1):
                            dve.wait_ge(lat_high, g + 2)
                            nc.vector.tensor_tensor(lat_l[1 - par][:], kv_t[1 - par][:, :, SEQ:KEYS], lat_h[1 - par][:].bitcast(F32), ALU.subtract
                                                    ).then_inc(lat_low, 1)
                        if u == 3 and there(g + 1):
                            dve.wait_ge(kv_high, g + 2)
                            nc.vector.tensor_tensor(kv_l[1 - par][:], ps_x[:].rearrange("p (b d) -> p b d", b=GB), kv_h[1 - par][:].bitcast(F32),
                                                    ALU.subtract).then_inc(kv_low, 1)
                        if u == 6 and there(g - 1):
                            residual(g - 1)
                        if u == 6 and there(g + 2):
                            dve.wait_ge(w.normed, g + 3)
                            if there(g + 1):
                                dve.wait_ge(hat_turned, g + 2)
                            for k, source in enumerate((v.cx, v.xa)):
                                for t in range(GT):
                                    at = GT * (g + 2) + t
                                    last = nc.vector.tensor_scalar(hat[:, k, t], source[:, at, :], w.rstd[:, k, bass.ds(at, 1)], w.shift[:, k, bass.ds(at, 1)],
                                                                   ALU.mult, ALU.add)
                            last.then_inc(hat_ready, 1)

                def residual(g):
                    dve.wait_ge(out_turned, g + 1)
                    if there(g - 1):
                        dve.wait_ge(x3_ready, g)
                    for t in range(GT):
                        n = GT * g + t
                        last = nc.vector.scalar_tensor_tensor(v.xb[:, n, :], ps_x[:, t * P:(t + 1) * P], v.tgate[:, 1:2], v.xa[:, n, :], ALU.mult, ALU.add)
                    last.then_inc(x3_ready, 1)
                    if there(g - 1):
                        for t in range(GT):
                            last = nc.vector.bn_stats(v.stat6[:, GT * (g - 1) + t, :], v.xb[:, GT * (g - 1) + t, :])
                        last.then_inc(x3_stats, 1)

                each_group(dve, step)
                dve.wait_ge(x3_ready, NG)
                for n in range(NT - GT, NT):
                    nc.vector.bn_stats(v.stat6[:, n, :], v.xb[:, n, :])

            @block.gpsimd
            def _(pool):
                norm_constants(nc, v.norm3, v.norm3_tile, 0.0).then_inc(x3_constants, 1)
                pool.wait_ge(x3_constants, 1)

                def step(g, par):
                    for u in range(U):
                        if there(g + 2) and not (isinstance(g, int) and g == -2):
                            for i in {0: (0, 1), 1: (2, 3), 2: (4,), 3: (5, 6), 4: (7, 8), 5: (9,)}.get(u, ()):
                                w.norm_part(pool, g + 2, i)
                        if there(g - 3) and u >= 6:
                            if u == 6:
                                pool.wait_ge(x3_stats, g - 2)
                            for i in ((0, 1, 2, 3), (4, 5, 6))[u - 6]:
                                v.norm3_part(pool, g - 3, i)
                        g1, u1, _ = ahead(g, u, 1)
                        if not there(g1):
                            continue
                        n1 = U * g1 + u1
                        pool.wait_ge(recip_ready, n1 + 1)
                        if there(g1 - 1) or u1 >= 2:
                            pool.wait_ge(probs_turned, n1 - 1)
                        nc.gpsimd.tensor_tensor(normed[u1 % 2][:], probs[u1 % 2][:], recip[u1 % 2][:].unsqueeze(2).broadcast_to([P, 4, KEYS]), ALU.mult
                                                ).then_inc(normed_ready, 1)

                each_group(pool, step)


def mixture1(nc, v, w, out):
    C = GT * P
    HALF = E // 2
    with ExitStack() as ctx:
        sem = lambda name: ctx.enter_context(nc.semaphore(name))
        sb = lambda name, shape, dt=F32: ctx.enter_context(nc.sbuf_tensor(name, shape, dt))
        pb = lambda name, shape: ctx.enter_context(nc.psum_tensor(name, shape, F32))
        hat = sb("d_hat", [P, GT, D])
        hat_t = sb("d_hat_t", [P, C])
        hat_h, hat_l = ([sb(f"d_hat_{n}{i}", [P, C], F32R) for i in range(2)] for n in "hl")
        logits, shifted, exps = sb("d_logits", [P, GT, E]), sb("d_shifted", [P, GT, E]), sb("d_exps", [P, GT, E])
        best, first, total = sb("d_best", [P, GT, 1]), sb("d_first", [P, GT, 1]), sb("d_total", [P, GT, 1])
        recip, best_weight = sb("d_recip", [P, GT, 1]), sb("d_best_weight", [P, GT, 1])
        equal, ranked, chosen = sb("d_equal", [P, GT, E]), sb("d_ranked", [P, GT, E]), sb("d_chosen", [P, GT, E])
        weight = [sb(f"d_weight{i}", [P, GT, E]) for i in range(2)]
        scaled = [sb(f"d_scaled{i}", [P, HALF, D]) for i in range(2)]
        pairs, four = sb("d_pairs", [P, 2, D]), sb("d_four", [P, D])
        ps_lo, ps_hi = ([pb(f"d_ps_{n}{i}", [P, HALF, D]) for i in range(2)] for n in ("lo", "hi"))
        ps_x, ps_r = pb("d_ps_x", [P, 512]), pb("d_ps_r", [P, 512])
        hat_ready, turned, copied, high_done, low_done, routed, route = (
            sem(n) for n in ("hat_ready", "turned", "copied", "high_done", "low_done", "routed", "route"))
        shifted_ready, exps_ready, weight_ready = sem("shifted_ready"), sem("exps_ready"), sem("weight_ready")
        low_experts_done, experts_done, added, scaled_done, pool_steps, tile_done, stored = (
            sem(n) for n in ("low_experts_done", "experts_done", "added", "scaled_done", "pool_steps", "tile_done", "stored"))
        ROUTE = 8

        with nc.Block() as block:

            def each_group(eng, step):
                for g in range(-3, 1):
                    step(g, g % 2)
                with eng.Fori(0, (NG - 4) // 2) as i:
                    step(2 * i + 1, 1)
                    step(2 * i + 2, 0)
                for g in range(NG - 3, NG):
                    step(g, g % 2)

            @block.sync
            def _(sp):
                rows = out.rearrange("(t c) s d -> (c s) t d", c=2)
                with sp.Fori(0, NG) as g:
                    sp.wait_ge(tile_done, GT * g + GT)
                    sp.dma_start(rows[:, bass.ds(GT * g, GT), :], v.xa[:, bass.ds(GT * g, GT), :]).then_inc(stored, 16)
                sp.wait_ge(stored, 16 * NG)

            @block.tensor
            def _(pe):
                def step(g, par):
                    for t in range(GT):
                        if there(g):
                            n = GT * g + t
                            pe.wait_ge(high_done, g + 1)
                            pe.wait_ge(low_done, g + 1)
                            if there(g - 1):
                                pe.wait_ge(added, HALF * (n - 1))
                                pe.wait_ge(scaled_done, n - 1)
                            for half, bank in enumerate((ps_lo[t], ps_hi[t])):
                                cols = slice(half * 512, (half + 1) * 512)
                                flat = bank[:].rearrange("p e d -> p (e d)")
                                nc.tensor.matmul(flat, w.ones_pair[:], w.bias_pair[:, cols], start=True, stop=False)
                                last = split_products(nc, flat, (hat_h[par][:, t * P:(t + 1) * P], hat_l[par][:, t * P:(t + 1) * P]),
                                                      (w.e_h[:, cols], w.e_l[:, cols]), False, True)
                                last.then_inc((low_experts_done, experts_done)[half], 1)
                        if t == 0 and there(g + 2):
                            pe.wait_ge(hat_ready, g + 3)
                            if there(g + 1):
                                pe.wait_ge(copied, g + 2)
                            for s in range(GT):
                                last = nc.tensor.transpose(ps_x[:, s * P:(s + 1) * P], hat[:, s], v.ident[:])
                            last.then_inc(turned, 1)
                        if t == 1 and there(g + 2):
                            pe.wait_ge(copied, g + 3)
                            if there(g + 1):
                                pe.wait_ge(route, ROUTE * (g + 1) + 1)
                            for s in range(GT):
                                last = nc.tensor.matmul(ps_r[:, s * E:(s + 1) * E], hat_t[:, s * P:(s + 1) * P], w.router[:], start=True, stop=True)
                            last.then_inc(routed, 1)

                each_group(pe, step)

            @block.scalar
            def _(act):
                def step(g, par):
                    for t in range(GT):
                        if t == 0 and there(g + 1):
                            act.wait_ge(copied, g + 2)
                            if there(g - 1):
                                act.wait_ge(experts_done, GT * g)
                            nc.scalar.activation(hat_h[1 - par][:], hat_t[:], ACT.Copy).then_inc(high_done, 1)
                        if t == 1 and there(g + 2):
                            act.wait_ge(turned, g + 3)
                            if there(g + 1):
                                act.wait_ge(routed, g + 2)
                                act.wait_ge(low_done, g + 2)
                            nc.scalar.activation(hat_t[:], ps_x[:, 0:C], ACT.Copy).then_inc(copied, 1)
                        if there(g):
                            n = GT * g + t
                            act.wait_ge(experts_done, n + 1)
                            act.wait_ge(weight_ready, g + 1)
                            if there(g - 1):
                                act.wait_ge(pool_steps, 2 * (n - 2) + 1)
                            for e in range(HALF):
                                last = nc.scalar.activation(scaled[t][:, e], ps_hi[t][:, e], ACT.Copy, scale=weight[par][:, t, HALF + e:HALF + e + 1])
                            last.then_inc(scaled_done, 1)
                        if t == 0 and there(g + 1):
                            act.wait_ge(shifted_ready, g + 2)
                            nc.scalar.activation(exps[:], shifted[:], ACT.Exp).then_inc(exps_ready, 1)
                        if t == 1 and there(g + 3):
                            if not isinstance(g, int) or g >= NG - 5:
                                act.wait_ge(v.normed3, NG)
                            if there(g + 2):
                                act.wait_ge(turned, g + 3)
                            for s in range(GT):
                                at = GT * (g + 3) + s
                                last = nc.scalar.activation(hat[:, s], v.xb[:, at, :], ACT.Identity, scale=v.rstd3[:, bass.ds(at, 1)],
                                                            bias=v.shift3[:, bass.ds(at, 1)])
                            last.then_inc(hat_ready, 1)

                each_group(act, step)

            @block.vector
            def _(dve):
                wide = [P, GT, E]

                def choose(g, par, i):
                    if not there(g):
                        return
                    if i == 0:
                        dve.wait_ge(routed, g + 1)
                        last = nc.vector.tensor_tensor(logits[:], ps_r[:, 0:GT * E].rearrange("p (t e) -> p t e", t=GT),
                                                       v.router_b_row[:].unsqueeze(1).broadcast_to(wide), ALU.add)
                    else:
                        dve.wait_ge(route, ROUTE * g + i)
                    if i == 1:
                        last = nc.vector.reduce_max(best[:, :, 0], logits[:], AX.X)
                    if i == 2:
                        if there(g - 1):
                            dve.wait_ge(exps_ready, g)
                        nc.vector.tensor_tensor(shifted[:], logits[:], best[:].broadcast_to(wide), ALU.subtract).then_inc(shifted_ready, 1)
                        last = nc.vector.tensor_tensor(equal[:], logits[:], best[:].broadcast_to(wide), ALU.is_equal)
                    if i == 3:
                        last = nc.vector.tensor_tensor(ranked[:], equal[:], v.first_wins[:].unsqueeze(1).broadcast_to(wide), ALU.mult)
                    if i == 4:
                        last = nc.vector.reduce_max(first[:, :, 0], ranked[:], AX.X)
                    if i == 5:
                        dve.wait_ge(exps_ready, g + 1)
                        nc.vector.tensor_tensor(chosen[:], ranked[:], first[:].broadcast_to(wide), ALU.is_equal)
                        last = nc.vector.reduce_sum(total[:, :, 0], exps[:], AX.X)
                    if i == 6:
                        last = nc.vector.reciprocal(recip[:], total[:])
                    if i == 7:
                        last = nc.vector.tensor_scalar(best_weight[:], recip[:], v.tgate[:, 3:4], None, ALU.mult)
                    if i == 8:
                        if there(g - 2):
                            dve.wait_ge(scaled_done, GT * (g - 1))
                        nc.vector.tensor_tensor(weight[par][:], chosen[:], best_weight[:].broadcast_to(wide), ALU.mult).then_inc(weight_ready, 1)
                    else:
                        last.then_inc(route, 1)

                def step(g, par):
                    for t in range(GT):
                        if t == 0 and there(g + 1):
                            dve.wait_ge(high_done, g + 2)
                            nc.vector.tensor_tensor(hat_l[1 - par][:], hat_t[:], hat_h[1 - par][:].bitcast(F32), ALU.subtract).then_inc(low_done, 1)
                        for e in range(HALF):
                            if there(g):
                                n = GT * g + t
                                if e == 0:
                                    dve.wait_ge(low_experts_done, n + 1)
                                    dve.wait_ge(weight_ready, g + 1)
                                else:
                                    dve.wait_ge(added, HALF * n + e)
                                before = v.xb[:, n, :] if e == 0 else v.xa[:, n, :]
                                nc.vector.scalar_tensor_tensor(v.xa[:, n, :], ps_lo[t][:, e], weight[par][:, t, e:e + 1], before, ALU.mult, ALU.add
                                                               ).then_inc(added, 1)
                            choose(g + 1, 1 - par, HALF * t + e)
                    choose(g + 1, 1 - par, ROUTE)

                each_group(dve, step)

            @block.gpsimd
            def _(pool):
                for g in range(NG - 2, NG):
                    for i in range(NORM_STEPS):
                        v.norm3_part(pool, g, i)

                def step(g, par):
                    for t in range(GT):
                        if there(g):
                            n = GT * g + t
                            pool.wait_ge(scaled_done, n + 1)
                            nc.gpsimd.tensor_tensor(pairs[:], scaled[t][:, 0:2], scaled[t][:, 2:4], ALU.add).then_inc(pool_steps, 1)
                            pool.wait_ge(pool_steps, 2 * n + 1)
                            nc.gpsimd.tensor_tensor(four[:], pairs[:, 0], pairs[:, 1], ALU.add).then_inc(pool_steps, 1)
                            pool.wait_ge(pool_steps, 2 * n + 2)
                            pool.wait_ge(added, HALF * (n + 1))
                            nc.gpsimd.tensor_tensor(v.xa[:, n, :], v.xa[:, n, :], four[:], ALU.add).then_inc(tile_done, 1)

                each_group(pool, step)


INPUTS = ["x", "ctx_1024", "mask_BxS2_bk0", "g_xattn", "g_ffn", "L0_xattn_Wq", "L0_xattn_bq", "L0_xattn_Wk", "L0_xattn_bk",
          "L0_xattn_Wv", "L0_xattn_bv", "L0_xattn_Wo", "L0_xattn_bo", "L0_ffn_norm_scale", "L0_ffn_w_router", "L0_ffn_w_up",
          "L0_ffn_w_down", "L1_xattn_g1", "L1_xattn_b1", "L1_xattn_g2", "L1_xattn_b2", "L1_xattn_Wq", "L1_xattn_Wkv",
          "L1_xattn_Wout", "L1_ffn_router_w", "L1_ffn_router_b", "L1_ffn_expert_w", "L1_ffn_expert_b"]


def build_program(nc, io, out):
    with ExitStack() as ctx:
        sem = lambda name: ctx.enter_context(nc.semaphore(name))
        sb = lambda name, shape, dt=F32: ctx.enter_context(nc.sbuf_tensor(name, shape, dt))
        v = Env()
        v.first_loaded, v.x_loaded, v.weights0_loaded, v.weights1_loaded = sem("first_loaded"), sem("x_loaded"), sem("weights0_loaded"), sem("weights1_loaded")
        v.weights2_loaded, v.weights3_loaded, v.gates_ready = sem("weights2_loaded"), sem("weights3_loaded"), sem("gates_ready")
        v.xa, v.xb, v.cx = sb("xa", [P, NT, D]), sb("xb", [P, NT, D]), sb("cx", [P, NT, D])
        v.stats, v.norm_work = sb("stats", [P, 2, NT, 6]), sb("norm_work", [P, 8, GT])
        v.ctx_stat6, v.stat6 = v.stats[:, 0], v.stats[:, 1]
        v.rstd3, v.shift3, v.norm3_tile = sb("rstd3", [P, NT]), sb("shift3", [P, NT]), sb("norm3_scratch", [P, 16, GT])
        v.norm3, v.normed3, v.norm3_parts = Env(), sem("normed3"), sem("norm3_parts")

        def norm3_part(pool, g, i):
            tiles = slice(GT * g, GT * (g + 1)) if isinstance(g, int) else bass.ds(GT * g, GT)
            last = norm_step(nc, pool, v.norm3, i, v.norm3_parts, (NORM_STEPS - 1) * g, lambda k: v.stat6[:, tiles, k], v.rstd3[:, tiles],
                             v.shift3[:, tiles])
            last.then_inc(v.normed3 if i == NORM_STEPS - 1 else v.norm3_parts, 1)

        v.norm3_part = norm3_part
        v.ident, v.minus_half = sb("ident", [P, P]), sb("minus_half", [P, NT])
        v.zeros = sb("zeros", [P, GT])
        v.ones_row = sb("ones_row", [1, P], BF16)
        v.first_wins = sb("first_wins", [P, E])
        v.head_in_four, v.four_rows, v.q_mask = sb("head_in_four", [P, 4]), sb("four_rows", [P, 4]), sb("q_mask", [P, 4])
        v.four_cols = sb("four_cols", [P, D])
        v.gate, v.tgate, v.half_gate = sb("gate", [P, 4]), sb("tgate", [P, 4]), sb("half_gate", [P, 1])
        v.wq1_raw, v.wkv1_raw, v.wout1_raw = sb("wq1_raw", [P, H * HD1]), sb("wkv1_raw", [P, 2 * H * HD1]), sb("wout1_raw", [P, H // 2, D])
        v.vec2 = sb("vec2", [P, 4])
        v.expert_raw, v.router1_raw = sb("expert_raw", [P, E, D]), sb("router1_raw", [E, D])
        v.router_b_row = sb("router_b_row", [P, E])
        with ExitStack() as layer0:
            sb0 = lambda name, shape, dt=F32: layer0.enter_context(nc.sbuf_tensor(name, shape, dt))
            v.w_up_raw, v.w_down_raw = sb0("w_up_raw", [P, E * 4, D]), sb0("w_down_raw", [P, E, HID])
            v.router0_raw, v.vec1 = sb0("router0_raw", [E, D]), sb0("vec1", [P, 1])
            with ExitStack() as first:
                sb0 = lambda name, shape, dt=F32: first.enter_context(nc.sbuf_tensor(name, shape, dt))
                v.wq0, v.wk0, v.wv0, v.wo0 = (sb0(n, [P, D]) for n in ("wq0", "wk0", "wv0", "wo0"))
                v.wq0_h, v.wq0_l, v.wk0_h, v.wk0_l = (sb0(n, [P, D], F32R) for n in ("wq0_h", "wq0_l", "wk0_h", "wk0_l"))
                v.vec0, v.bk_four = sb0("vec0", [P, 3]), sb0("bk_four", [P, 4])
                v.bo_row, v.gbo = sb0("bo_row", [P, D]), sb0("gbo", [P, D])
                setup(nc, v, io)
                attention0(nc, v, io)
            mixture0(nc, v)
        w = Env()
        w.e_h, w.e_l = sb("d_e_h", [P, E * D], F32R), sb("d_e_l", [P, E * D], F32R)
        w.router, w.bias_pair, w.ones_pair = sb("d_router", [P, E]), sb("d_bias_pair", [2, E * D], F32R), sb("d_ones_pair", [2, P], F32R)
        attention1(nc, v, io, w)
        mixture1(nc, v, w, out)


def kernel(**inputs):
    import numpy as _np
    import concourse.bacc as _bacc
    from concourse import mybir as _mybir
    from concourse.bass_utils import run_bass_kernel_spmd as _run

    nc = _bacc.Bacc("TRN2", target_bir_lowering=False, num_devices=1)
    arrays, io = {}, {}
    for name in INPUTS:
        a = _np.ascontiguousarray(_np.asarray(inputs[name]))
        arrays[f"in_{name}"] = a
        io[name] = nc.dram_tensor(f"in_{name}", a.shape, _mybir.dt.from_np(a.dtype), kind="ExternalInput").ap()
    out = nc.dram_tensor("out_tokens", (BATCH, SEQ, D), _mybir.dt.float32, kind="ExternalOutput").ap()
    build_program(nc, io, out)
    r = _run(nc, [arrays], core_ids=[0])
    return r.results[0]["out_tokens"]
```
